# Optimizing a Trainium2 kernel written in Bass

```python
import numpy as np
import jax
import jax.numpy as jnp

def _softmax(x, axis=-1):
    return jax.nn.softmax(x, axis=axis)

def _gelu(x):
    return jax.nn.gelu(x, approximate=True)

def _silu(x):
    return jax.nn.silu(x)

def _sigmoid(x):
    return jax.nn.sigmoid(x)

def _layernorm(x, axis=-1, eps=1e-05):
    m = jnp.mean(x, axis=axis, keepdims=True)
    v = jnp.var(x, axis=axis, keepdims=True)
    return (x - m) / jnp.sqrt(v + eps)

def _scatter_add(tgt, idx, src, axis=0):
    return tgt.at[idx].add(src)

def _segment_sum(src, seg, n):
    return jax.ops.segment_sum(src, seg, n)
kernel_name = 'mk_gps_d2_gnn_r32_d03c0d'

def setup_inputs(seed: int=0):
    np.random.seed(seed)
    _w = jnp.asarray

    def _rec_inputs():
        import jax
        import jax.numpy as jnp
        _gk = jax.random.key(seed)
        x = -0.0005963 + 1.001 * jax.random.normal(jax.random.fold_in(_gk, 1), (128, 768), jnp.float32)
        src = jax.random.randint(jax.random.fold_in(_gk, 2), (2048,), 0, 128, jnp.int32)
        dst = jnp.minimum((128 * jax.random.uniform(jax.random.fold_in(_gk, 3), (2048,)) ** 2.0).astype(jnp.int32), 4095)
        _o = jnp.argsort(dst, stable=True)
        src = src[_o]
        dst = dst[_o]
        edge_attr_256 = 0.000121155 + 1.00018 * jax.random.normal(jax.random.fold_in(_gk, 11), (2048, 256), jnp.float32)
        return (x, src, dst, edge_attr_256)
    x, src, dst, edge_attr_256 = _rec_inputs()

    def _L0_gnn_setup():
        import jax, jax.numpy as jnp
        import numpy as np
        N_NODES = 128
        N_EDGES = 4096
        D = 768
        DE = 256
        L = 3
        H = 8
        DH = D // H
        EPS = 1e-05

        def _layernorm(x, g, b):
            mu = jnp.mean(x, axis=-1, keepdims=True)
            var = jnp.var(x, axis=-1, keepdims=True)
            return (x - mu) * jax.lax.rsqrt(var + EPS) * g + b
        key = jax.random.key(seed)
        ks = jax.random.split(key, 20)
        s = 0.02
        inp = {'node_features': jax.random.normal(ks[0], (N_NODES, D), jnp.float32), 'edge_index': jax.random.randint(ks[1], (2, N_EDGES), 0, N_NODES, jnp.int64 if jax.config.x64_enabled else jnp.int32), 'edge_features': jax.random.normal(ks[2], (N_EDGES, DE), jnp.float32), 'Wn': jax.random.normal(ks[3], (D, D), jnp.float32) * s, 'bn': jnp.zeros((D,), jnp.float32), 'We': jax.random.normal(ks[4], (D, DE), jnp.float32) * s, 'be': jnp.zeros((D,), jnp.float32), 'W1': jax.random.normal(ks[5], (L, D, 2 * D), jnp.float32) * s, 'b1': jnp.zeros((L, D), jnp.float32), 'ln_g': jnp.ones((L, D), jnp.float32), 'ln_b': jnp.zeros((L, D), jnp.float32), 'W2': jax.random.normal(ks[6], (L, D, D), jnp.float32) * s, 'b2': jnp.zeros((L, D), jnp.float32), 'Wqkv': jax.random.normal(ks[7], (3 * D, D), jnp.float32) * s, 'bqkv': jnp.zeros((3 * D,), jnp.float32), 'Wo': jax.random.normal(ks[8], (D, D), jnp.float32) * s, 'bo': jnp.zeros((D,), jnp.float32)}
        return inp
    _L0_gnn_all = _L0_gnn_setup()
    _L0_gnn_in = {k: v for k, v in _L0_gnn_all.items() if k in ('Wn', 'bn', 'We', 'be', 'W1', 'b1', 'ln_g', 'ln_b', 'W2', 'b2', 'Wqkv', 'bqkv', 'Wo', 'bo')}
    del _L0_gnn_all

    def _L0_mix_setup():
        import jax, jax.numpy as jnp
        import numpy as np
        NUM_HEADS = 12

        def _reference_tuple_inner(x, w_qkv, w_proj, b_proj):
            b, n, c = x.shape
            h = NUM_HEADS
            d = c // h
            qkv = (x @ w_qkv.T).reshape(b, n, 3, h, d).transpose(2, 0, 3, 1, 4)
            q, k, v = (qkv[0], qkv[1], qkv[2])
            q = jax.nn.elu(q) + 1.0
            k = jax.nn.elu(k) + 1.0
            kv = jnp.einsum('bhsd,bhse->bhde', k, v)
            z = 1.0 / jnp.einsum('bhsd,bhd->bhs', q, k.sum(axis=-2))
            out = jnp.einsum('bhde,bhsd,bhs->bhse', kv, q, z)
            out = out.transpose(0, 2, 1, 3).reshape(b, n, c)
            out = out @ w_proj.T + b_proj
            return (out, kv)
        key = jax.random.key(seed)
        k0, k1, k2 = jax.random.split(key, 3)
        b, n, c = (4, 128, 768)
        x = jax.random.normal(k0, (b, n, c), dtype=jnp.float32)
        w_qkv = jax.random.normal(k1, (3 * c, c), dtype=jnp.float32) * 0.02
        w_proj = jax.random.normal(k2, (c, c), dtype=jnp.float32) * 0.02
        b_proj = jnp.zeros((c,), dtype=jnp.float32)
        return {'x': x, 'w_qkv': w_qkv, 'w_proj': w_proj, 'b_proj': b_proj}
    _L0_mix_all = _L0_mix_setup()
    _L0_mix_in = {k: v for k, v in _L0_mix_all.items() if k in ('w_qkv', 'w_proj', 'b_proj')}
    del _L0_mix_all

    def _L0_ffn_setup():
        import jax, jax.numpy as jnp
        import numpy as np
        B, L, D, E, TOP_K = (8, 1024, 768, 4, 2)
        H = 2 * D
        LN_EPS = 1e-05

        def _gelu(v):
            return jax.nn.gelu(v, approximate=False)

        def _mish(v):
            return v * jnp.tanh(jax.nn.softplus(v))
        _ACTS = [_gelu, jax.nn.silu, _mish, _gelu]
        key = jax.random.key(seed)
        ks = jax.random.split(key, 8)
        x = jax.random.normal(ks[0], (B, L, D), dtype=jnp.float32)
        router_w = jax.random.normal(ks[1], (E, D), dtype=jnp.float32) * 0.02
        router_b = jnp.zeros((E,), dtype=jnp.float32)
        w1 = jax.random.normal(ks[2], (E, D, H), dtype=jnp.float32) * (1.0 / np.sqrt(D))
        b1 = jax.random.normal(ks[3], (E, H), dtype=jnp.float32) * 0.01
        w2 = jax.random.normal(ks[4], (E, H, D), dtype=jnp.float32) * (1.0 / np.sqrt(H))
        b2 = jax.random.normal(ks[5], (E, D), dtype=jnp.float32) * 0.01
        ln_g = jnp.ones((D,), dtype=jnp.float32)
        ln_b = jnp.zeros((D,), dtype=jnp.float32)
        return {'x': x, 'router_w': router_w, 'router_b': router_b, 'w1': w1, 'b1': b1, 'w2': w2, 'b2': b2, 'ln_g': ln_g, 'ln_b': ln_b}
    _L0_ffn_all = _L0_ffn_setup()
    _L0_ffn_in = {k: v for k, v in _L0_ffn_all.items() if k in ('router_w', 'router_b', 'w1', 'b1', 'w2', 'b2', 'ln_g', 'ln_b')}
    del _L0_ffn_all

    def _L1_gnn_setup():
        import jax, jax.numpy as jnp
        import numpy as np
        N_NODES = 10000
        N_EDGES = 3125
        DIM = 768
        NEG_SLOPE = 0.2

        def gat_conv(x, src, dst, W, att_src, att_dst, bias, num_nodes):
            h = x @ W
            a_s = h @ att_src
            a_d = h @ att_dst
            e = jax.nn.leaky_relu(a_s[src] + a_d[dst], NEG_SLOPE)
            m = jax.ops.segment_max(e, dst, num_segments=num_nodes)
            e = jnp.exp(e - m[dst])
            denom = jax.ops.segment_sum(e, dst, num_segments=num_nodes)
            alpha = e / denom[dst]
            msg = alpha[:, None] * h[src]
            out = jax.ops.segment_sum(msg, dst, num_segments=num_nodes)
            return out + bias
        key = jax.random.key(seed)
        ks = jax.random.split(key, 12)
        s = 1.0 / np.sqrt(DIM)
        inp = {'x': jax.random.normal(ks[0], (N_NODES, DIM), dtype=jnp.float32), 'edge_index': jax.random.randint(ks[1], (2, N_EDGES), 0, N_NODES, dtype=jnp.int64), 'W1': jax.random.normal(ks[2], (DIM, DIM), dtype=jnp.float32) * s, 'att_src1': jax.random.normal(ks[3], (DIM,), dtype=jnp.float32) * s, 'att_dst1': jax.random.normal(ks[4], (DIM,), dtype=jnp.float32) * s, 'b1': jnp.zeros((DIM,), dtype=jnp.float32), 'W2': jax.random.normal(ks[5], (DIM, DIM), dtype=jnp.float32) * s, 'att_src2': jax.random.normal(ks[6], (DIM,), dtype=jnp.float32) * s, 'att_dst2': jax.random.normal(ks[7], (DIM,), dtype=jnp.float32) * s, 'b2': jnp.zeros((DIM,), dtype=jnp.float32)}
        return inp
    _L1_gnn_all = _L1_gnn_setup()
    _L1_gnn_in = {k: v for k, v in _L1_gnn_all.items() if k in ('W1', 'att_src1', 'att_dst1', 'b1', 'W2', 'att_src2', 'att_dst2', 'b2')}
    del _L1_gnn_all

    def _L1_mix_setup():
        import jax, jax.numpy as jnp
        import numpy as np
        B, N, C = (16, 128, 768)
        H = 12
        D = C // H
        SCALE = D ** (-0.5)
        key = jax.random.key(seed)
        k1, k2, k3, k4 = jax.random.split(key, 4)
        x = jax.random.normal(k1, (B, N, C), dtype=jnp.float32)
        w_qkv = jax.random.normal(k2, (C, 3 * C), dtype=jnp.float32) * 0.02
        w_proj = jax.random.normal(k3, (C, C), dtype=jnp.float32) * 0.02
        b_proj = jax.random.normal(k4, (C,), dtype=jnp.float32) * 0.02
        return {'x': x, 'w_qkv': w_qkv, 'w_proj': w_proj, 'b_proj': b_proj}
    _L1_mix_all = _L1_mix_setup()
    _L1_mix_in = {k: v for k, v in _L1_mix_all.items() if k in ('w_qkv', 'w_proj', 'b_proj')}
    del _L1_mix_all

    def _L1_ffn_setup():
        import jax, jax.numpy as jnp
        import numpy as np
        S, B, DIM = (1024, 4, 768)
        N_EXPERTS = 8
        HID = 64
        key = jax.random.key(seed)
        ks = jax.random.split(key, 6)
        scale = 0.02
        return {'hidden_states': jax.random.normal(ks[0], (S, B, DIM), dtype=jnp.float32), 'router_w': jax.random.normal(ks[1], (DIM, N_EXPERTS), dtype=jnp.float32) * scale, 'router_b': jnp.zeros((N_EXPERTS,), dtype=jnp.float32), 'w1': jax.random.normal(ks[2], (N_EXPERTS, DIM, HID), dtype=jnp.float32) * scale, 'w2': jax.random.normal(ks[3], (N_EXPERTS, DIM, HID), dtype=jnp.float32) * scale, 'w3': jax.random.normal(ks[4], (N_EXPERTS, HID, DIM), dtype=jnp.float32) * scale}
    _L1_ffn_all = _L1_ffn_setup()
    _L1_ffn_in = {k: v for k, v in _L1_ffn_all.items() if k in ('router_w', 'router_b', 'w1', 'w2', 'w3')}
    del _L1_ffn_all
    return {'x': x, 'src': src, 'dst': dst, 'edge_attr_256': edge_attr_256, 'L0_gnn_Wn': _L0_gnn_in['Wn'], 'L0_gnn_bn': _L0_gnn_in['bn'], 'L0_gnn_We': _L0_gnn_in['We'], 'L0_gnn_be': _L0_gnn_in['be'], 'L0_gnn_W1': _L0_gnn_in['W1'], 'L0_gnn_b1': _L0_gnn_in['b1'], 'L0_gnn_ln_g': _L0_gnn_in['ln_g'], 'L0_gnn_ln_b': _L0_gnn_in['ln_b'], 'L0_gnn_W2': _L0_gnn_in['W2'], 'L0_gnn_b2': _L0_gnn_in['b2'], 'L0_gnn_Wqkv': _L0_gnn_in['Wqkv'], 'L0_gnn_bqkv': _L0_gnn_in['bqkv'], 'L0_gnn_Wo': _L0_gnn_in['Wo'], 'L0_gnn_bo': _L0_gnn_in['bo'], 'L0_mix_w_qkv': _L0_mix_in['w_qkv'], 'L0_mix_w_proj': _L0_mix_in['w_proj'], 'L0_mix_b_proj': _L0_mix_in['b_proj'], 'L0_ffn_router_w': _L0_ffn_in['router_w'], 'L0_ffn_router_b': _L0_ffn_in['router_b'], 'L0_ffn_w1': _L0_ffn_in['w1'], 'L0_ffn_b1': _L0_ffn_in['b1'], 'L0_ffn_w2': _L0_ffn_in['w2'], 'L0_ffn_b2': _L0_ffn_in['b2'], 'L0_ffn_ln_g': _L0_ffn_in['ln_g'], 'L0_ffn_ln_b': _L0_ffn_in['ln_b'], 'L1_gnn_W1': _L1_gnn_in['W1'], 'L1_gnn_att_src1': _L1_gnn_in['att_src1'], 'L1_gnn_att_dst1': _L1_gnn_in['att_dst1'], 'L1_gnn_b1': _L1_gnn_in['b1'], 'L1_gnn_W2': _L1_gnn_in['W2'], 'L1_gnn_att_src2': _L1_gnn_in['att_src2'], 'L1_gnn_att_dst2': _L1_gnn_in['att_dst2'], 'L1_gnn_b2': _L1_gnn_in['b2'], 'L1_mix_w_qkv': _L1_mix_in['w_qkv'], 'L1_mix_w_proj': _L1_mix_in['w_proj'], 'L1_mix_b_proj': _L1_mix_in['b_proj'], 'L1_ffn_router_w': _L1_ffn_in['router_w'], 'L1_ffn_router_b': _L1_ffn_in['router_b'], 'L1_ffn_w1': _L1_ffn_in['w1'], 'L1_ffn_w2': _L1_ffn_in['w2'], 'L1_ffn_w3': _L1_ffn_in['w3']}

def reference(x, src, dst, edge_attr_256, L0_gnn_Wn, L0_gnn_bn, L0_gnn_We, L0_gnn_be, L0_gnn_W1, L0_gnn_b1, L0_gnn_ln_g, L0_gnn_ln_b, L0_gnn_W2, L0_gnn_b2, L0_gnn_Wqkv, L0_gnn_bqkv, L0_gnn_Wo, L0_gnn_bo, L0_mix_w_qkv, L0_mix_w_proj, L0_mix_b_proj, L0_ffn_router_w, L0_ffn_router_b, L0_ffn_w1, L0_ffn_b1, L0_ffn_w2, L0_ffn_b2, L0_ffn_ln_g, L0_ffn_ln_b, L1_gnn_W1, L1_gnn_att_src1, L1_gnn_att_dst1, L1_gnn_b1, L1_gnn_W2, L1_gnn_att_src2, L1_gnn_att_dst2, L1_gnn_b2, L1_mix_w_qkv, L1_mix_w_proj, L1_mix_b_proj, L1_ffn_router_w, L1_ffn_router_b, L1_ffn_w1, L1_ffn_w2, L1_ffn_w3):
    import jax
    import jax.numpy as jnp

    def _L0_gnn_ref(node_features, edge_index, edge_features, Wn, bn, We, be, W1, b1, ln_g, ln_b, W2, b2, Wqkv, bqkv, Wo, bo):
        import jax, jax.numpy as jnp
        import numpy as np
        N_NODES = 128
        N_EDGES = 4096
        D = 768
        DE = 256
        L = 3
        H = 8
        DH = D // H
        EPS = 1e-05

        def _layernorm(x, g, b):
            mu = jnp.mean(x, axis=-1, keepdims=True)
            var = jnp.var(x, axis=-1, keepdims=True)
            return (x - mu) * jax.lax.rsqrt(var + EPS) * g + b
        n = node_features.shape[0]
        nodes = node_features @ Wn.T + bn
        edge_proj = edge_features @ We.T + be
        src, dst = (edge_index[0], edge_index[1])
        for l in range(L):
            msgs = nodes[src] + nodes[dst] + edge_proj
            agg = jax.ops.segment_sum(msgs, dst, num_segments=n)
            combined = jnp.concatenate([nodes, agg], axis=-1)
            h = combined @ W1[l].T + b1[l]
            h = _layernorm(h, ln_g[l], ln_b[l])
            h = jax.nn.relu(h)
            h = h @ W2[l].T + b2[l]
            nodes = h + nodes
        qkv = nodes @ Wqkv.T + bqkv
        q, k, v = jnp.split(qkv, 3, axis=-1)
        q = q.reshape(n, H, DH) * DH ** (-0.5)
        k = k.reshape(n, H, DH)
        v = v.reshape(n, H, DH)
        scores = jnp.einsum('nhd,mhd->hnm', q, k)
        probs = jax.nn.softmax(scores, axis=-1)
        attn = jnp.einsum('hnm,mhd->nhd', probs, v).reshape(n, D)
        attended = attn @ Wo.T + bo
        return nodes + attended

    def _L0_mix_ref(x, w_qkv, w_proj, b_proj):
        import jax, jax.numpy as jnp
        import numpy as np
        NUM_HEADS = 12

        def _reference_tuple_inner(x, w_qkv, w_proj, b_proj):
            b, n, c = x.shape
            h = NUM_HEADS
            d = c // h
            qkv = (x @ w_qkv.T).reshape(b, n, 3, h, d).transpose(2, 0, 3, 1, 4)
            q, k, v = (qkv[0], qkv[1], qkv[2])
            q = jax.nn.elu(q) + 1.0
            k = jax.nn.elu(k) + 1.0
            kv = jnp.einsum('bhsd,bhse->bhde', k, v)
            z = 1.0 / jnp.einsum('bhsd,bhd->bhs', q, k.sum(axis=-2))
            out = jnp.einsum('bhde,bhsd,bhs->bhse', kv, q, z)
            out = out.transpose(0, 2, 1, 3).reshape(b, n, c)
            out = out @ w_proj.T + b_proj
            return (out, kv)
        return _reference_tuple_inner(x, w_qkv, w_proj, b_proj)[0]

    def _L0_ffn_ref(x, router_w, router_b, w1, b1, w2, b2, ln_g, ln_b):
        import jax, jax.numpy as jnp
        import numpy as np
        B, L, D, E, TOP_K = (8, 1024, 768, 4, 2)
        H = 2 * D
        LN_EPS = 1e-05

        def _gelu(v):
            return jax.nn.gelu(v, approximate=False)

        def _mish(v):
            return v * jnp.tanh(jax.nn.softplus(v))
        _ACTS = [_gelu, jax.nn.silu, _mish, _gelu]
        b, l, d = x.shape
        e = router_w.shape[0]
        pooled = x.mean(axis=1)
        logits = pooled @ router_w.T + router_b
        top_v, top_i = jax.lax.top_k(logits, TOP_K)
        gates_k = jax.nn.softmax(top_v, axis=-1)
        gate = jnp.zeros((b, e), x.dtype).at[jnp.arange(b)[:, None], top_i].add(gates_k)
        h = jnp.einsum('bld,edh->belh', x, w1) + b1[None, :, None, :]
        h = jnp.stack([_ACTS[i](h[:, i]) for i in range(e)], axis=1)
        out = jnp.einsum('belh,ehd->beld', h, w2) + b2[None, :, None, :]
        y = jnp.einsum('be,beld->bld', gate, out) + x
        mu = y.mean(axis=-1, keepdims=True)
        var = ((y - mu) ** 2).mean(axis=-1, keepdims=True)
        return (y - mu) * jax.lax.rsqrt(var + LN_EPS) * ln_g + ln_b

    def _L1_gnn_ref(x, edge_index, W1, att_src1, att_dst1, b1, W2, att_src2, att_dst2, b2):
        import jax, jax.numpy as jnp
        import numpy as np
        N_NODES = 10000
        N_EDGES = 3125
        DIM = 768
        NEG_SLOPE = 0.2

        def gat_conv(x, src, dst, W, att_src, att_dst, bias, num_nodes):
            h = x @ W
            a_s = h @ att_src
            a_d = h @ att_dst
            e = jax.nn.leaky_relu(a_s[src] + a_d[dst], NEG_SLOPE)
            m = jax.ops.segment_max(e, dst, num_segments=num_nodes)
            e = jnp.exp(e - m[dst])
            denom = jax.ops.segment_sum(e, dst, num_segments=num_nodes)
            alpha = e / denom[dst]
            msg = alpha[:, None] * h[src]
            out = jax.ops.segment_sum(msg, dst, num_segments=num_nodes)
            return out + bias
        n = x.shape[0]
        loops = jnp.arange(n, dtype=edge_index.dtype)
        src = jnp.concatenate([edge_index[0], loops])
        dst = jnp.concatenate([edge_index[1], loops])
        h = gat_conv(x, src, dst, W1, att_src1, att_dst1, b1, n)
        h = jax.nn.relu(h)
        out = gat_conv(h, src, dst, W2, att_src2, att_dst2, b2, n)
        return out

    def _L1_mix_ref(x, w_qkv, w_proj, b_proj):
        import jax, jax.numpy as jnp
        import numpy as np
        B, N, C = (16, 128, 768)
        H = 12
        D = C // H
        SCALE = D ** (-0.5)
        b, n, c = x.shape
        qkv = (x @ w_qkv).reshape(b, n, 3, H, D).transpose(2, 0, 3, 1, 4)
        q, k, v = (qkv[0], qkv[1], qkv[2])
        kv = jnp.einsum('bhnd,bhne->bhde', k, v) * SCALE
        gq = jax.nn.gelu(q, approximate=False)
        gkv = jax.nn.gelu(kv, approximate=False)
        out = jnp.einsum('bhtd,bhde->bhte', gq, gkv)
        out = out.transpose(0, 2, 1, 3).reshape(b, n, c)
        return out @ w_proj + b_proj

    def _L1_ffn_ref(hidden_states, router_w, router_b, w1, w2, w3):
        import jax, jax.numpy as jnp
        import numpy as np
        S, B, DIM = (1024, 4, 768)
        N_EXPERTS = 8
        HID = 64
        s, b, h = hidden_states.shape
        route = jax.nn.softmax(hidden_states @ router_w + router_b, axis=2)
        max_prob = jnp.max(route, axis=2).reshape(-1, 1)
        max_ind = jnp.argmax(route, axis=2).reshape(-1)
        x = hidden_states.reshape(-1, h)
        out = jnp.zeros_like(x)
        for e in range(N_EXPERTS):
            mask = (max_ind == e)[:, None]
            xe = jnp.where(mask, x, 0.0)
            oe = jax.nn.silu(xe @ w1[e]) * (xe @ w2[e]) @ w3[e]
            out = out + jnp.where(mask, oe, 0.0)
        out = out.astype(jnp.bfloat16) * max_prob
        return out.reshape(s, b, h)
    edge_index = jnp.stack([src, dst])
    xn = _layernorm(x, axis=-1)
    x = x + _L0_gnn_ref(xn, edge_index, edge_attr_256, L0_gnn_Wn, L0_gnn_bn, L0_gnn_We, L0_gnn_be, L0_gnn_W1, L0_gnn_b1, L0_gnn_ln_g, L0_gnn_ln_b, L0_gnn_W2, L0_gnn_b2, L0_gnn_Wqkv, L0_gnn_bqkv, L0_gnn_Wo, L0_gnn_bo) + _L0_mix_ref(xn[None], L0_mix_w_qkv, L0_mix_w_proj, L0_mix_b_proj)[0]
    x = x + _L0_ffn_ref(_layernorm(x, axis=-1)[None], L0_ffn_router_w, L0_ffn_router_b, L0_ffn_w1, L0_ffn_b1, L0_ffn_w2, L0_ffn_b2, L0_ffn_ln_g, L0_ffn_ln_b)[0]
    xn = _layernorm(x, axis=-1)
    x = x + _L1_gnn_ref(xn, edge_index, L1_gnn_W1, L1_gnn_att_src1, L1_gnn_att_dst1, L1_gnn_b1, L1_gnn_W2, L1_gnn_att_src2, L1_gnn_att_dst2, L1_gnn_b2) + _L1_mix_ref(xn[None], L1_mix_w_qkv, L1_mix_w_proj, L1_mix_b_proj)[0]
    x = x + _L1_ffn_ref(_layernorm(x, axis=-1)[None], L1_ffn_router_w, L1_ffn_router_b, L1_ffn_w1, L1_ffn_w2, L1_ffn_w3)[0]
    return x

_drawn_inputs = setup_inputs


def setup_inputs(seed=0):
    import zlib

    import numpy as np

    out = dict(_drawn_inputs(seed))
    spreads = {'L0_gnn_bn': (0.0, 0.1),
     'L0_gnn_be': (0.0, 0.1),
     'L0_gnn_b1': (0.0, 0.379),
     'L0_gnn_ln_g': (1.0, 0.2),
     'L0_gnn_ln_b': (0.0, 0.1),
     'L0_gnn_b2': (0.0, 0.1),
     'L0_gnn_bqkv': (0.0, 0.1),
     'L0_gnn_bo': (0.0, 0.1),
     'L0_mix_b_proj': (0.0, 0.1),
     'L0_ffn_router_b': (0.0, 0.8),
     'L0_ffn_ln_g': (1.0, 0.2),
     'L0_ffn_ln_b': (0.0, 0.1),
     'L1_gnn_b1': (0.0, 0.355),
     'L1_gnn_b2': (0.0, 0.1),
     'L1_ffn_router_b': (0.0, 0.8)}
    factors = {'L0_ffn_b1': 8.0,
     'L0_ffn_b2': 8.0,
     'L1_gnn_att_src1': 3.807,
     'L1_gnn_att_dst1': 8.0,
     'L1_gnn_att_src2': 8.0,
     'L1_gnn_att_dst2': 8.0,
     'L1_mix_b_proj': 8.0,
     'L1_ffn_router_w': 8.0,
     'L1_ffn_w1': 8.0,
     'L1_ffn_w2': 8.0,
     'L1_ffn_w3': 8.0}
    for name, (base, spread) in spreads.items():
        noise = np.random.default_rng([zlib.crc32(name.encode()), seed]).standard_normal(out[name].shape)
        drawn = base * np.exp(spread * noise) if base else spread * noise
        out[name] = jnp.asarray(drawn.astype(out[name].dtype))
    for name, factor in factors.items():
        out[name] = (out[name] * factor).astype(out[name].dtype)
    return out
```

```python
import numpy as np
import concourse.bass as bass
from concourse import mybir
from contextlib import ExitStack

P = 128
D = 768
HALF = D // 2
KT = D // P
E_EDGES = 2048
ET = E_EDGES // P
DE = 256
L_GNN = 3
CH = KT * HALF
SLOTS = 8
H0, DH0 = 8, D // 8
HM, DM = 12, D // 12
TOP_K = 2
E_FFN, E_MOE, HID = 4, 8, 64
FH = E_MOE * HID
EPS = 1e-5

C_WN = 0
C_LOOP = 2
C_QKV = C_LOOP + 8 * L_GNN
C_MIXP = C_QKV + 6
C_WO = C_MIXP + 2
C_FFN = C_WO + 2
C_GAT1 = C_FFN + 8 * E_FFN
C_L1 = C_GAT1 + 2
N_CHUNKS = C_L1 + 10
R_FFN = C_FFN
R_L1 = R_FFN + 8 * TOP_K
B_BN, B_B1, B_B2, B_QKV, B_BO, B_MIX0, B_GAT2, B_MIX1 = 0, 1, 4, 7, 10, 11, 12, 13
N_BIAS = 14
K_ID, K_IOTA, K_ONE, K_AVG, K_EPS, K_W4, K_D4, K_W8 = 0, 128, 256, 384, 512, 513, 517, 521
N_CST = 529
G_G, G_B, G_GB1, G_RW0, G_RB0, G_RW1, G_RB1 = 0, 18, 36, 42, 66, 70, 118
N_COLS = 126
V_AS1, V_AD1, V_AS2, V_AD2, V_LG, V_LB = range(6)


def gps_kernel(nc, x, src, dst, edge, w_edge, be_row, chunks, moe_w, bias_rows, gate_b2, cols, vecs,
               cst, sel, out):
    f32, bf16, i32 = mybir.dt.float32, mybir.dt.bfloat16, mybir.dt.int32
    ALU, ACT, AX = mybir.AluOpType, mybir.ActivationFunctionType, mybir.AxisListType.X
    ctx = ExitStack()
    with ctx:
        sems = {}

        def S(name):
            if name not in sems:
                sems[name] = ctx.enter_context(nc.semaphore(name))
            return sems[name]

        def sb(name, shape, dt=f32):
            return ctx.enter_context(nc.sbuf_tensor(name, shape, dt))

        ring = sb("ring", [P, SLOTS, CH])
        early = sb("early", [P, 2, CH])
        moe = sb("moe", [P, 4 * CH])
        vec = sb("vec", [P, 6, D])
        X = sb("X", [P, D])
        nodes = sb("nodes", [P, D])
        nodT = sb("nodT", [P, KT, P])
        agg = sb("agg", [P, KT, P])
        ept = sb("ept", [P, 780])
        xnt = sb("xnt", [P, 780])
        zh = sb("zh", [P, 2, D])
        mix = sb("mix", [P, 3, D])
        blk = sb("blk", [P, 3072])
        con = sb("con", [P, N_CST])
        col = sb("col", [P, N_COLS])
        selb = sb("selb", [96, N_BIAS * P], bf16)
        btab = sb("btab", [96, 3 * D], bf16)
        b2f = sb("b2f", [E_FFN, D])
        apT = sb("apT", [P, P])
        cnt = sb("cnt", [P, P])
        cneg = sb("cneg", [P, P])
        deg = sb("deg", [1, P])
        sd_i = sb("sd_i", [P, 2, ET], i32)
        sd_f = sb("sd_f", [P, 2, ET])
        st = sb("st", [P, 2, 6])
        mv = sb("mv", [P, 2])
        std = sb("std", [P, 1])
        rstd = sb("rstd", [P, 1])
        sm = sb("sm", [P, 3, 16])
        rt = sb("rt", [P, 96])
        oh = sb("oh", [P, TOP_K, E_FFN])
        kind = sb("kind", [P, E_FFN])
        gate = sb("gate", [P, TOP_K])
        par = sb("par", [P, 3, TOP_K])
        eidx = sb("eidx", [P, TOP_K], i32)
        selx = sb("selx", [96, TOP_K * P], bf16)
        g4 = sb("g4", [E_FFN, P])
        ab = sb("ab", [P, 8])
        half_c = con[:, K_EPS:K_EPS + 1]

        ident = con[:, K_ID:K_ID + P]
        iota = con[:, K_IOTA:K_IOTA + P]
        xnT = xnt[:, 0:D].rearrange("p (k n) -> p k n", k=KT)
        eptT = ept[:, 0:D].rearrange("p (k n) -> p k n", k=KT)
        hT = zh[:, 1, :].rearrange("p (k n) -> p k n", k=KT)
        z = zh[:, 0, :]
        xn = mix[:, 0, :]
        edg = moe[:, 0:4096].rearrange("p (t k) -> p t k", t=ET)
        ohb = moe[:, 4096:7168].bitcast(bf16).rearrange("p (a t n) -> p a t n", a=3, t=ET)
        ohd32 = moe[:, 7168:9216].rearrange("p (t n) -> p t n", t=ET)
        we = zh[:, :, :]
        eat = agg[:, 0:2, :]
        be_s = blk[0:1, 0:D]
        bsrc = early[0:96, 0, :]

        B = [ctx.enter_context(nc.psum_tensor(f"B{i}", [P, 512], f32)) for i in range(8)]

        block = ctx.enter_context(nc.Block())

        @block.sync
        def _(sp):
            sp.dma_start(X[:, :], x).then_inc(S("x_loaded"), 16)
            sp.dma_start(con[:, :], cst).then_inc(S("con_loaded"), 16)

            def load(slot, index):
                sp.dma_start(ring[:, slot, :], chunks[index]).then_inc(S(f"slot{slot}"), 16)

            load(0, 0)
            sp.dma_start(bsrc, bias_rows).then_inc(S("bias_loaded"), 16)
            sp.dma_start(selb[:, :], sel).then_inc(S("sel_loaded"), 16)
            load(1, 1)
            sp.dma_start(sd_i[:, 0, :], src.rearrange("(p t) -> p t", t=ET)).then_inc(S("index_loaded"), 16)
            sp.dma_start(sd_i[:, 1, :], dst.rearrange("(p t) -> p t", t=ET)).then_inc(S("index_loaded"), 16)
            sp.dma_start(edg, edge.rearrange("(p t) k -> p t k", t=ET)).then_inc(S("edge_loaded"), 16)
            sp.dma_start(we, w_edge.rearrange("p (k f) -> p k f", k=2)).then_inc(S("we_loaded"), 16)
            sp.dma_start(be_s, be_row).then_inc(S("we_loaded"), 16)
            sp.dma_start(col[:, :], cols).then_inc(S("cols_loaded"), 16)
            for c in range(2, SLOTS):
                load(c, c)
            with sp.Fori(1, C_FFN // SLOTS) as r:
                for k in range(SLOTS):
                    sp.wait_ge(S("units_done"), (r - 1) * SLOTS + (k + 1))
                    load(k, r * SLOTS + k)
            for c in range(C_FFN // SLOTS * SLOTS, C_FFN):
                sp.wait_ge(S("units_done"), c - SLOTS + 1)
                load(c % SLOTS, c)
            sp.wait_ge(S("elu_ready"), 1)
            sp.dma_start(vec[:, :, :], vecs.rearrange("(a v) -> a v", a=1).broadcast_to([P, 6 * D])
                         .rearrange("p (a v) -> p a v", a=6)).then_inc(S("vec_loaded"), 16)
            sp.dma_start(b2f[:, :], gate_b2).then_inc(S("b2_loaded"), 16)
            for h in range(2):
                sp.dma_start(early[:, h, :], chunks[C_GAT1 + h]).then_inc(S(f"early{h}_loaded"), 16)
            sp.dma_start(moe[:, :], moe_w).then_inc(S("moe_loaded"), 16)
            sp.wait_ge(S("routed"), 1)
            for s in range(TOP_K):
                e = sp.value_load(eidx[0:1, s:s + 1], min_val=0, max_val=E_FFN - 1)
                for j in range(8):
                    c = R_FFN + 8 * s + j
                    sp.wait_ge(S("units_done"), c - SLOTS + 1)
                    load(c % SLOTS, e * 8 + (C_FFN + j))
            for j in range(10):
                c = R_L1 + j
                sp.wait_ge(S("units_done"), c - SLOTS + 1)
                load(c % SLOTS, C_L1 + j)
            sp.wait_ge(S("out_ready"), 2)
            sp.dma_start(out, nodes[:, :]).then_inc(S("out_stored"), 16)
            sp.wait_ge(S("out_stored"), 16)

        @block.tensor
        def _(pe):
            mm = nc.tensor.matmul

            def transposes(src_tiles, bank, rows=P):
                for i, t in enumerate(src_tiles):
                    last = nc.tensor.transpose(bank[0:rows, i * P:(i + 1) * P], t, ident)
                return last

            def tiles(row, half, n=3, w=P):
                return [row[:, (half * n + i) * w:(half * n + i + 1) * w] for i in range(n)]

            def bias(bank, row, half, start=True):
                mm(bank[:, 0:HALF], selb[:, row * P:(row + 1) * P], btab[:, half * HALF:(half + 1) * HALF],
                   start=start, stop=False)

            def unit(bank, lhsT, chunk, start=False, stop=True, skip=False):
                for k in range(KT):
                    last = mm(bank[:, 0:HALF], lhsT[:, k, :], chunk[:, k * HALF:(k + 1) * HALF],
                              start=start and k == 0, stop=stop and k == KT - 1, skip_group_check=skip)
                return last

            def ring_unit(c, turn, bank, lhsT, **kw):
                pe.wait_ge(S(f"slot{c % SLOTS}"), 16 * (turn + 1))
                unit(bank, lhsT, ring[:, c % SLOTS, :], **kw).then_inc(S("units_done"), 1)

            pe.wait_ge(S("con_loaded"), 16)
            pe.wait_ge(S("xn_ready"), 1)
            for h in range(2):
                transposes(tiles(xn, h), B[6 + h]).then_inc(S("xn_tr"), 1)
            pe.wait_ge(S("sel_loaded"), 16)
            pe.wait_ge(S("btab_ready"), 3)
            bias(B[2], B_BN, 0)
            pe.wait_ge(S("xnT_saved"), 2)
            ring_unit(0, 0, B[2], xnT)
            bias(B[3], B_BN, 1)
            ring_unit(1, 0, B[3], xnT)
            pe.wait_ge(S("edge_loaded"), 16)
            pe.wait_ge(S("onehot_ready"), 1)
            for k in range(2):
                for t in range(ET):
                    last = mm(B[4][:, k * P:(k + 1) * P], edg[:, t, k * P:(k + 1) * P], ohd32[:, t, :],
                              start=t == 0, stop=t == ET - 1)
            last.then_inc(S("eat_done"), 1)
            for o, a, b in ((0, 2, 1), (P, 1, 0)):
                for t in range(ET):
                    mm(B[5][:, o:o + P], ohb[:, a, t, :], ohb[:, b, t, :], start=t == 0, stop=t == ET - 1)
            for t in range(ET):
                last = mm(B[5][0:1, 2 * P:3 * P], con[:, K_ONE:K_ONE + 1], ohd32[:, t, :],
                          start=t == 0, stop=t == ET - 1)
            last.then_inc(S("adj_done"), 1)
            pe.wait_ge(S("we_loaded"), 32)
            pe.wait_ge(S("b4_free"), 1)
            pe.wait_ge(S("b5_free"), 1)
            for f in range(KT):
                o = B[f // 3][:, f % 3 * P:(f % 3 + 1) * P]
                for k in range(2):
                    mm(o, we[:, k, f * P:(f + 1) * P], eat[:, k, :], start=k == 0, stop=False)
                last = mm(o, be_s[:, f * P:(f + 1) * P], deg[:, :], start=False, stop=True)
                if f % 3 == 2:
                    last.then_inc(S("ept_done"), 1)
            pe.wait_ge(S("ept_saved"), 2)

            with pe.Fori(0, L_GNN) as l:
                for h in range(2):
                    pe.wait_ge(S("nodes_ready"), 2 * l + (h + 1))
                    transposes(tiles(nodes, h), B[6 + h]).then_inc(S("nodes_tr"), 1)
                for h in range(2):
                    pe.wait_ge(S(f"b{4 + h}_free"), l + 1)
                    for i in range(3):
                        f = 3 * h + i
                        last = mm(B[4 + h][:, i * P:(i + 1) * P], nodes[:, f * P:(f + 1) * P], apT[:, :],
                                  start=True, stop=True)
                    last.then_inc(S("agg_done"), 1)
                pe.wait_ge(S("nodT_saved"), 2 * l + 2)
                for h in range(2):
                    mm(B[h][:, 0:HALF], selb[:, bass.ds((l + B_B1) * P, P)], btab[:, h * HALF:(h + 1) * HALF],
                       start=True, stop=False)
                    ring_unit(C_LOOP + h, l + (C_LOOP + h) // SLOTS, B[h], nodT, stop=False)
                pe.wait_ge(S("agg_saved"), 2 * l + 2)
                for h in range(2):
                    c = C_LOOP + 2 + h
                    ring_unit(c, l + c // SLOTS, B[h], agg)
                c = C_LOOP + 4
                ring_unit(c, l + c // SLOTS, B[4], xnT, start=True)
                for h in range(2):
                    pe.wait_ge(S("z_ready"), 2 * l + (h + 1))
                    transposes(tiles(z, h), B[6 + h]).then_inc(S("z_tr"), 1)
                for h in range(2):
                    mm(B[2 + h][:, 0:HALF], selb[:, bass.ds((l + B_B2) * P, P)],
                       btab[:, h * HALF:(h + 1) * HALF], start=True, stop=False)
                    pe.wait_ge(S("hT_saved"), 2 * l + 2)
                    c = C_LOOP + 5 + h
                    ring_unit(c, l + c // SLOTS, B[2 + h], hT)
                c = C_LOOP + 7
                ring_unit(c, l + c // SLOTS, B[5], xnT, start=True)

            for h in range(2):
                pe.wait_ge(S("nodes_ready"), 2 * L_GNN + h + 1)
                transposes(tiles(nodes, h), B[6 + h]).then_inc(S("nodes_tr"), 1)

            def qkv_unit(i, bank):
                bias(bank, B_QKV + i // 2, i % 2)
                ring_unit(C_QKV + i, (C_QKV + i) // SLOTS, bank, nodT)

            pe.wait_ge(S("nodT_saved"), 2 * L_GNN + 2)
            for i in range(4):
                qkv_unit(i, B[i])
            q0, k0 = zh[:, 0, :], zh[:, 1, :]
            for h in range(2):
                pe.wait_ge(S(f"q{h}_saved"), 1)
                transposes(tiles(q0, h, 4, DH0), B[6 + h], DH0).then_inc(S(f"q{h}_tr"), 1)
            pe.wait_ge(S("b4_free"), L_GNN + 1)
            qkv_unit(4, B[4])
            for h in range(2):
                pe.wait_ge(S(f"k{h}_saved"), 1)
                transposes(tiles(k0, h, 4, DH0), B[h], DH0).then_inc(S(f"k{h}_tr"), 1)
            pe.wait_ge(S("b5_free"), L_GNN + 1)
            qkv_unit(5, B[5])
            qT = blk[0:DH0, 0:1024]
            kT = blk[0:DH0, 1024:2048]
            for h in range(2):
                pe.wait_ge(S(f"q{h}T_saved"), 1)
                pe.wait_ge(S(f"k{h}T_saved"), 1)
                for i in range(4):
                    o = (4 * h + i) * P
                    last = mm(B[2 + h][:, i * P:(i + 1) * P], qT[:, o:o + P], kT[:, o:o + P], start=True, stop=True)
                last.then_inc(S("scores_done"), 1)
            pe.wait_ge(S("elu_ready"), 1)
            for h in range(2):
                transposes(tiles(mix[:, 0, :], h), B[6 + h]).then_inc(S("mq_tr"), 1)
            pe.wait_ge(S("vaug_ready"), 1)
            for h in range(2):
                for i in range(3):
                    g = 3 * h + i
                    last = mm(B[h][:, i * 130:(i + 1) * 130], mix[:, 1, g * P:(g + 1) * P],
                              ept[:, g * 130:(g + 1) * 130], start=True, stop=True)
                last.then_inc(S("kv_done"), 1)
            pe.wait_ge(S("mqT_saved"), 2)
            for h in range(2):
                pe.wait_ge(S("kv_saved"), h + 1)
                for i in range(3):
                    g = 3 * h + i
                    last = mm(B[6 + h][:, i * 130:(i + 1) * 130], nodT[:, g, :],
                              xnt[:, g * 130:(g + 1) * 130], start=True, stop=True)
                last.then_inc(S("lin_done"), 1)
            probs, probT = blk[:, 2048:3072], blk[:, 0:1024]
            for h in range(2):
                pe.wait_ge(S("probs_ready"), h + 1)
                transposes([probs[:, (4 * h + i) * P:(4 * h + i + 1) * P] for i in range(4)],
                           B[2 + h]).then_inc(S("probs_tr"), 1)
            pe.wait_ge(S("lin_ready"), 2)
            for h in range(2):
                transposes(tiles(zh[:, 0, :], h), B[h]).then_inc(S("lin_tr"), 1)
            v0 = agg[:, :, :].rearrange("p k n -> p (k n)")
            for h in range(2):
                pe.wait_ge(S("probT_saved"), h + 1)
                for i in range(4):
                    o = 4 * h + i
                    last = mm(B[6 + h][:, i * DH0:(i + 1) * DH0], probT[:, o * P:(o + 1) * P],
                              v0[:, o * DH0:(o + 1) * DH0], start=True, stop=True)
                last.then_inc(S("attn_done"), 1)
            pe.wait_ge(S("v_saved"), 2)
            pe.wait_ge(S("linT_saved"), 2)
            for h in range(2):
                bias(B[4 + h], B_BO, h)
                bias(B[4 + h], B_MIX0, h, start=False)
                ring_unit(C_MIXP + h, (C_MIXP + h) // SLOTS, B[4 + h], hT, stop=False)
            for h in range(2):
                pe.wait_ge(S("attn_ready"), h + 1)
                transposes(tiles(mix[:, 0, :], h), B[h]).then_inc(S("attn_tr"), 1)
            attnT = mix[:, 1, :].rearrange("p (k n) -> p k n", k=KT)
            pe.wait_ge(S("attnT_saved"), 2)
            for h in range(2):
                ring_unit(C_WO + h, (C_WO + h) // SLOTS, B[4 + h], attnT)

            pe.wait_ge(S("xl_ready"), 1)
            for h in range(2):
                transposes(tiles(nodes, h), B[6 + h]).then_inc(S("xl_tr"), 1)
            pe.wait_ge(S("cols_loaded"), 16)
            pe.wait_ge(S("xlT_saved"), 2)
            for k in range(KT):
                last = mm(B[0][:, 0:E_FFN], nodT[:, k, :], col[:, G_RW0 + k * 4:G_RW0 + k * 4 + 4],
                          start=k == 0, stop=k == KT - 1)
            last.then_inc(S("logit_done"), 1)
            pe.wait_ge(S("logit_saved"), 1)
            mm(B[1][:, 0:E_FFN], con[:, K_AVG:K_AVG + P], rt[:, 0:4], start=True, stop=True).then_inc(S("mean_done"), 1)
            pe.wait_ge(S("b2_loaded"), 16)
            pe.wait_ge(S("gates_ready"), 1)
            for h in range(2):
                mm(B[6 + h][:, 0:HALF], g4[:, :], b2f[:, h * HALF:(h + 1) * HALF], start=True, stop=True,
                   skip_group_check=True)
            act_s = mix[:, 0:2, :].rearrange("p a (c n) -> p (a c) n", n=HALF)
            heT = zh[:, :, :].rearrange("p a (k n) -> p (a k) n", n=P)

            with pe.Fori(0, TOP_K) as s:
                def up(q):
                    mm(B[q][:, 0:HALF], selx[:, bass.ds(s * P, P)], btab[:, D + q * HALF:D + (q + 1) * HALF],
                       start=True, stop=False)
                    ring_unit(R_FFN + q, s + (R_FFN + q) // SLOTS, B[q], nodT)

                def turn(q):
                    pe.wait_ge(S("act_ready"), 4 * s + (q + 1))
                    if q >= 2:
                        pe.wait_ge(S("heT_saved"), 4 * s + (q - 1))
                    transposes([act_s[:, q, i * P:(i + 1) * P] for i in range(3)], B[4 + q % 2]).then_inc(S("act_tr"), 1)

                def down(g, h):
                    c = R_FFN + 4 + 2 * g + h
                    pe.wait_ge(S("heT_saved"), 4 * s + 2 * (g + 1))
                    ring_unit(c, s + c // SLOTS, B[6 + h], heT[:, 6 * g:6 * g + 6, :], stop=True, skip=True)

                up(0)
                up(1)
                up(2)
                turn(0)
                up(3)
                turn(1)
                down(0, 0)
                turn(2)
                down(0, 1)
                turn(3)
                down(1, 0)
                down(1, 1)

            pe.wait_ge(S("xn2_ready"), 1)
            for h in range(2):
                transposes(tiles(nodes, h), B[4 + h]).then_inc(S("xn2_tr"), 1)
            pe.wait_ge(S("xn2T_saved"), 2)

            def l1(j, bank, lhsT, **kw):
                c = R_L1 + j
                ring_unit(c, c // SLOTS, bank, lhsT, **kw)

            for h in range(2):
                pe.wait_ge(S(f"early{h}_loaded"), 16)
                unit(B[h], nodT, early[:, h, :], start=True).then_inc(S("gat_h1_done"), 1)
            l1(0, B[2], nodT, start=True)
            l1(1, B[3], nodT, start=True)

            def spread(g, bank):
                pe.wait_ge(S("diag_ready"), g + 1)
                mm(bank[:, 0:P], con[:, K_ONE:K_ONE + P], blk[:, 0:P], start=True, stop=True).then_inc(S("spread_done"), 1)

            def alpha_turn(g, bank):
                pe.wait_ge(S("alpha_ready"), g + 1)
                nc.tensor.transpose(bank[:, 0:P], blk[:, P:2 * P], ident).then_inc(S("alpha_tr"), 1)

            spread(0, B[6])
            pe.wait_ge(S("xn2T_saved"), 2)
            l1(2, B[4], nodT, start=True)
            alpha_turn(0, B[7])
            l1(3, B[5], nodT, start=True)
            h1 = agg[:, :, :].rearrange("p k n -> p (k n)")
            h2 = ept[:, 0:D]
            alT = blk[:, 2 * P:3 * P]
            pe.wait_ge(S("alphaT_saved"), 1)
            for h in range(2):
                for i in range(3):
                    f = 3 * h + i
                    last = mm(B[6 + h][:, i * P:(i + 1) * P], h1[:, f * P:(f + 1) * P], alT, start=True, stop=True)
                last.then_inc(S("gat1_done"), 1)
            pe.wait_ge(S("h1_saved"), 2)
            l1(4, B[0], nodT, start=True)
            l1(5, B[1], nodT, start=True)
            g1T = blk[:, 1024:1024 + D].rearrange("p (k n) -> p k n", k=KT)
            pe.wait_ge(S("g1T_saved"), 2)
            pe.wait_ge(S("mq1_ready"), 2)
            l1(6, B[2], g1T, start=True)
            l1(7, B[3], g1T, start=True)
            for h in range(2):
                transposes(tiles(mix[:, 0, :], h), B[6 + h]).then_inc(S("mq1_tr"), 1)
            pe.wait_ge(S("mk1_saved"), 2)
            pe.wait_ge(S("mv1_saved"), 2)
            for h in range(2):
                for i in range(3):
                    g = 3 * h + i
                    last = mm(B[4 + h][:, i * P:(i + 1) * P], mix[:, 1, g * P:(g + 1) * P],
                              mix[:, 2, g * P:(g + 1) * P], start=True, stop=True)
                last.then_inc(S("kv1_done"), 1)
            spread(1, B[2])
            pe.wait_ge(S("mq1T_saved"), 2)
            for h in range(2):
                pe.wait_ge(S("kv1_saved"), h + 1)
                for i in range(3):
                    g = 3 * h + i
                    last = mm(B[6 + h][:, i * P:(i + 1) * P], xnT[:, g, :], zh[:, 0, g * P:(g + 1) * P],
                              start=True, stop=True)
                last.then_inc(S("lin1_done"), 1)
            for h in range(2):
                pe.wait_ge(S("lin1_saved"), h + 1)
                transposes(tiles(zh[:, 1, :], h), B[4 + h]).then_inc(S("lin1_tr"), 1)
            l1T = blk[:, 2048:2048 + D].rearrange("p (k n) -> p k n", k=KT)
            pe.wait_ge(S("lin1T_saved"), 2)
            for h in range(2):
                bias(B[h], B_GAT2, h)
                bias(B[h], B_MIX1, h, start=False)
                l1(8 + h, B[h], l1T, stop=False)
            alpha_turn(1, B[3])
            pe.wait_ge(S("alphaT_saved"), 2)
            for h in range(2):
                mm(B[h][:, 0:HALF], alT, h2[:, h * HALF:(h + 1) * HALF], start=False,
                   stop=True).then_inc(S("x3_done"), 1)

            pe.wait_ge(S("xl3_ready"), 1)
            for h in range(2):
                transposes(tiles(nodes, h), B[4 + h]).then_inc(S("xl3_tr"), 1)
            pe.wait_ge(S("xl3T_saved"), 2)
            for k in range(KT):
                last = mm(B[6][:, 0:E_MOE], nodT[:, k, :], col[:, G_RW1 + k * 8:G_RW1 + k * 8 + 8],
                          start=k == 0, stop=k == KT - 1)
            last.then_inc(S("route1_done"), 1)
            pe.wait_ge(S("moe_loaded"), 16)
            for w in range(2):
                for k in range(KT):
                    o = (w * KT + k) * FH
                    last = mm(B[2 + w][:, :], nodT[:, k, :], moe[:, o:o + FH], start=k == 0, stop=k == KT - 1)
                last.then_inc(S("moe_up_done"), 1)
            pe.wait_ge(S("moe_h_ready"), 1)
            hm = agg[:, :, :].rearrange("p k n -> p (k n)")
            transposes([hm[:, i * P:(i + 1) * P] for i in range(4)], B[7]).then_inc(S("moe_h_tr"), 1)
            pe.wait_ge(S("moe_hT_saved"), 1)
            for h in range(2):
                for k in range(4):
                    o = 2 * KT * FH + k * D + h * HALF
                    last = mm(B[h][:, 0:HALF], ept[:, k * P:(k + 1) * P], moe[:, o:o + HALF],
                              start=k == 0, stop=k == 3)
                last.then_inc(S("moe_done"), 1)

        @block.scalar
        def _(act):
            A = nc.scalar.activation
            chain = [0]

            def link(ins):
                chain[0] += 1
                ins.then_inc(S("act_chain"), 1)
                act.wait_ge(S("act_chain"), chain[0])

            def root(k):
                act.wait_ge(S("var_ready"), k)
                A(std[:, :], mv[:, 1:2], ACT.Sqrt, bias=half_c).then_inc(S("std_ready"), 1)

            def save(out_ap, in_ap, name):
                A(out_ap, in_ap, ACT.Copy).then_inc(S(name), 1)

            def h3(bank):
                return bank[:, 0:HALF]

            def flat(t, h):
                return t[:, 3 * h:3 * h + 3, :].rearrange("p k n -> p (k n)")

            act.wait_ge(S("con_loaded"), 16)
            root(1)
            act.wait_ge(S("xn_tr"), 1)
            save(flat(xnT, 0), h3(B[6]), "xnT_saved")
            act.wait_ge(S("eat_done"), 1)
            save(eat.rearrange("p k n -> p (k n)"), B[4][:, 0:2 * P], "b4_free")
            act.wait_ge(S("ept_done"), 1)
            save(flat(eptT, 0), h3(B[0]), "ept_saved")
            act.wait_ge(S("cols_loaded"), 16)

            with act.Fori(0, L_GNN) as l:
                act.wait_ge(S("nodes_tr"), 2 * l + 1)
                save(flat(nodT, 0), h3(B[6]), "nodT_saved")
                root(l + 2)
                for h in range(2):
                    act.wait_ge(S("z_tr"), 2 * l + (h + 1))
                    for i in range(3):
                        f = 3 * h + i
                        last = A(hT[:, f, :], B[6 + h][:, i * P:(i + 1) * P], ACT.Relu,
                                 scale=col[:, bass.ds(l * KT + (G_G + f), 1)],
                                 bias=col[:, bass.ds(l * KT + (G_B + f), 1)])
                    last.then_inc(S("hT_saved"), 1)
                act.wait_ge(S("units_done"), l * 8 + (C_LOOP + 5))
                A(mix[:, bass.ds(l, 1), 0:HALF].rearrange("p a n -> p (a n)"), h3(B[4]), ACT.Copy).then_inc(S("b4_free"), 1)
                act.wait_ge(S("units_done"), l * 8 + (C_LOOP + 8))
                A(mix[:, bass.ds(l, 1), HALF:D].rearrange("p a n -> p (a n)"), h3(B[5]), ACT.Copy).then_inc(S("b5_free"), 1)

            act.wait_ge(S("nodes_tr"), 2 * L_GNN + 1)
            save(flat(nodT, 0), h3(B[6]), "nodT_saved")
            ex = early[:, 0, 0:2 * D]
            act.wait_ge(S("elu_min_ready"), 1)
            A(ex, ex, ACT.Exp).then_inc(S("elu_exp_ready"), 1)
            act.wait_ge(S("units_done"), C_QKV + 2)
            save(zh[:, 0, HALF:D], h3(B[1]), "q1_saved")
            act.wait_ge(S("q0_tr"), 1)
            save(blk[0:DH0, 0:512], B[6][0:DH0, :], "q0T_saved")
            act.wait_ge(S("units_done"), C_QKV + 4)
            save(zh[:, 1, HALF:D], h3(B[3]), "k1_saved")
            act.wait_ge(S("k0_tr"), 1)
            save(blk[0:DH0, 1024:1536], B[0][0:DH0, :], "k0T_saved")
            act.wait_ge(S("k1_tr"), 1)
            save(blk[0:DH0, 1536:2048], B[1][0:DH0, :], "k1T_saved")
            act.wait_ge(S("units_done"), C_QKV + 6)
            save(agg[:, 3:6, :].rearrange("p k n -> p (k n)"), h3(B[5]), "v_saved")
            for h in range(2):
                act.wait_ge(S("mq_tr"), h + 1)
                save(flat(nodT, h), h3(B[6 + h]), "mqT_saved")
                act.wait_ge(S("shifted"), h + 1)
                pr = blk[:, 2048 + 512 * h:2560 + 512 * h]
                A(pr, pr, ACT.Exp, scale=DH0 ** -0.5).then_inc(S("probs_ready"), 1)
            act.wait_ge(S("probs_tr"), 1)
            save(blk[:, 0:512], B[2][:, :], "probT_saved")
            act.wait_ge(S("probs_tr"), 2)
            save(blk[:, 512:1024], B[3][:, :], "probT_saved")
            act.wait_ge(S("lin_tr"), 1)
            save(flat(hT, 0), h3(B[0]), "linT_saved")
            act.wait_ge(S("attn_tr"), 1)
            save(mix[:, 1, 0:HALF], h3(B[0]), "attnT_saved")

            root(5)
            act.wait_ge(S("xl_tr"), 1)
            save(flat(nodT, 0), h3(B[6]), "xlT_saved")
            act.wait_ge(S("logit_done"), 1)
            save(rt[:, 0:4], B[0][:, 0:E_FFN], "logit_saved")
            act.wait_ge(S("margin_ready"), 1)
            A(rt[:, 5:6], rt[:, 4:5], ACT.Tanh, scale=0.5).then_inc(S("margin_tanh"), 1)
            act.wait_ge(S("params_ready"), 1)
            buf = blk[:, :].rearrange("p (b a n) -> p b a n", b=2, a=4)
            n_act = chain[0]
            with act.Fori(0, TOP_K) as s:
                def quarter(q):
                    act.wait_ge(S("units_done"), s * 8 + (R_FFN + q + 1))
                    if q >= 2:
                        act.wait_ge(S("act_ready"), s * 4 + (q - 1))
                    b = buf[:, q % 2]
                    A(b[:, 1, :], h3(B[q]), ACT.Gelu)
                    A(b[:, 0, :], h3(B[q]), ACT.Tanh, scale=0.5).then_inc(S("th_ready"), 1)
                    act.wait_ge(S("th_ready"), s * 4 + (q + 1))
                    A(b[:, 2, :], b[:, 0, :], ACT.Copy, scale=-1.0, bias=1.0).then_inc(S("s_ready"), 1)
                    act.wait_ge(S("s_ready"), s * 4 + (q + 1))
                    A(b[:, 3, :], b[:, 2, :], ACT.Identity, scale=kind[:, 2:3], bias=kind[:, 1:2]).then_inc(S("soft_ready"), 1)

                def turned(q):
                    act.wait_ge(S("act_tr"), s * 4 + (q + 1))
                    A(zh[:, q // 2, q % 2 * HALF:(q % 2 + 1) * HALF], h3(B[4 + q % 2]), ACT.Copy).then_inc(S("heT_saved"), 1)

                A(kind[:, :], oh[:, bass.ds(s, 1), :].rearrange("p a e -> p (a e)"), ACT.Copy).then_inc(S("kind_ready"), 1)
                act.wait_ge(S("kind_ready"), s + 1)
                quarter(0)
                quarter(1)
                quarter(2)
                turned(0)
                quarter(3)
                turned(1)
                turned(2)
                turned(3)

            root(6)
            root(7)
            act.wait_ge(S("xn2_tr"), 1)
            save(flat(nodT, 0), h3(B[4]), "xn2T_saved")
            act.wait_ge(S("gat_h1_done"), 1)
            save(flat(agg, 0), h3(B[0]), "h1_saved")
            act.wait_ge(S("gat_h1_done"), 2)
            save(flat(agg, 1), h3(B[1]), "h1_saved")
            act.wait_ge(S("gat_logit"), 1)
            A(blk[:, P:2 * P], blk[:, P:2 * P], ACT.Exp).then_inc(S("gat_exp"), 1)
            for h in range(2):
                act.wait_ge(S("units_done"), R_L1 + 1 + h)
                A(mix[:, 0, h * HALF:(h + 1) * HALF], h3(B[2 + h]), ACT.Gelu).then_inc(S("mq1_ready"), 1)
            for h in range(2):
                act.wait_ge(S("gat1_done"), h + 1)
                for i in range(3):
                    f = 3 * h + i
                    last = A(blk[:, 1024 + f * P:1024 + (f + 1) * P], B[6 + h][:, i * P:(i + 1) * P], ACT.Relu,
                             bias=col[:, G_GB1 + f:G_GB1 + f + 1])
                last.then_inc(S("g1T_saved"), 1)
            for h in range(2):
                act.wait_ge(S("units_done"), R_L1 + 5 + h)
                save(mix[:, 2, h * HALF:(h + 1) * HALF], h3(B[h]), "mv1_saved")
            act.wait_ge(S("mq1_tr"), 1)
            save(flat(xnT, 0), h3(B[6]), "mq1T_saved")
            act.wait_ge(S("zh_clear"), 1)
            for h in range(2):
                act.wait_ge(S("kv1_done"), h + 1)
                for o in range(2):
                    rows = slice(64 * o, 64 * o + 64)
                    dstk = zh[rows, 0, h * HALF:(h + 1) * HALF].rearrange("p (g c) -> p g c", g=3)[:, :, 64 * o:64 * o + 64]
                    srck = B[4 + h][rows, 0:HALF].rearrange("p (g c) -> p g c", g=3)[:, :, 64 * o:64 * o + 64]
                    last = A(dstk, srck, ACT.Gelu, scale=DM ** -0.5)
                last.then_inc(S("kv1_saved"), 1)
            act.wait_ge(S("gat_logit"), 2)
            A(blk[:, P:2 * P], blk[:, P:2 * P], ACT.Exp).then_inc(S("gat_exp"), 1)
            act.wait_ge(S("lin1_done"), 1)
            save(zh[:, 1, 0:HALF], h3(B[6]), "lin1_saved")
            act.wait_ge(S("lin1_done"), 2)
            save(zh[:, 1, HALF:D], h3(B[7]), "lin1_saved")
            act.wait_ge(S("lin1_tr"), 1)
            save(blk[:, 2048:2048 + HALF], h3(B[4]), "lin1T_saved")
            act.wait_ge(S("lin1_tr"), 2)
            save(blk[:, 2048 + HALF:2048 + D], h3(B[5]), "lin1T_saved")
            root(8)
            act.wait_ge(S("xl3_tr"), 1)
            save(flat(nodT, 0), h3(B[4]), "xl3T_saved")
            act.wait_ge(S("moe_shift"), 1)
            A(rt[:, 40:48], rt[:, 32:40], ACT.Exp, accum_out=rt[:, 48:49]).then_inc(S("moe_exp"), 1)
            act.wait_ge(S("moe_up_done"), 1)
            A(z[:, 0:FH], B[2][:, :], ACT.Silu).then_inc(S("silu_ready"), 1)
            act.wait_ge(S("moe_h_tr"), 1)
            save(ept[:, 0:512], B[7][:, :], "moe_hT_saved")

        @block.vector
        def _(dve):
            V = nc.vector
            base, chain, in_loop = [0], [0], [False]

            def link(ins):
                chain[0] += 1
                ins.then_inc(S("dve_chain"), 1)
                dve.wait_ge(S("dve_chain"), base[0] + chain[0])

            def h3(bank):
                return bank[:, 0:HALF]

            def halves(t):
                return t[:, 0:HALF], t[:, HALF:D]

            def flat(t, h):
                return t[:, 3 * h:3 * h + 3, :].rearrange("p k n -> p (k n)")

            def stats(h, ap):
                link(V.bn_stats(st[:, h, :], ap))

            def spread_of(k):
                if in_loop[0]:
                    V.tensor_copy(rt[:, 64:65], st[:, 0, 0:1])
                V.bn_aggr(mv[:, :], st[:, :, :].rearrange("p a b -> p (a b)")).then_inc(S("var_ready"), 1)
                dve.wait_ge(S("std_ready"), k)
                link(V.reciprocal(rstd[:, :], std[:, :]))

            def norm(o, i):
                return V.tensor_scalar(o, i, mv[:, 0:1], rstd[:, 0:1], ALU.subtract, ALU.mult)

            dve.wait_ge(S("x_loaded"), 16)
            for h in range(2):
                stats(h, halves(X)[h])
            spread_of(1)
            norm(xn, X[:, :]).then_inc(S("xn_ready"), 1)
            dve.wait_ge(S("bias_loaded"), 16)
            done = []
            link(V.tensor_copy(btab[:, :], bsrc))
            for rows in (slice(32, 64), slice(64, 96), slice(64, 96)):
                link(V.tensor_tensor(bsrc[rows, :], bsrc[rows, :], btab[rows, :], ALU.subtract))
                V.tensor_copy(btab[rows, :], bsrc[rows, :]).then_inc(S("btab_ready"), 1)
                dve.wait_ge(S("btab_ready"), 1 + len(done))
                done.append(rows)
            dve.wait_ge(S("xn_tr"), 2)
            V.tensor_copy(flat(xnT, 1), h3(B[7])).then_inc(S("xnT_saved"), 1)
            dve.wait_ge(S("index_loaded"), 32)
            dve.wait_ge(S("con_loaded"), 16)
            link(V.tensor_copy(sd_f[:, :, :], sd_i[:, :, :]))
            for a in range(2):
                link(V.tensor_tensor(ohb[:, a, :, :],
                                     iota.rearrange("p (a n) -> p a n", a=1).broadcast_to([P, ET, P]),
                                     sd_f[:, a, :].rearrange("p (t a) -> p t a", a=1).broadcast_to([P, ET, P]),
                                     ALU.is_equal))
            V.tensor_copy(ohd32, ohb[:, 1, :, :])
            V.tensor_tensor(ohb[:, 2, :, :], ohb[:, 0, :, :], ohb[:, 1, :, :], ALU.add).then_inc(S("onehot_ready"), 1)
            for h in range(2):
                dve.wait_ge(S("units_done"), h + 1)
                V.tensor_copy(halves(nodes)[h], h3(B[2 + h])).then_inc(S("nodes_ready"), 1)
            dve.wait_ge(S("adj_done"), 1)
            V.tensor_copy(apT[:, :], B[5][:, 0:P])
            link(V.tensor_tensor(cnt[:, :], B[5][:, P:2 * P], ident, ALU.add))
            V.tensor_scalar(cneg[:, :], cnt[:, :], 0.0, -1e30, ALU.is_equal, ALU.mult)
            V.tensor_copy(deg[:, :], B[5][0:1, 2 * P:3 * P]).then_inc(S("b5_free"), 1)
            dve.wait_ge(S("ept_done"), 2)
            V.tensor_copy(flat(eptT, 1), h3(B[1])).then_inc(S("ept_saved"), 1)
            dve.wait_ge(S("ept_saved"), 2)

            per_layer = 3
            c0 = chain[0]
            with dve.Fori(0, L_GNN) as l:
                chain[0] = c0
                base[0], in_loop[0] = l * per_layer, True
                dve.wait_ge(S("nodes_tr"), 2 * l + 2)
                V.tensor_copy(flat(nodT, 1), h3(B[7])).then_inc(S("nodT_saved"), 1)
                for h in range(2):
                    dve.wait_ge(S("agg_done"), 2 * l + (h + 1))
                    V.tensor_tensor(flat(agg, h), h3(B[4 + h]), flat(eptT, h), ALU.add).then_inc(S("agg_saved"), 1)
                for h in range(2):
                    dve.wait_ge(S("units_done"), l * 8 + (C_LOOP + 3 + h))
                    stats(h, h3(B[h]))
                spread_of(l + 2)
                for h in range(2):
                    norm(halves(z)[h], h3(B[h])).then_inc(S("z_ready"), 1)
                for h in range(2):
                    dve.wait_ge(S("units_done"), l * 8 + (C_LOOP + 6 + h))
                    n = halves(nodes)[h]
                    V.tensor_tensor(n, h3(B[2 + h]), n, ALU.add).then_inc(S("nodes_ready"), 1)
            assert chain[0] == c0 + per_layer
            base[0], chain[0], in_loop[0] = 0, c0 + per_layer * L_GNN, False

            dve.wait_ge(S("nodes_tr"), 2 * L_GNN + 2)
            V.tensor_copy(flat(nodT, 1), h3(B[7])).then_inc(S("nodT_saved"), 1)
            dve.wait_ge(S("b4_free"), L_GNN + 1)
            dve.wait_ge(S("b5_free"), L_GNN + 1)
            ex = early[:, 0, 0:2 * D]
            mqk = mix[:, 0:2, :].rearrange("p a n -> p (a n)")
            V.tensor_scalar(ex, mqk, 0.0, None, ALU.min).then_inc(S("elu_min_ready"), 1)
            link(V.tensor_tensor(X[:, :], X[:, :], nodes[:, :], ALU.add))
            dve.wait_ge(S("elu_exp_ready"), 1)
            V.scalar_tensor_tensor(mqk, mqk, 0.0, ex, ALU.max, ALU.add).then_inc(S("elu_ready"), 1)
            dve.wait_ge(S("units_done"), C_QKV + 1)
            V.tensor_copy(zh[:, 0, 0:HALF], h3(B[0])).then_inc(S("q0_saved"), 1)
            dve.wait_ge(S("units_done"), C_QKV + 3)
            V.tensor_copy(zh[:, 1, 0:HALF], h3(B[2])).then_inc(S("k0_saved"), 1)
            dve.wait_ge(S("q1_tr"), 1)
            V.tensor_copy(blk[0:DH0, 512:1024], B[7][0:DH0, :]).then_inc(S("q1T_saved"), 1)
            dve.wait_ge(S("units_done"), C_QKV + 5)
            V.tensor_copy(flat(agg, 0), h3(B[4])).then_inc(S("v_saved"), 1)
            mxs, sums, rec = sm[:, 0, 0:H0], sm[:, 1, 0:H0], sm[:, 2, 0:H0]

            def g3(ap, n):
                return ap.rearrange("p (g n) -> p g n", n=n)

            def rep(ap, n):
                g = ap.shape[1]
                return ap.rearrange("p (g a) -> p g a", a=1).broadcast_to([P, g, n])

            for h in range(2):
                dve.wait_ge(S("scores_done"), h + 1)
                m4 = mxs[:, 4 * h:4 * h + 4]
                link(V.tensor_reduce(m4, g3(B[2 + h][:, :], P), AX, ALU.max))
                V.tensor_tensor(g3(blk[:, 2048 + 512 * h:2560 + 512 * h], P), g3(B[2 + h][:, :], P), rep(m4, P),
                                ALU.subtract).then_inc(S("shifted"), 1)
            dve.wait_ge(S("kv_clear"), 1)
            for h in range(2):
                dve.wait_ge(S("kv_done"), h + 1)
                for o in range(2):
                    rows = slice(64 * o, 64 * o + 64)
                    last = V.tensor_copy(g3(xnt[rows, h * 390:(h + 1) * 390], 130)[:, :, 65 * o:65 * o + 65],
                                         g3(B[h][rows, 0:390], 130)[:, :, 65 * o:65 * o + 65])
                last.then_inc(S("kv_saved"), 1)
            for h in range(2):
                dve.wait_ge(S("probs_ready"), h + 1)
                link(V.tensor_reduce(sums[:, 4 * h:4 * h + 4], g3(blk[:, 2048 + 512 * h:2560 + 512 * h], P), AX, ALU.add))
            link(V.reciprocal(rec, sums))
            for h in range(2):
                dve.wait_ge(S("lin_done"), h + 1)
                lin = g3(B[6 + h][:, 0:390], 65)
                zr = sm[:, h, 8:14]
                link(V.reciprocal(zr.rearrange("p (g a) -> p g a", a=1), lin[:, :, 64:65]))
                V.tensor_tensor(g3(zh[:, 0, h * HALF:(h + 1) * HALF], 64), lin[:, :, 0:64], rep(zr, 64),
                                ALU.mult).then_inc(S("lin_ready"), 1)
            dve.wait_ge(S("lin_tr"), 2)
            V.tensor_copy(flat(hT, 1), h3(B[1])).then_inc(S("linT_saved"), 1)
            for h in range(2):
                dve.wait_ge(S("attn_done"), h + 1)
                V.tensor_tensor(g3(mix[:, 0, h * HALF:(h + 1) * HALF], DH0), g3(h3(B[6 + h]), DH0),
                                rep(rec[:, 4 * h:4 * h + 4], DH0), ALU.mult).then_inc(S("attn_ready"), 1)
            dve.wait_ge(S("attn_tr"), 2)
            V.tensor_copy(mix[:, 1, HALF:D], h3(B[1])).then_inc(S("attnT_saved"), 1)
            for h in range(2):
                dve.wait_ge(S("units_done"), C_WO + 1 + h)
                xh = halves(X)[h]
                link(V.tensor_tensor(xh, h3(B[4 + h]), xh, ALU.add))
                stats(h, xh)
            spread_of(5)
            norm(nodes[:, :], X[:, :]).then_inc(S("xl_ready"), 1)
            dve.wait_ge(S("xl_tr"), 2)
            V.tensor_copy(flat(nodT, 1), h3(B[7])).then_inc(S("xlT_saved"), 1)

            dve.wait_ge(S("mean_done"), 1)
            lg, eq, wgt, l2, keep = rt[:, 8:12], rt[:, 12:16], rt[:, 16:20], rt[:, 20:24], rt[:, 24:28]
            top, wm = rt[:, 28:30], rt[:, 30:32]
            w4, d4 = con[:, K_W4:K_W4 + 4], con[:, K_D4:K_D4 + 4]
            link(V.tensor_tensor(lg, B[1][:, 0:4], col[:, G_RB0:G_RB0 + 4], ALU.add))
            for s, v in enumerate((lg, l2)):
                link(V.tensor_reduce(top[:, s:s + 1], v, AX, ALU.max))
                link(V.scalar_tensor_tensor(wgt, v, top[:, s:s + 1], w4, ALU.is_equal, ALU.mult))
                link(V.tensor_reduce(wm[:, s:s + 1], wgt, AX, ALU.max))
                link(V.tensor_scalar(oh[:, s, :], wgt, wm[:, s:s + 1], None, ALU.is_equal))
                if s == 0:
                    link(V.tensor_scalar(keep, oh[:, 0, :], -1.0, 1.0, ALU.mult, ALU.add))
                    link(V.tensor_tensor(keep, lg, keep, ALU.mult))
                    link(V.scalar_tensor_tensor(l2, oh[:, 0, :], -3e38, keep, ALU.mult, ALU.add))
            V.tensor_scalar(eidx[:, :], wm, -1.0, float(E_FFN), ALU.mult, ALU.add).then_inc(S("routed"), 1)
            V.tensor_tensor(rt[:, 4:5], top[:, 0:1], top[:, 1:2], ALU.subtract).then_inc(S("margin_ready"), 1)
            dve.wait_ge(S("margin_tanh"), 1)
            V.tensor_scalar(gate[:, 0:1], rt[:, 5:6], 0.5, 0.5, ALU.mult, ALU.add)
            link(V.tensor_scalar(gate[:, 1:2], rt[:, 5:6], -0.5, 0.5, ALU.mult, ALU.add))
            own = rt[:, 66:68]
            tmp = rt[:, 68:76].rearrange("p (s e) -> p s e", s=2)
            link(V.tensor_tensor(tmp, oh[:, :, :], d4.rearrange("p (a e) -> p a e", a=1).broadcast_to([P, 2, 4]), ALU.mult))
            link(V.tensor_reduce(own, tmp, AX, ALU.add))
            V.tensor_copy(selx[:, :].rearrange("p (s n) -> p s n", s=2),
                          own[0:96, :].rearrange("p (s a) -> p s a", a=1).broadcast_to([96, 2, P]))
            link(V.tensor_tensor(rt[:, 76:78], own, gate[:, :], ALU.mult))
            link(V.tensor_reduce(rt[:, 78:79], rt[:, 76:78], AX, ALU.add))
            V.tensor_copy(g4[:, :], rt[0:E_FFN, 78:79].broadcast_to([E_FFN, P])).then_inc(S("gates_ready"), 1)
            silu, mish = oh[:, :, 1], oh[:, :, 2]
            link(V.tensor_tensor(rt[:, 80:82], silu, mish, ALU.add))
            link(V.tensor_scalar(par[:, 0, :], mish, 2.0, 1.0, ALU.mult, ALU.add))
            link(V.tensor_tensor(par[:, 0, :], par[:, 0, :], rt[:, 80:82], ALU.add))
            link(V.scalar_tensor_tensor(par[:, 1, :], rt[:, 80:82], -1.0, gate[:, :], ALU.mult, ALU.mult))
            V.tensor_tensor(par[:, 2, :], par[:, 1, :], gate[:, :], ALU.add).then_inc(S("params_ready"), 1)
            dve.wait_ge(S("params_ready"), 1)

            buf = blk[:, :].rearrange("p (b a n) -> p b a n", b=2, a=4)
            vv = agg[:, :, :].rearrange("p k n -> p (k n)")[:, 0:HALF]
            den = agg[:, :, :].rearrange("p k n -> p (k n)")[:, HALF:D]
            rcp = ept[:, 0:HALF]
            act_s = mix[:, 0:2, :].rearrange("p a (c n) -> p (a c) n", n=HALF)
            per_expert = 4 * 5
            c0 = chain[0]
            with dve.Fori(0, TOP_K) as s:
                chain[0] = c0
                base[0] = s * per_expert

                def p1(t, i):
                    return t[:, i, bass.ds(s, 1)]

                for q in range(4):
                    b = buf[:, q % 2]
                    dve.wait_ge(S("soft_ready"), s * 4 + (q + 1))
                    link(V.tensor_tensor(vv, b[:, 2, :], b[:, 3, :], ALU.mult))
                    mcol = oh[:, bass.ds(s, 1), 2:3].rearrange("p a b -> p (a b)")
                    link(V.tensor_scalar(den, vv, mcol, p1(par, 0), ALU.mult, ALU.add))
                    link(V.reciprocal(rcp, den))
                    link(V.scalar_tensor_tensor(rcp, vv, p1(par, 0), rcp, ALU.subtract, ALU.mult))
                    link(V.scalar_tensor_tensor(rcp, rcp, p1(par, 1), h3(B[q]), ALU.mult, ALU.mult))
                    V.scalar_tensor_tensor(act_s[:, q, :], b[:, 1, :], p1(par, 2), rcp, ALU.mult,
                                           ALU.add).then_inc(S("act_ready"), 1)
            assert chain[0] == c0 + per_expert
            base[0], chain[0] = 0, c0 + per_expert * TOP_K

            for h in range(2):
                dve.wait_ge(S("units_done"), R_L1 - 1 + h)
                n = halves(nodes)[h]
                link(V.tensor_tensor(n, h3(B[6 + h]), n, ALU.add))
                stats(h, n)
            spread_of(6)
            dve.wait_ge(S("xlb_ready"), 1)
            link(V.scalar_tensor_tensor(nodes[:, :], nodes[:, :], mv[:, 0:1], vec[:, V_LG, :], ALU.subtract, ALU.mult))
            for h in range(2):
                xh = halves(X)[h]
                link(V.scalar_tensor_tensor(xh, halves(nodes)[h], rstd[:, 0:1], xh, ALU.mult, ALU.add))
                stats(h, xh)
            spread_of(7)
            norm(nodes[:, :], X[:, :]).then_inc(S("xn2_ready"), 1)
            dve.wait_ge(S("xn2_tr"), 2)
            V.tensor_copy(flat(nodT, 1), h3(B[5])).then_inc(S("xn2T_saved"), 1)

            def attend(g, hsb, bank, before=None):
                for i, v in enumerate((V_AS1 + 2 * g, V_AD1 + 2 * g)):
                    V.tensor_tensor_reduce(out=mvs, in0=hsb, in1=vec[:, v, :], scale=1.0, scalar=0.0,
                                           op0=ALU.mult, op1=ALU.add, accum_out=ab[:, i:i + 1]).then_inc(S("dve_chain"), 1)
                    chain[0] += 1
                    dve.wait_ge(S("dve_chain"), chain[0])
                V.tensor_scalar(blk[:, 0:P], ident, ab[:, 0:1], None, ALU.mult).then_inc(S("diag_ready"), 1)
                if before:
                    before()
                dve.wait_ge(S("spread_done"), g + 1)
                lo = blk[:, P:2 * P]
                sc = blk[:, 3 * P:4 * P]
                link(V.tensor_scalar(sc, bank[:, 0:P], ab[:, 1:2], None, ALU.add))
                link(V.scalar_tensor_tensor(sc, sc, 0.2, sc, ALU.mult, ALU.max))
                link(V.tensor_tensor(sc, sc, cneg[:, :], ALU.add))
                link(V.tensor_reduce(ab[:, 2:3], sc, AX, ALU.max))
                V.tensor_scalar(lo, sc, ab[:, 2:3], None, ALU.subtract).then_inc(S("gat_logit"), 1)
                dve.wait_ge(S("gat_exp"), g + 1)
                link(V.tensor_tensor(lo, lo, cnt[:, :], ALU.mult))
                link(V.tensor_reduce(ab[:, 3:4], lo, AX, ALU.add))
                link(V.reciprocal(ab[:, 4:5], ab[:, 3:4]))
                V.tensor_scalar(lo, lo, ab[:, 4:5], None, ALU.mult).then_inc(S("alpha_ready"), 1)
                dve.wait_ge(S("alpha_tr"), g + 1)
                V.tensor_copy(blk[:, 2 * P:3 * P], B[7 - 4 * g][:, 0:P]).then_inc(S("alphaT_saved"), 1)

            mvs = blk[:, 2048:2048 + D]
            dve.wait_ge(S("h1_saved"), 2)
            attend(0, agg[:, :, :].rearrange("p k n -> p (k n)"), B[6])
            for h in range(2):
                dve.wait_ge(S("units_done"), R_L1 + 3 + h)
                V.tensor_copy(mix[:, 1, h * HALF:(h + 1) * HALF], h3(B[4 + h])).then_inc(S("mk1_saved"), 1)
            for h in range(2):
                dve.wait_ge(S("units_done"), R_L1 + 7 + h)
                link(V.tensor_copy(ept[:, h * HALF:(h + 1) * HALF], h3(B[2 + h])))

            def between():
                dve.wait_ge(S("mq1_tr"), 2)
                V.tensor_copy(flat(xnT, 1), h3(B[7])).then_inc(S("mq1T_saved"), 1)

            attend(1, ept[:, 0:D], B[2], between)
            for h in range(2):
                dve.wait_ge(S("x3_done"), h + 1)
                xh = halves(X)[h]
                link(V.tensor_tensor(xh, h3(B[h]), xh, ALU.add))
                stats(h, xh)
            spread_of(8)
            norm(nodes[:, :], X[:, :]).then_inc(S("xl3_ready"), 1)
            dve.wait_ge(S("xl3_tr"), 2)
            V.tensor_copy(flat(nodT, 1), h3(B[5])).then_inc(S("xl3T_saved"), 1)
            dve.wait_ge(S("route1_done"), 1)
            l8, w8, m8 = rt[:, 8:16], rt[:, 16:24], rt[:, 24:32]
            link(V.tensor_tensor(l8, B[6][:, 0:E_MOE], col[:, G_RB1:G_RB1 + E_MOE], ALU.add))
            link(V.tensor_reduce(rt[:, 50:51], l8, AX, ALU.max))
            V.tensor_scalar(rt[:, 32:40], l8, rt[:, 50:51], None, ALU.subtract).then_inc(S("moe_shift"), 1)
            link(V.scalar_tensor_tensor(w8, l8, rt[:, 50:51], con[:, K_W8:K_W8 + 8], ALU.is_equal, ALU.mult))
            link(V.tensor_reduce(rt[:, 51:52], w8, AX, ALU.max))
            link(V.tensor_scalar(m8, w8, rt[:, 51:52], None, ALU.is_equal))
            dve.wait_ge(S("moe_exp"), 1)
            link(V.reciprocal(rt[:, 52:53], rt[:, 48:49]))
            hm = agg[:, :, :].rearrange("p k n -> p (k n)")[:, 0:FH]
            dve.wait_ge(S("silu_ready"), 1)
            link(V.tensor_tensor(g3(z[:, 0:FH], HID), g3(z[:, 0:FH], HID), rep(m8, HID), ALU.mult))
            dve.wait_ge(S("moe_up_done"), 2)
            V.tensor_tensor(hm, B[3][:, :], z[:, 0:FH], ALU.mult).then_inc(S("moe_h_ready"), 1)
            o16 = blk[:, 0:HALF].bitcast(bf16)
            for h in range(2):
                dve.wait_ge(S("moe_done"), h + 1)
                link(V.tensor_copy(o16[:, h * HALF:(h + 1) * HALF], h3(B[h])))
                V.scalar_tensor_tensor(halves(nodes)[h], o16[:, h * HALF:(h + 1) * HALF], rt[:, 52:53],
                                       halves(X)[h], ALU.mult, ALU.add).then_inc(S("out_ready"), 1)

        @block.gpsimd
        def _(pool):
            pool.wait_ge(S("b4_free"), L_GNN + 1)
            pool.wait_ge(S("b5_free"), L_GNN + 1)
            va = ept[:, :].rearrange("p (g n) -> p g n", n=65)
            nc.gpsimd.memset(va[:, :, 64:65], 1.0)
            nc.gpsimd.tensor_copy(va[:, :, 0:64], mix[:, 2, :].rearrange("p (g n) -> p g n", n=64)).then_inc(S("vaug_ready"), 1)
            nc.gpsimd.memset(xnt[:, :], 0.0).then_inc(S("kv_clear"), 1)
            pool.wait_ge(S("xl_ready"), 1)
            pool.wait_ge(S("vec_loaded"), 16)
            nc.gpsimd.tensor_tensor(X[:, :], X[:, :], vec[:, V_LB, :], ALU.add).then_inc(S("xlb_ready"), 1)
            pool.wait_ge(S("xn2_ready"), 1)
            nc.gpsimd.memset(zh[:, 0, :], 0.0).then_inc(S("zh_clear"), 1)


def kernel(**inputs):
    import numpy as _np
    import concourse.bacc as _bacc
    from concourse import mybir as _mybir
    from concourse.bass_utils import run_bass_kernel_spmd as _run
    import ml_dtypes as _ml

    g = {k: _np.asarray(v) for k, v in inputs.items()}

    def chunk(w):
        k, n = w.shape
        return w.reshape(KT, P, n // HALF, HALF).transpose(2, 1, 0, 3).reshape(n // HALF, P, CH)

    def colk(v):
        return v.reshape(-1, KT, P).transpose(2, 0, 1).reshape(P, -1)

    parts = [chunk(g["L0_gnn_Wn"].T)]
    wm = g["L0_mix_w_qkv"].T
    for l in range(L_GNN):
        w1, w2 = g["L0_gnn_W1"][l].T, g["L0_gnn_W2"][l].T
        m = chunk(wm[:, l * D:(l + 1) * D])
        parts += [chunk(w1[:D]), chunk(w1[D:]), m[:1], chunk(w2), m[1:]]
    parts += [chunk(g["L0_gnn_Wqkv"].T), chunk(g["L0_mix_w_proj"].T), chunk(g["L0_gnn_Wo"].T)]
    for e in range(E_FFN):
        parts += [chunk(g["L0_ffn_w1"][e]), chunk(g["L0_ffn_w2"][e][:D]), chunk(g["L0_ffn_w2"][e][D:])]
    parts += [chunk(g["L1_gnn_W1"]), chunk(g["L1_mix_w_qkv"]), chunk(g["L1_gnn_W2"]), chunk(g["L1_mix_w_proj"])]
    chunks = _np.concatenate(parts)

    def rows(w):
        return w.reshape(-1, P, w.shape[1]).transpose(1, 0, 2).reshape(P, -1)

    up = [rows(g[n].transpose(1, 0, 2).reshape(D, FH)) for n in ("L1_ffn_w1", "L1_ffn_w2")]
    moe_w = _np.concatenate(up + [rows(g["L1_ffn_w3"].reshape(FH, D))], axis=1)

    table = _np.zeros((32, 3 * D), _np.float32)
    table[:N_BIAS, :D] = _np.concatenate([
        g["L0_gnn_bn"][None], g["L0_gnn_b1"], g["L0_gnn_b2"], g["L0_gnn_bqkv"].reshape(3, D), g["L0_gnn_bo"][None],
        g["L0_mix_b_proj"][None], g["L1_gnn_b2"][None], g["L1_mix_b_proj"][None]])
    table[:E_FFN, D:] = g["L0_ffn_b1"]
    bias_rows = _np.concatenate([table] * 3)

    cols = _np.concatenate([
        colk(g["L0_gnn_ln_g"]), colk(g["L0_gnn_ln_b"]), colk(g["L1_gnn_b1"]), rows(g["L0_ffn_router_w"].T),
        _np.broadcast_to(g["L0_ffn_router_b"], (P, E_FFN)), rows(g["L1_ffn_router_w"]),
        _np.broadcast_to(g["L1_ffn_router_b"], (P, E_MOE))], axis=1)
    vecs = _np.concatenate([g[n] for n in ("L1_gnn_att_src1", "L1_gnn_att_dst1", "L1_gnn_att_src2", "L1_gnn_att_dst2",
                                           "L0_ffn_ln_g", "L0_ffn_ln_b")])

    cst = _np.zeros((P, N_CST), _np.float32)
    cst[:, K_ID:K_ID + P] = _np.eye(P)
    cst[:, K_IOTA:K_IOTA + P] = _np.arange(P)
    cst[:, K_ONE:K_ONE + P] = 1
    cst[:, K_AVG:K_AVG + P] = 1 / P
    cst[:, K_EPS] = EPS
    cst[:, K_W4:K_W4 + 4] = E_FFN - _np.arange(E_FFN)
    cst[:, K_D4:K_D4 + 4] = _np.arange(P)[:, None] % 32 == _np.arange(E_FFN)
    cst[:, K_W8:K_W8 + 8] = E_MOE - _np.arange(E_MOE)
    sel = _np.zeros((96, N_BIAS, P), _ml.bfloat16)
    for b in range(N_BIAS):
        sel[b::32, b] = 1
    sel = sel.reshape(96, -1)

    f = [("x", g["x"]), ("src", g["src"]), ("dst", g["dst"]), ("edge", g["edge_attr_256"]),
         ("w_edge", rows(g["L0_gnn_We"].T)), ("be", g["L0_gnn_be"][None]), ("chunks", chunks), ("moe_w", moe_w),
         ("bias_rows", bias_rows), ("gate_b2", g["L0_ffn_b2"]), ("cols", cols), ("vecs", vecs), ("cst", cst),
         ("sel", sel)]
    nc = _bacc.Bacc("TRN2", target_bir_lowering=False, num_devices=1)
    arrays, args = {}, []
    for name, a in f:
        a = _np.ascontiguousarray(a)
        arrays[f"in_{name}"] = a
        args.append(nc.dram_tensor(f"in_{name}", a.shape, _mybir.dt.from_np(a.dtype), kind="ExternalInput").ap())
    args.append(nc.dram_tensor("out_x", (P, D), _mybir.dt.float32, kind="ExternalOutput").ap())
    gps_kernel(nc, *args)
    r = _run(nc, [arrays], core_ids=[0])
    return r.results[0]["out_x"]
```

```python
import numpy as np
import concourse.bass as bass
from concourse import mybir
from contextlib import ExitStack

P = 128
D = 768
HALF = D // 2
KT = D // P
E_EDGES = 2048
ET = E_EDGES // P
DE = 256
L_GNN = 3
CH = KT * HALF
SLOTS = 8
H0, DH0 = 8, D // 8
HM, DM = 12, D // 12
TOP_K = 2
E_FFN, E_MOE, HID = 4, 8, 64
FH = E_MOE * HID
EPS = 1e-5

C_WN = 0
C_LOOP = 2
C_QKV = C_LOOP + 8 * L_GNN
C_MIXP = C_QKV + 6
C_WO = C_MIXP + 2
C_FFN = C_WO + 2
C_GAT1 = C_FFN + 8 * E_FFN
C_L1 = C_GAT1 + 2
N_CHUNKS = C_L1 + 10
R_FFN = C_FFN
FFN_ORDER = [(0, 1), (0, 2), (0, 3), (0, 4), (0, 5), (1, 1), (1, 2), (1, 3), (0, 6), (0, 7), (1, 4), (1, 5),
             (1, 6), (1, 7)]
R_EXP = R_FFN + E_FFN
R_L1 = R_EXP + len(FFN_ORDER)
QUARTERS = [(0, 0), (1, 0), (0, 1), (0, 2), (0, 3), (1, 1), (1, 2), (1, 3)]
B_BN, B_B1, B_B2, B_QKV, B_BO, B_MIX0, B_GAT2, B_MIX1 = 0, 1, 4, 7, 10, 11, 12, 13
N_BIAS = 14
K_ID, K_IOTA, K_ONE, K_AVG, K_EPS, K_W4, K_D4, K_W8, K_HALF = 0, 128, 256, 384, 512, 513, 517, 521, 529
N_CST = 530
G_G, G_B, G_GB1, G_RW0, G_RB0, G_RW1, G_RB1 = 0, 18, 36, 42, 66, 70, 118
N_COLS = 126
V_AS1, V_AD1, V_AS2, V_AD2, V_LG, V_LB = range(6)


def gps_kernel(nc, x, src, dst, edge, w_edge, be_row, chunks, moe_w, bias_rows, gate_b2, cols, vecs,
               cst, sel, out):
    f32, bf16, i32 = mybir.dt.float32, mybir.dt.bfloat16, mybir.dt.int32
    ALU, ACT, AX = mybir.AluOpType, mybir.ActivationFunctionType, mybir.AxisListType.X
    ctx = ExitStack()
    with ctx:
        sems = {}

        def S(name):
            if name not in sems:
                sems[name] = ctx.enter_context(nc.semaphore(name))
            return sems[name]

        def sb(name, shape, dt=f32):
            return ctx.enter_context(nc.sbuf_tensor(name, shape, dt))

        ring = sb("ring", [P, SLOTS, CH])
        early = sb("early", [P, 2, CH])
        moe = sb("moe", [P, 4 * CH])
        vec = sb("vec", [P, 6, D])
        X = sb("X", [P, D])
        nodes = sb("nodes", [P, D])
        nodT = sb("nodT", [P, KT, P])
        agg = sb("agg", [P, KT, P])
        ept = sb("ept", [P, 780])
        xnt = sb("xnt", [P, 780])
        zh = sb("zh", [P, 2, D])
        mix = sb("mix", [P, 3, D])
        blk = sb("blk", [P, 3072])
        con = sb("con", [P, N_CST])
        col = sb("col", [P, N_COLS])
        selb = sb("selb", [96, N_BIAS * P], bf16)
        btab = sb("btab", [96, 3 * D], bf16)
        b2f = sb("b2f", [E_FFN, D])
        apT = sb("apT", [P, P])
        cnt = sb("cnt", [P, P])
        cneg = sb("cneg", [P, P])
        deg = sb("deg", [1, P])
        sd_i = sb("sd_i", [P, 2, ET], i32)
        sd_f = sb("sd_f", [P, 2, ET])
        st = sb("st", [P, 2, 6])
        mv = sb("mv", [P, 2])
        std = sb("std", [P, 1])
        rstd = sb("rstd", [P, 1])
        sm = sb("sm", [P, 3, 16])
        rt = sb("rt", [P, 96])
        oh = sb("oh", [P, TOP_K, E_FFN])
        gate = sb("gate", [P, TOP_K])
        par = sb("par", [P, 3, TOP_K])
        eidx = sb("eidx", [P, TOP_K], i32)
        selx = sb("selx", [96, TOP_K * P], bf16)
        g4 = sb("g4", [E_FFN, P])
        ab = sb("ab", [P, 8])
        half_c = con[:, K_EPS:K_EPS + 1]

        ident = con[:, K_ID:K_ID + P]
        iota = con[:, K_IOTA:K_IOTA + P]
        xnT = xnt[:, 0:D].rearrange("p (k n) -> p k n", k=KT)
        eptT = ept[:, 0:D].rearrange("p (k n) -> p k n", k=KT)
        hT = zh[:, 1, :].rearrange("p (k n) -> p k n", k=KT)
        z = zh[:, 0, :]
        xn = mix[:, 0, :]
        edg = moe[:, 0:4096].rearrange("p (t k) -> p t k", t=ET)
        ohb = moe[:, 4096:7168].bitcast(bf16).rearrange("p (a t n) -> p a t n", a=3, t=ET)
        ohd32 = moe[:, 7168:9216].rearrange("p (t n) -> p t n", t=ET)
        we = zh[:, :, :]
        eat = agg[:, 0:2, :]
        be_s = blk[0:1, 0:D]
        bsrc = early[0:96, 0, :]

        B = [ctx.enter_context(nc.psum_tensor(f"B{i}", [P, 512], f32)) for i in range(8)]

        block = ctx.enter_context(nc.Block())

        @block.sync
        def _(sp):
            sp.dma_start(X[:, :], x).then_inc(S("x_loaded"), 16)
            sp.dma_start(con[:, :], cst).then_inc(S("con_loaded"), 16)

            def load(slot, index):
                sp.dma_start(ring[:, slot, :], chunks[index]).then_inc(S(f"slot{slot}"), 16)

            load(0, 0)
            sp.dma_start(sd_i[:, 0, :], src.rearrange("(p t) -> p t", t=ET)).then_inc(S("index_loaded"), 16)
            sp.dma_start(sd_i[:, 1, :], dst.rearrange("(p t) -> p t", t=ET)).then_inc(S("index_loaded"), 16)
            sp.dma_start(bsrc[:, 0:D], bias_rows[:, 0:D]).then_inc(S("bias_loaded"), 16)
            sp.dma_start(selb[:, :], sel).then_inc(S("sel_loaded"), 16)
            load(1, 1)
            sp.dma_start(edg, edge.rearrange("(p t) k -> p t k", t=ET)).then_inc(S("edge_loaded"), 16)
            sp.dma_start(we, w_edge.rearrange("p (k f) -> p k f", k=2)).then_inc(S("we_loaded"), 16)
            sp.dma_start(be_s, be_row).then_inc(S("we_loaded"), 16)
            load(2, 2)
            load(3, 3)
            sp.dma_start(col[:, :], cols).then_inc(S("cols_loaded"), 16)
            load(4, 4)
            sp.dma_start(bsrc[:, D:3 * D], bias_rows[:, D:3 * D]).then_inc(S("bias2_loaded"), 16)
            for c in range(5, SLOTS):
                load(c, c)
            with sp.Fori(1, C_FFN // SLOTS) as r:
                for k in range(SLOTS):
                    sp.wait_ge(S("units_done"), (r - 1) * SLOTS + (k + 1))
                    load(k, r * SLOTS + k)
            for c in range(C_FFN // SLOTS * SLOTS, C_FFN):
                sp.wait_ge(S("units_done"), c - SLOTS + 1)
                load(c % SLOTS, c)
            for e in range(E_FFN):
                sp.wait_ge(S("units_done"), R_FFN + e - SLOTS + 1)
                load((R_FFN + e) % SLOTS, C_FFN + 8 * e)
            sp.wait_ge(S("elu_ready"), 1)
            sp.dma_start(vec[:, :, :], vecs.rearrange("(a v) -> a v", a=1).broadcast_to([P, 6 * D])
                         .rearrange("p (a v) -> p a v", a=6)).then_inc(S("vec_loaded"), 16)
            sp.dma_start(b2f[:, :], gate_b2).then_inc(S("b2_loaded"), 16)
            for h in range(2):
                sp.dma_start(early[:, h, :], chunks[C_GAT1 + h]).then_inc(S(f"early{h}_loaded"), 16)
            sp.dma_start(moe[:, :], moe_w).then_inc(S("moe_loaded"), 16)
            sp.wait_ge(S("routed"), 1)
            chosen = [sp.value_load(eidx[0:1, s:s + 1], min_val=0, max_val=E_FFN - 1) for s in range(TOP_K)]
            for i, (s, j) in enumerate(FFN_ORDER):
                sp.wait_ge(S("units_done"), R_EXP + i - SLOTS + 1)
                load((R_EXP + i) % SLOTS, chosen[s] * 8 + (C_FFN + j))
            for j in range(10):
                c = R_L1 + j
                sp.wait_ge(S("units_done"), c - SLOTS + 1)
                load(c % SLOTS, C_L1 + j)
            sp.wait_ge(S("out_ready"), 2)
            sp.dma_start(out, nodes[:, :]).then_inc(S("out_stored"), 16)
            sp.wait_ge(S("out_stored"), 16)

        @block.tensor
        def _(pe):
            mm = nc.tensor.matmul

            def transposes(src_tiles, bank, rows=P):
                for i, t in enumerate(src_tiles):
                    last = nc.tensor.transpose(bank[0:rows, i * P:(i + 1) * P], t, ident)
                return last

            def tiles(row, half, n=3, w=P):
                return [row[:, (half * n + i) * w:(half * n + i + 1) * w] for i in range(n)]

            def bias(bank, row, half, start=True, stop=False):
                return mm(bank[:, 0:HALF], selb[:, row * P:(row + 1) * P], btab[:, half * HALF:(half + 1) * HALF],
                          start=start, stop=stop)

            def unit(bank, lhsT, chunk, start=False, stop=True, skip=False, second=None):
                for k in range(KT):
                    if second and k == KT // 2:
                        second()
                    last = mm(bank[:, 0:HALF], lhsT[:, k, :], chunk[:, k * HALF:(k + 1) * HALF],
                              start=start and k == 0, stop=stop and k == KT - 1, skip_group_check=skip)
                return last

            def ring_unit(c, turn, bank, lhsT, **kw):
                pe.wait_ge(S(f"slot{c % SLOTS}"), 16 * (turn + 1))
                unit(bank, lhsT, ring[:, c % SLOTS, :], **kw).then_inc(S("units_done"), 1)

            pe.wait_ge(S("con_loaded"), 16)
            pe.wait_ge(S("xn_ready"), 1)
            for h in range(2):
                transposes(tiles(xn, h), B[6 + h]).then_inc(S("xn_tr"), 1)
            pe.wait_ge(S("xnT_saved"), 2)
            for h in range(2):
                ring_unit(h, 0, B[2 + h], xnT, start=True, stop=False)
                if h == 0:
                    pe.wait_ge(S("sel_loaded"), 16)
                    pe.wait_ge(S("btab_ready"), 3)
                bias(B[2 + h], B_BN, h, start=False, stop=True).then_inc(S("wn_done"), 1)
            pe.wait_ge(S("edge_loaded"), 16)
            pe.wait_ge(S("onehot_ready"), 1)
            for k in range(2):
                for t in range(ET):
                    last = mm(B[4][:, k * P:(k + 1) * P], edg[:, t, k * P:(k + 1) * P], ohd32[:, t, :],
                              start=t == 0, stop=t == ET - 1)
            last.then_inc(S("eat_done"), 1)
            for o, a, b in ((0, 2, 1), (P, 1, 0)):
                for t in range(ET):
                    last = mm(B[5][:, o:o + P], ohb[:, a, t, :], ohb[:, b, t, :], start=t == 0, stop=t == ET - 1)
            last.then_inc(S("adj_done"), 1)
            pe.wait_ge(S("we_loaded"), 32)
            pe.wait_ge(S("b5_free"), 1)
            mm(B[5][0:1, 2 * P:3 * P], con[:, K_HALF:K_HALF + 1], apT[:, :], start=True, stop=True).then_inc(S("deg_done"), 1)
            pe.wait_ge(S("b4_free"), 1)
            for f in range(KT):
                o = B[f // 3][:, f % 3 * P:(f % 3 + 1) * P]
                for k in range(2):
                    mm(o, we[:, k, f * P:(f + 1) * P], eat[:, k, :], start=k == 0, stop=False)
                if f == 0:
                    pe.wait_ge(S("deg_saved"), 1)
                last = mm(o, be_s[:, f * P:(f + 1) * P], deg[:, :], start=False, stop=True)
                if f % 3 == 2:
                    last.then_inc(S("ept_done"), 1)
            pe.wait_ge(S("ept_saved"), 2)

            with pe.Fori(0, L_GNN) as l:
                for h in range(2):
                    pe.wait_ge(S("nodes_ready"), 2 * l + (h + 1))
                    transposes(tiles(nodes, h), B[6 + h]).then_inc(S("nodes_tr"), 1)
                for h in range(2):
                    pe.wait_ge(S(f"b{4 + h}_free"), l + 1)
                    for i in range(3):
                        f = 3 * h + i
                        last = mm(B[4 + h][:, i * P:(i + 1) * P], nodes[:, f * P:(f + 1) * P], apT[:, :],
                                  start=True, stop=True)
                    last.then_inc(S("agg_done"), 1)
                pe.wait_ge(S("nodT_saved"), 2 * l + 2)
                for h in range(2):
                    mm(B[h][:, 0:HALF], selb[:, bass.ds((l + B_B1) * P, P)], btab[:, h * HALF:(h + 1) * HALF],
                       start=True, stop=False)
                    ring_unit(C_LOOP + h, l + (C_LOOP + h) // SLOTS, B[h], nodT, stop=False)
                pe.wait_ge(S("agg_saved"), 2 * l + 2)
                for h in range(2):
                    c = C_LOOP + 2 + h
                    ring_unit(c, l + c // SLOTS, B[h], agg)
                c = C_LOOP + 4
                ring_unit(c, l + c // SLOTS, B[4], xnT, start=True)
                for h in range(2):
                    pe.wait_ge(S("z_ready"), 2 * l + (h + 1))
                    transposes(tiles(z, h), B[6 + h]).then_inc(S("z_tr"), 1)
                for h in range(2):
                    mm(B[2 + h][:, 0:HALF], selb[:, bass.ds((l + B_B2) * P, P)],
                       btab[:, h * HALF:(h + 1) * HALF], start=True, stop=False)
                    c = C_LOOP + 5 + h
                    if h == 0:
                        pe.wait_ge(S("hT0_saved"), l + 1)
                    ring_unit(c, l + c // SLOTS, B[2 + h], hT,
                              second=(lambda: pe.wait_ge(S("hT1_saved"), l + 1)) if h == 0 else None)
                c = C_LOOP + 7
                ring_unit(c, l + c // SLOTS, B[5], xnT, start=True)

            for h in range(2):
                pe.wait_ge(S("nodes_ready"), 2 * L_GNN + h + 1)
                transposes(tiles(nodes, h), B[6 + h]).then_inc(S("nodes_tr"), 1)

            def qkv_unit(i, bank):
                bias(bank, B_QKV + i // 2, i % 2)
                ring_unit(C_QKV + i, (C_QKV + i) // SLOTS, bank, nodT)

            pe.wait_ge(S("nodT_saved"), 2 * L_GNN + 2)
            for i in range(4):
                qkv_unit(i, B[i])
            q0, k0 = zh[:, 0, :], zh[:, 1, :]
            for h in range(2):
                pe.wait_ge(S(f"q{h}_saved"), 1)
                transposes(tiles(q0, h, 4, DH0), B[6 + h], DH0).then_inc(S(f"q{h}_tr"), 1)
            pe.wait_ge(S("b4_free"), L_GNN + 1)
            qkv_unit(4, B[4])
            for h in range(2):
                pe.wait_ge(S(f"k{h}_saved"), 1)
                transposes(tiles(k0, h, 4, DH0), B[h], DH0).then_inc(S(f"k{h}_tr"), 1)
            pe.wait_ge(S("b5_free"), L_GNN + 1)
            qkv_unit(5, B[5])
            qT = blk[0:DH0, 0:1024]
            kT = blk[0:DH0, 1024:2048]
            for h in range(2):
                pe.wait_ge(S(f"q{h}T_saved"), 1)
                pe.wait_ge(S(f"k{h}T_saved"), 1)
                for i in range(4):
                    o = (4 * h + i) * P
                    last = mm(B[2 + h][:, i * P:(i + 1) * P], qT[:, o:o + P], kT[:, o:o + P], start=True, stop=True)
                last.then_inc(S("scores_done"), 1)
            pe.wait_ge(S("elu_ready"), 1)
            for h in range(2):
                transposes(tiles(mix[:, 0, :], h), B[6 + h]).then_inc(S("mq_tr"), 1)
            pe.wait_ge(S("vaug_ready"), 1)
            for h in range(2):
                for i in range(3):
                    g = 3 * h + i
                    last = mm(B[h][:, i * 130:(i + 1) * 130], mix[:, 1, g * P:(g + 1) * P],
                              ept[:, g * 130:(g + 1) * 130], start=True, stop=True)
                last.then_inc(S("kv_done"), 1)
            pe.wait_ge(S("mqT_saved"), 2)
            for h in range(2):
                pe.wait_ge(S("kv_saved"), h + 1)
                for i in range(3):
                    g = 3 * h + i
                    last = mm(B[6 + h][:, i * 130:(i + 1) * 130], nodT[:, g, :],
                              xnt[:, g * 130:(g + 1) * 130], start=True, stop=True)
                last.then_inc(S("lin_done"), 1)
            probs, probT = blk[:, 2048:3072], blk[:, 0:1024]
            for h in range(2):
                pe.wait_ge(S("probs_ready"), h + 1)
                transposes([probs[:, (4 * h + i) * P:(4 * h + i + 1) * P] for i in range(4)],
                           B[2 + h]).then_inc(S("probs_tr"), 1)
            pe.wait_ge(S("lin_ready"), 2)
            for h in range(2):
                transposes(tiles(zh[:, 0, :], h), B[h]).then_inc(S("lin_tr"), 1)
            v0 = agg[:, :, :].rearrange("p k n -> p (k n)")
            for h in range(2):
                pe.wait_ge(S("probT_saved"), h + 1)
                for i in range(4):
                    o = 4 * h + i
                    last = mm(B[6 + h][:, i * DH0:(i + 1) * DH0], probT[:, o * P:(o + 1) * P],
                              v0[:, o * DH0:(o + 1) * DH0], start=True, stop=True)
                last.then_inc(S("attn_done"), 1)
            pe.wait_ge(S("v_saved"), 2)
            pe.wait_ge(S("linT_saved"), 2)
            for h in range(2):
                bias(B[4 + h], B_BO, h)
                bias(B[4 + h], B_MIX0, h, start=False)
                ring_unit(C_MIXP + h, (C_MIXP + h) // SLOTS, B[4 + h], hT, stop=False)
            for h in range(2):
                pe.wait_ge(S("attn_ready"), h + 1)
                transposes(tiles(mix[:, 0, :], h), B[h]).then_inc(S("attn_tr"), 1)
            attnT = mix[:, 1, :].rearrange("p (k n) -> p k n", k=KT)
            pe.wait_ge(S("attnT_saved"), 2)
            for h in range(2):
                ring_unit(C_WO + h, (C_WO + h) // SLOTS, B[4 + h], attnT)

            for h in range(2):
                pe.wait_ge(S("xl_ready"), h + 1)
                transposes(tiles(nodes, h), B[6 + h]).then_inc(S("xl_tr"), 1)
            pe.wait_ge(S("cols_loaded"), 16)
            pe.wait_ge(S("xlT_saved"), 2)
            for k in range(KT):
                last = mm(B[0][:, 0:E_FFN], nodT[:, k, :], col[:, G_RW0 + k * 4:G_RW0 + k * 4 + 4],
                          start=k == 0, stop=k == KT - 1)
            last.then_inc(S("logit_done"), 1)
            pe.wait_ge(S("logit_saved"), 1)
            mm(B[1][:, 0:E_FFN], con[:, K_AVG:K_AVG + P], rt[:, 0:4], start=True, stop=True).then_inc(S("mean_done"), 1)
            act_s = mix[:, 0, :].rearrange("p (b n) -> p b n", b=2)
            heT = [zh[:, :, :].rearrange("p a (k n) -> p (a k) n", n=P),
                   mix[:, 1:3, :].rearrange("p a (k n) -> p (a k) n", n=P)]

            def up(i):
                s, q = QUARTERS[i]
                bank = B[i % 4]
                if i >= 4:
                    pe.wait_ge(S("act_ready"), i - 3)
                if q == 0:
                    for e in range(E_FFN if s == 0 else 0):
                        pe.wait_ge(S(f"slot{(R_FFN + e) % SLOTS}"), 16 * ((R_FFN + e) // SLOTS + 1))
                    for k in range(KT):
                        last = mm(
                           bank[:, 0:HALF], nodT[:, k, :],
                           ring[:, bass.ds(mine[s] + R_FFN % SLOTS, 1), k * HALF:(k + 1) * HALF]
                           .rearrange("p a n -> p (a n)"), start=k == 0, stop=False)
                    if s == 1:
                        last.then_inc(S("units_done"), E_FFN)
                else:
                    c = R_EXP + FFN_ORDER.index((s, q))
                    pe.wait_ge(S(f"slot{c % SLOTS}"), 16 * (c // SLOTS + 1))
                    unit(bank, nodT, ring[:, c % SLOTS, :], start=True, stop=False).then_inc(S("units_done"), 1)
                if i == 0:
                    pe.wait_ge(S("selx_ready"), 1)
                mm(bank[:, 0:HALF], selx[:, s * P:(s + 1) * P], btab[:, D + q * HALF:D + (q + 1) * HALF],
                   start=False, stop=True).then_inc(S("up_done"), 1)

            def turn(i):
                pe.wait_ge(S("act_ready"), i + 1)
                if i >= 2:
                    pe.wait_ge(S("heT_saved"), i - 1)
                transposes([act_s[:, i % 2, j * P:(j + 1) * P] for j in range(3)], B[4 + i % 2]).then_inc(S("act_tr"), 1)

            def down(s, g):
                for h in range(2):
                    c = R_EXP + FFN_ORDER.index((s, 4 + 2 * g + h))
                    pe.wait_ge(S("heT_saved"), QUARTERS.index((s, 2 * g + 1)) + 1)
                    ring_unit(c, c // SLOTS, B[6 + h], heT[s][:, 6 * g:6 * g + 6, :], stop=s == 1 and g == 1)

            pe.wait_ge(S("routed"), 1)
            mine = [pe.value_load(eidx[0:1, s:s + 1], min_val=0, max_val=E_FFN - 1) for s in range(TOP_K)]
            up(0)
            up(1)
            pe.wait_ge(S("b2_loaded"), 16)
            pe.wait_ge(S("gates_ready"), 1)
            for h in range(2):
                mm(B[6 + h][:, 0:HALF], g4[:, :], b2f[:, h * HALF:(h + 1) * HALF], start=True, stop=False)
            up(2)
            turn(0)
            up(3)
            turn(1)
            up(4)
            turn(2)
            down(0, 0)
            turn(3)
            up(5)
            turn(4)
            up(6)
            turn(5)
            up(7)
            turn(6)
            down(0, 1)
            turn(7)
            down(1, 0)
            down(1, 1)

            for h in range(2):
                pe.wait_ge(S("xn2_ready"), h + 1)
                transposes(tiles(nodes, h), B[4 + h]).then_inc(S("xn2_tr"), 1)
            pe.wait_ge(S("xn2T_saved"), 2)

            def l1(j, bank, lhsT, **kw):
                c = R_L1 + j
                ring_unit(c, c // SLOTS, bank, lhsT, **kw)

            for h in range(2):
                pe.wait_ge(S(f"early{h}_loaded"), 16)
                unit(B[h], nodT, early[:, h, :], start=True).then_inc(S("gat_h1_done"), 1)
            l1(0, B[2], nodT, start=True)
            l1(1, B[3], nodT, start=True)

            def spread(g, bank):
                pe.wait_ge(S("diag_ready"), g + 1)
                mm(bank[:, 0:P], con[:, K_ONE:K_ONE + P], blk[:, 0:P], start=True, stop=True).then_inc(S("spread_done"), 1)

            def alpha_turn(g, bank):
                pe.wait_ge(S("alpha_ready"), g + 1)
                nc.tensor.transpose(bank[:, 0:P], blk[:, P:2 * P], ident).then_inc(S("alpha_tr"), 1)

            spread(0, B[6])
            pe.wait_ge(S("xn2T_saved"), 2)
            l1(2, B[4], nodT, start=True)
            alpha_turn(0, B[7])
            l1(3, B[5], nodT, start=True)
            h1 = agg[:, :, :].rearrange("p k n -> p (k n)")
            h2 = ept[:, 0:D]
            alT = blk[:, 2 * P:3 * P]
            pe.wait_ge(S("alphaT_saved"), 1)
            for h in range(2):
                for i in range(3):
                    f = 3 * h + i
                    last = mm(B[6 + h][:, i * P:(i + 1) * P], h1[:, f * P:(f + 1) * P], alT, start=True, stop=True)
                last.then_inc(S("gat1_done"), 1)
            pe.wait_ge(S("h1_saved"), 2)
            l1(4, B[0], nodT, start=True)
            l1(5, B[1], nodT, start=True)
            g1T = blk[:, 1024:1024 + D].rearrange("p (k n) -> p k n", k=KT)
            pe.wait_ge(S("g1T_saved"), 2)
            pe.wait_ge(S("mq1_ready"), 2)
            l1(6, B[2], g1T, start=True)
            l1(7, B[3], g1T, start=True)
            for h in range(2):
                transposes(tiles(mix[:, 0, :], h), B[6 + h]).then_inc(S("mq1_tr"), 1)
            pe.wait_ge(S("mk1_saved"), 2)
            pe.wait_ge(S("mv1_saved"), 2)
            for h in range(2):
                for i in range(3):
                    g = 3 * h + i
                    last = mm(B[4 + h][:, i * P:(i + 1) * P], mix[:, 1, g * P:(g + 1) * P],
                              mix[:, 2, g * P:(g + 1) * P], start=True, stop=True)
                last.then_inc(S("kv1_done"), 1)
            spread(1, B[2])
            pe.wait_ge(S("mq1T_saved"), 2)
            for h in range(2):
                pe.wait_ge(S("kv1_saved"), h + 1)
                for i in range(3):
                    g = 3 * h + i
                    last = mm(B[6 + h][:, i * P:(i + 1) * P], xnT[:, g, :], zh[:, 0, g * P:(g + 1) * P],
                              start=True, stop=True)
                last.then_inc(S("lin1_done"), 1)
            for h in range(2):
                pe.wait_ge(S("lin1_saved"), h + 1)
                transposes(tiles(zh[:, 1, :], h), B[4 + h]).then_inc(S("lin1_tr"), 1)
            l1T = blk[:, 2048:2048 + D].rearrange("p (k n) -> p k n", k=KT)
            pe.wait_ge(S("lin1T_saved"), 2)
            for h in range(2):
                bias(B[h], B_GAT2, h)
                bias(B[h], B_MIX1, h, start=False)
                l1(8 + h, B[h], l1T, stop=False)
            alpha_turn(1, B[3])
            pe.wait_ge(S("alphaT_saved"), 2)
            for h in range(2):
                mm(B[h][:, 0:HALF], alT, h2[:, h * HALF:(h + 1) * HALF], start=False,
                   stop=True).then_inc(S("x3_done"), 1)

            for h in range(2):
                pe.wait_ge(S("xl3_ready"), h + 1)
                transposes(tiles(nodes, h), B[4 + h]).then_inc(S("xl3_tr"), 1)
            pe.wait_ge(S("xl3T_saved"), 2)
            for k in range(KT):
                last = mm(B[6][:, 0:E_MOE], nodT[:, k, :], col[:, G_RW1 + k * 8:G_RW1 + k * 8 + 8],
                          start=k == 0, stop=k == KT - 1)
            last.then_inc(S("route1_done"), 1)
            pe.wait_ge(S("moe_loaded"), 16)
            for w in range(2):
                for k in range(KT):
                    o = (w * KT + k) * FH
                    last = mm(B[2 + w][:, :], nodT[:, k, :], moe[:, o:o + FH], start=k == 0, stop=k == KT - 1)
                last.then_inc(S("moe_up_done"), 1)
            pe.wait_ge(S("moe_h_ready"), 1)
            hm = agg[:, :, :].rearrange("p k n -> p (k n)")
            transposes([hm[:, i * P:(i + 1) * P] for i in range(4)], B[7]).then_inc(S("moe_h_tr"), 1)
            pe.wait_ge(S("moe_hT_saved"), 1)
            for h in range(2):
                for k in range(4):
                    o = 2 * KT * FH + k * D + h * HALF
                    last = mm(B[h][:, 0:HALF], ept[:, k * P:(k + 1) * P], moe[:, o:o + HALF],
                              start=k == 0, stop=k == 3)
                last.then_inc(S("moe_done"), 1)

        @block.scalar
        def _(act):
            A = nc.scalar.activation
            chain = [0]

            def link(ins):
                chain[0] += 1
                ins.then_inc(S("act_chain"), 1)
                act.wait_ge(S("act_chain"), chain[0])

            def root(k):
                act.wait_ge(S("var_ready"), k)
                A(std[:, :], mv[:, 1:2], ACT.Sqrt, bias=half_c).then_inc(S("std_ready"), 1)

            def save(out_ap, in_ap, name):
                A(out_ap, in_ap, ACT.Copy).then_inc(S(name), 1)

            def h3(bank):
                return bank[:, 0:HALF]

            def flat(t, h):
                return t[:, 3 * h:3 * h + 3, :].rearrange("p k n -> p (k n)")

            act.wait_ge(S("con_loaded"), 16)
            root(1)
            act.wait_ge(S("xn_tr"), 1)
            save(flat(xnT, 0), h3(B[6]), "xnT_saved")
            act.wait_ge(S("eat_done"), 1)
            save(eat.rearrange("p k n -> p (k n)"), B[4][:, 0:2 * P], "b4_free")
            act.wait_ge(S("ept_done"), 1)
            save(flat(eptT, 0), h3(B[0]), "ept_saved")
            act.wait_ge(S("cols_loaded"), 16)

            with act.Fori(0, L_GNN) as l:
                act.wait_ge(S("nodes_tr"), 2 * l + 1)
                save(flat(nodT, 0), h3(B[6]), "nodT_saved")
                root(l + 2)
                act.wait_ge(S("z_tr"), 2 * l + 1)
                for f in range(3):
                    last = A(hT[:, f, :], B[6][:, f * P:(f + 1) * P], ACT.Relu,
                             scale=col[:, bass.ds(l * KT + (G_G + f), 1)],
                             bias=col[:, bass.ds(l * KT + (G_B + f), 1)])
                last.then_inc(S("hT0_saved"), 1)
                act.wait_ge(S("units_done"), l * 8 + (C_LOOP + 5))
                A(mix[:, bass.ds(l, 1), 0:HALF].rearrange("p a n -> p (a n)"), h3(B[4]), ACT.Copy).then_inc(S("b4_free"), 1)
                act.wait_ge(S("units_done"), l * 8 + (C_LOOP + 8))
                A(mix[:, bass.ds(l, 1), HALF:D].rearrange("p a n -> p (a n)"), h3(B[5]), ACT.Copy).then_inc(S("b5_free"), 1)

            act.wait_ge(S("nodes_tr"), 2 * L_GNN + 1)
            save(flat(nodT, 0), h3(B[6]), "nodT_saved")
            ex = early[:, 1, 0:2 * D]
            act.wait_ge(S("elu_min_ready"), 1)
            A(ex, ex, ACT.Exp).then_inc(S("elu_exp_ready"), 1)
            act.wait_ge(S("units_done"), C_QKV + 2)
            save(zh[:, 0, HALF:D], h3(B[1]), "q1_saved")
            act.wait_ge(S("q0_tr"), 1)
            save(blk[0:DH0, 0:512], B[6][0:DH0, :], "q0T_saved")
            act.wait_ge(S("units_done"), C_QKV + 4)
            save(zh[:, 1, HALF:D], h3(B[3]), "k1_saved")
            act.wait_ge(S("k0_tr"), 1)
            save(blk[0:DH0, 1024:1536], B[0][0:DH0, :], "k0T_saved")
            act.wait_ge(S("k1_tr"), 1)
            save(blk[0:DH0, 1536:2048], B[1][0:DH0, :], "k1T_saved")
            act.wait_ge(S("units_done"), C_QKV + 6)
            save(agg[:, 3:6, :].rearrange("p k n -> p (k n)"), h3(B[5]), "v_saved")
            for h in range(2):
                act.wait_ge(S("mq_tr"), h + 1)
                save(flat(nodT, h), h3(B[6 + h]), "mqT_saved")
                act.wait_ge(S("shifted"), h + 1)
                pr = blk[:, 2048 + 512 * h:2560 + 512 * h]
                A(pr, pr, ACT.Exp, scale=DH0 ** -0.5).then_inc(S("probs_ready"), 1)
            act.wait_ge(S("probs_tr"), 1)
            save(blk[:, 0:512], B[2][:, :], "probT_saved")
            act.wait_ge(S("probs_tr"), 2)
            save(blk[:, 512:1024], B[3][:, :], "probT_saved")
            act.wait_ge(S("lin_tr"), 1)
            save(flat(hT, 0), h3(B[0]), "linT_saved")
            act.wait_ge(S("attn_tr"), 1)
            save(mix[:, 1, 0:HALF], h3(B[0]), "attnT_saved")

            root(5)
            act.wait_ge(S("xl_tr"), 1)
            save(flat(nodT, 0), h3(B[6]), "xlT_saved")
            act.wait_ge(S("logit_done"), 1)
            save(rt[:, 0:4], B[0][:, 0:E_FFN], "logit_saved")
            act.wait_ge(S("margin_ready"), 1)
            A(rt[:, 5:6], rt[:, 4:5], ACT.Tanh, scale=0.5).then_inc(S("margin_tanh"), 1)
            buf = blk[:, :].rearrange("p (b a n) -> p b a n", b=2, a=4)
            heT = [zh[:, :, :], mix[:, 1:3, :]]

            def quarter(i):
                s = QUARTERS[i][0]
                act.wait_ge(S("up_done"), i + 1)
                if i >= 2:
                    act.wait_ge(S("act_ready"), i - 1)
                b = buf[:, i % 2]
                A(b[:, 1, :], h3(B[i % 4]), ACT.Gelu)
                A(b[:, 0, :], h3(B[i % 4]), ACT.Tanh, scale=0.5).then_inc(S("th_ready"), 1)
                act.wait_ge(S("th_ready"), i + 1)
                A(b[:, 2, :], b[:, 0, :], ACT.Copy, scale=-1.0, bias=1.0).then_inc(S("s_ready"), 1)
                act.wait_ge(S("s_ready"), i + 1)
                A(b[:, 3, :], b[:, 2, :], ACT.Identity, scale=oh[:, s, 2:3], bias=oh[:, s, 1:2]).then_inc(S("soft_ready"), 1)

            def turned(i):
                s, q = QUARTERS[i]
                act.wait_ge(S("act_tr"), i + 1)
                A(heT[s][:, q // 2, q % 2 * HALF:(q % 2 + 1) * HALF], h3(B[4 + i % 2]), ACT.Copy).then_inc(S("heT_saved"), 1)

            quarter(0)
            quarter(1)
            for i in range(2, 8):
                quarter(i)
                turned(i - 2)
            turned(6)
            turned(7)

            root(6)
            root(7)
            act.wait_ge(S("xn2_tr"), 1)
            save(flat(nodT, 0), h3(B[4]), "xn2T_saved")
            act.wait_ge(S("gat_h1_done"), 1)
            save(flat(agg, 0), h3(B[0]), "h1_saved")
            act.wait_ge(S("gat_h1_done"), 2)
            save(flat(agg, 1), h3(B[1]), "h1_saved")
            act.wait_ge(S("gat_logit"), 1)
            A(blk[:, P:2 * P], blk[:, P:2 * P], ACT.Exp).then_inc(S("gat_exp"), 1)
            for h in range(2):
                act.wait_ge(S("units_done"), R_L1 + 1 + h)
                A(mix[:, 0, h * HALF:(h + 1) * HALF], h3(B[2 + h]), ACT.Gelu).then_inc(S("mq1_ready"), 1)
            for h in range(2):
                act.wait_ge(S("gat1_done"), h + 1)
                for i in range(3):
                    f = 3 * h + i
                    last = A(blk[:, 1024 + f * P:1024 + (f + 1) * P], B[6 + h][:, i * P:(i + 1) * P], ACT.Relu,
                             bias=col[:, G_GB1 + f:G_GB1 + f + 1])
                last.then_inc(S("g1T_saved"), 1)
            for h in range(2):
                act.wait_ge(S("units_done"), R_L1 + 5 + h)
                save(mix[:, 2, h * HALF:(h + 1) * HALF], h3(B[h]), "mv1_saved")
            act.wait_ge(S("mq1_tr"), 1)
            save(flat(xnT, 0), h3(B[6]), "mq1T_saved")
            act.wait_ge(S("zh_clear"), 1)
            for h in range(2):
                act.wait_ge(S("kv1_done"), h + 1)
                for o in range(2):
                    rows = slice(64 * o, 64 * o + 64)
                    dstk = zh[rows, 0, h * HALF:(h + 1) * HALF].rearrange("p (g c) -> p g c", g=3)[:, :, 64 * o:64 * o + 64]
                    srck = B[4 + h][rows, 0:HALF].rearrange("p (g c) -> p g c", g=3)[:, :, 64 * o:64 * o + 64]
                    last = A(dstk, srck, ACT.Gelu, scale=DM ** -0.5)
                last.then_inc(S("kv1_saved"), 1)
            act.wait_ge(S("gat_logit"), 2)
            A(blk[:, P:2 * P], blk[:, P:2 * P], ACT.Exp).then_inc(S("gat_exp"), 1)
            act.wait_ge(S("lin1_done"), 1)
            save(zh[:, 1, 0:HALF], h3(B[6]), "lin1_saved")
            act.wait_ge(S("lin1_done"), 2)
            save(zh[:, 1, HALF:D], h3(B[7]), "lin1_saved")
            act.wait_ge(S("lin1_tr"), 1)
            save(blk[:, 2048:2048 + HALF], h3(B[4]), "lin1T_saved")
            act.wait_ge(S("lin1_tr"), 2)
            save(blk[:, 2048 + HALF:2048 + D], h3(B[5]), "lin1T_saved")
            root(8)
            act.wait_ge(S("xl3_tr"), 1)
            save(flat(nodT, 0), h3(B[4]), "xl3T_saved")
            act.wait_ge(S("moe_shift"), 1)
            A(rt[:, 40:48], rt[:, 32:40], ACT.Exp, accum_out=rt[:, 48:49]).then_inc(S("moe_exp"), 1)
            act.wait_ge(S("moe_up_done"), 1)
            A(z[:, 0:FH], B[2][:, :], ACT.Silu).then_inc(S("silu_ready"), 1)
            act.wait_ge(S("moe_h_tr"), 1)
            save(ept[:, 0:512], B[7][:, :], "moe_hT_saved")

        @block.vector
        def _(dve):
            V = nc.vector
            base, chain, in_loop = [0], [0], [False]

            def link(ins):
                chain[0] += 1
                ins.then_inc(S("dve_chain"), 1)
                dve.wait_ge(S("dve_chain"), base[0] + chain[0])

            def h3(bank):
                return bank[:, 0:HALF]

            def halves(t):
                return t[:, 0:HALF], t[:, HALF:D]

            def flat(t, h):
                return t[:, 3 * h:3 * h + 3, :].rearrange("p k n -> p (k n)")

            def stats(h, ap):
                link(V.bn_stats(st[:, h, :], ap))

            def spread_of(k):
                if in_loop[0]:
                    V.tensor_copy(rt[:, 64:65], st[:, 0, 0:1])
                V.bn_aggr(mv[:, :], st[:, :, :].rearrange("p a b -> p (a b)")).then_inc(S("var_ready"), 1)
                dve.wait_ge(S("std_ready"), k)
                link(V.reciprocal(rstd[:, :], std[:, :]))

            def norm(o, i):
                return V.tensor_scalar(o, i, mv[:, 0:1], rstd[:, 0:1], ALU.subtract, ALU.mult)

            dve.wait_ge(S("x_loaded"), 16)
            for h in range(2):
                stats(h, halves(X)[h])
            spread_of(1)
            norm(xn, X[:, :]).then_inc(S("xn_ready"), 1)
            dve.wait_ge(S("bias_loaded"), 16)

            def split_rows(c, name):
                link(V.tensor_copy(btab[:, c], bsrc[:, c]))
                for i, rows in enumerate((slice(32, 64), slice(64, 96), slice(64, 96))):
                    link(V.tensor_tensor(bsrc[rows, c], bsrc[rows, c], btab[rows, c], ALU.subtract))
                    V.tensor_copy(btab[rows, c], bsrc[rows, c]).then_inc(S(name), 1)
                    dve.wait_ge(S(name), i + 1)

            split_rows(slice(0, D), "btab_ready")
            dve.wait_ge(S("xn_tr"), 2)
            V.tensor_copy(flat(xnT, 1), h3(B[7])).then_inc(S("xnT_saved"), 1)
            dve.wait_ge(S("index_loaded"), 32)
            dve.wait_ge(S("con_loaded"), 16)
            link(V.tensor_copy(sd_f[:, :, :], sd_i[:, :, :]))
            for a in range(2):
                link(V.tensor_tensor(ohb[:, a, :, :],
                                     iota.rearrange("p (a n) -> p a n", a=1).broadcast_to([P, ET, P]),
                                     sd_f[:, a, :].rearrange("p (t a) -> p t a", a=1).broadcast_to([P, ET, P]),
                                     ALU.is_equal))
            V.tensor_copy(ohd32, ohb[:, 1, :, :])
            V.tensor_tensor(ohb[:, 2, :, :], ohb[:, 0, :, :], ohb[:, 1, :, :], ALU.add).then_inc(S("onehot_ready"), 1)
            for h in range(2):
                dve.wait_ge(S("wn_done"), h + 1)
                V.tensor_copy(halves(nodes)[h], h3(B[2 + h])).then_inc(S("nodes_ready"), 1)
            dve.wait_ge(S("adj_done"), 1)
            link(V.tensor_tensor(cnt[:, :], B[5][:, P:2 * P], ident, ALU.add))
            V.tensor_copy(apT[:, :], B[5][:, 0:P]).then_inc(S("b5_free"), 1)
            V.tensor_scalar(cneg[:, :], cnt[:, :], 0.0, -1e30, ALU.is_equal, ALU.mult)
            dve.wait_ge(S("deg_done"), 1)
            V.tensor_copy(deg[:, :], B[5][0:1, 2 * P:3 * P]).then_inc(S("deg_saved"), 1)
            dve.wait_ge(S("ept_done"), 2)
            V.tensor_copy(flat(eptT, 1), h3(B[1])).then_inc(S("ept_saved"), 1)
            dve.wait_ge(S("ept_saved"), 2)

            per_layer = 4
            c0 = chain[0]
            with dve.Fori(0, L_GNN) as l:
                chain[0] = c0
                base[0], in_loop[0] = l * per_layer, True
                dve.wait_ge(S("nodes_tr"), 2 * l + 2)
                V.tensor_copy(flat(nodT, 1), h3(B[7])).then_inc(S("nodT_saved"), 1)
                for h in range(2):
                    dve.wait_ge(S("agg_done"), 2 * l + (h + 1))
                    V.tensor_tensor(flat(agg, h), h3(B[4 + h]), flat(eptT, h), ALU.add).then_inc(S("agg_saved"), 1)
                for h in range(2):
                    dve.wait_ge(S("units_done"), l * 8 + (C_LOOP + 3 + h))
                    stats(h, h3(B[h]))
                spread_of(l + 2)
                for h in range(2):
                    norm(halves(z)[h], h3(B[h])).then_inc(S("z_ready"), 1)
                dve.wait_ge(S("z_tr"), 2 * l + 2)
                for i in range(3):
                    last = V.tensor_scalar(hT[:, 3 + i, :], B[7][:, i * P:(i + 1) * P],
                                           col[:, bass.ds(l * KT + (G_G + 3 + i), 1)],
                                           col[:, bass.ds(l * KT + (G_B + 3 + i), 1)], ALU.mult, ALU.add)
                link(last)
                V.tensor_scalar(flat(hT, 1), flat(hT, 1), 0.0, None, ALU.max).then_inc(S("hT1_saved"), 1)
                for h in range(2):
                    dve.wait_ge(S("units_done"), l * 8 + (C_LOOP + 6 + h))
                    n = halves(nodes)[h]
                    V.tensor_tensor(n, h3(B[2 + h]), n, ALU.add).then_inc(S("nodes_ready"), 1)
            assert chain[0] == c0 + per_layer
            base[0], chain[0], in_loop[0] = 0, c0 + per_layer * L_GNN, False

            dve.wait_ge(S("nodes_tr"), 2 * L_GNN + 2)
            V.tensor_copy(flat(nodT, 1), h3(B[7])).then_inc(S("nodT_saved"), 1)
            dve.wait_ge(S("bias2_loaded"), 16)
            split_rows(slice(D, 3 * D), "btab2_ready")
            dve.wait_ge(S("b4_free"), L_GNN + 1)
            dve.wait_ge(S("b5_free"), L_GNN + 1)
            ex = early[:, 1, 0:2 * D]
            mqk = mix[:, 0:2, :].rearrange("p a n -> p (a n)")
            V.tensor_scalar(ex, mqk, 0.0, None, ALU.min).then_inc(S("elu_min_ready"), 1)
            link(V.tensor_tensor(X[:, :], X[:, :], nodes[:, :], ALU.add))
            dve.wait_ge(S("elu_exp_ready"), 1)
            V.scalar_tensor_tensor(mqk, mqk, 0.0, ex, ALU.max, ALU.add).then_inc(S("elu_ready"), 1)
            dve.wait_ge(S("units_done"), C_QKV + 1)
            V.tensor_copy(zh[:, 0, 0:HALF], h3(B[0])).then_inc(S("q0_saved"), 1)
            dve.wait_ge(S("units_done"), C_QKV + 3)
            V.tensor_copy(zh[:, 1, 0:HALF], h3(B[2])).then_inc(S("k0_saved"), 1)
            dve.wait_ge(S("q1_tr"), 1)
            V.tensor_copy(blk[0:DH0, 512:1024], B[7][0:DH0, :]).then_inc(S("q1T_saved"), 1)
            dve.wait_ge(S("units_done"), C_QKV + 5)
            V.tensor_copy(flat(agg, 0), h3(B[4])).then_inc(S("v_saved"), 1)
            mxs, sums, rec = sm[:, 0, 0:H0], sm[:, 1, 0:H0], sm[:, 2, 0:H0]

            def g3(ap, n):
                return ap.rearrange("p (g n) -> p g n", n=n)

            def rep(ap, n):
                g = ap.shape[1]
                return ap.rearrange("p (g a) -> p g a", a=1).broadcast_to([P, g, n])

            for h in range(2):
                dve.wait_ge(S("scores_done"), h + 1)
                m4 = mxs[:, 4 * h:4 * h + 4]
                link(V.tensor_reduce(m4, g3(B[2 + h][:, :], P), AX, ALU.max))
                V.tensor_tensor(g3(blk[:, 2048 + 512 * h:2560 + 512 * h], P), g3(B[2 + h][:, :], P), rep(m4, P),
                                ALU.subtract).then_inc(S("shifted"), 1)
            dve.wait_ge(S("kv_clear"), 1)
            for h in range(2):
                dve.wait_ge(S("kv_done"), h + 1)
                for o in range(2):
                    rows = slice(64 * o, 64 * o + 64)
                    last = V.tensor_copy(g3(xnt[rows, h * 390:(h + 1) * 390], 130)[:, :, 65 * o:65 * o + 65],
                                         g3(B[h][rows, 0:390], 130)[:, :, 65 * o:65 * o + 65])
                last.then_inc(S("kv_saved"), 1)
            for h in range(2):
                dve.wait_ge(S("probs_ready"), h + 1)
                link(V.tensor_reduce(sums[:, 4 * h:4 * h + 4], g3(blk[:, 2048 + 512 * h:2560 + 512 * h], P), AX, ALU.add))
            link(V.reciprocal(rec, sums))
            for h in range(2):
                dve.wait_ge(S("lin_done"), h + 1)
                lin = g3(B[6 + h][:, 0:390], 65)
                zr = sm[:, h, 8:14]
                link(V.reciprocal(zr.rearrange("p (g a) -> p g a", a=1), lin[:, :, 64:65]))
                V.tensor_tensor(g3(zh[:, 0, h * HALF:(h + 1) * HALF], 64), lin[:, :, 0:64], rep(zr, 64),
                                ALU.mult).then_inc(S("lin_ready"), 1)
            dve.wait_ge(S("lin_tr"), 2)
            V.tensor_copy(flat(hT, 1), h3(B[1])).then_inc(S("linT_saved"), 1)
            for h in range(2):
                dve.wait_ge(S("attn_done"), h + 1)
                V.tensor_tensor(g3(mix[:, 0, h * HALF:(h + 1) * HALF], DH0), g3(h3(B[6 + h]), DH0),
                                rep(rec[:, 4 * h:4 * h + 4], DH0), ALU.mult).then_inc(S("attn_ready"), 1)
            dve.wait_ge(S("attn_tr"), 2)
            V.tensor_copy(mix[:, 1, HALF:D], h3(B[1])).then_inc(S("attnT_saved"), 1)
            for h in range(2):
                dve.wait_ge(S("units_done"), C_WO + 1 + h)
                xh = halves(X)[h]
                link(V.tensor_tensor(xh, h3(B[4 + h]), xh, ALU.add))
                stats(h, xh)
            spread_of(5)
            for h in range(2):
                norm(halves(nodes)[h], halves(X)[h]).then_inc(S("xl_ready"), 1)
            dve.wait_ge(S("xl_tr"), 2)
            V.tensor_copy(flat(nodT, 1), h3(B[7])).then_inc(S("xlT_saved"), 1)

            dve.wait_ge(S("mean_done"), 1)
            lg, eq, wgt, l2, keep = rt[:, 8:12], rt[:, 12:16], rt[:, 16:20], rt[:, 20:24], rt[:, 24:28]
            top, wm = rt[:, 28:30], rt[:, 30:32]
            w4, d4 = con[:, K_W4:K_W4 + 4], con[:, K_D4:K_D4 + 4]
            link(V.tensor_tensor(lg, B[1][:, 0:4], col[:, G_RB0:G_RB0 + 4], ALU.add))
            for s, v in enumerate((lg, l2)):
                link(V.tensor_reduce(top[:, s:s + 1], v, AX, ALU.max))
                link(V.scalar_tensor_tensor(wgt, v, top[:, s:s + 1], w4, ALU.is_equal, ALU.mult))
                link(V.tensor_reduce(wm[:, s:s + 1], wgt, AX, ALU.max))
                link(V.tensor_scalar(oh[:, s, :], wgt, wm[:, s:s + 1], None, ALU.is_equal))
                if s == 0:
                    link(V.tensor_scalar(keep, oh[:, 0, :], -1.0, 1.0, ALU.mult, ALU.add))
                    link(V.tensor_tensor(keep, lg, keep, ALU.mult))
                    link(V.scalar_tensor_tensor(l2, oh[:, 0, :], -3e38, keep, ALU.mult, ALU.add))
            V.tensor_scalar(eidx[:, :], wm, -1.0, float(E_FFN), ALU.mult, ALU.add).then_inc(S("routed"), 1)
            V.tensor_tensor(rt[:, 4:5], top[:, 0:1], top[:, 1:2], ALU.subtract).then_inc(S("margin_ready"), 1)
            dve.wait_ge(S("margin_tanh"), 1)
            V.tensor_scalar(gate[:, 0:1], rt[:, 5:6], 0.5, 0.5, ALU.mult, ALU.add)
            link(V.tensor_scalar(gate[:, 1:2], rt[:, 5:6], -0.5, 0.5, ALU.mult, ALU.add))
            own = rt[:, 66:68]
            tmp = rt[:, 68:76].rearrange("p (s e) -> p s e", s=2)
            link(V.tensor_tensor(tmp, oh[:, :, :], d4.rearrange("p (a e) -> p a e", a=1).broadcast_to([P, 2, 4]), ALU.mult))
            link(V.tensor_reduce(own, tmp, AX, ALU.add))
            V.tensor_copy(selx[:, :].rearrange("p (s n) -> p s n", s=2),
                          own[0:96, :].rearrange("p (s a) -> p s a", a=1).broadcast_to([96, 2, P])).then_inc(S("selx_ready"), 1)
            link(V.tensor_tensor(rt[:, 76:78], own, gate[:, :], ALU.mult))
            link(V.tensor_reduce(rt[:, 78:79], rt[:, 76:78], AX, ALU.add))
            V.tensor_copy(g4[:, :], rt[0:E_FFN, 78:79].broadcast_to([E_FFN, P])).then_inc(S("gates_ready"), 1)
            silu, mish = oh[:, :, 1], oh[:, :, 2]
            link(V.tensor_tensor(rt[:, 80:82], silu, mish, ALU.add))
            link(V.tensor_scalar(par[:, 0, :], mish, 2.0, 1.0, ALU.mult, ALU.add))
            link(V.tensor_tensor(par[:, 0, :], par[:, 0, :], rt[:, 80:82], ALU.add))
            link(V.scalar_tensor_tensor(par[:, 1, :], rt[:, 80:82], -1.0, gate[:, :], ALU.mult, ALU.mult))
            V.tensor_tensor(par[:, 2, :], par[:, 1, :], gate[:, :], ALU.add).then_inc(S("params_ready"), 1)
            dve.wait_ge(S("params_ready"), 1)

            buf = blk[:, :].rearrange("p (b a n) -> p b a n", b=2, a=4)
            vv = agg[:, :, :].rearrange("p k n -> p (k n)")[:, 0:HALF]
            den = agg[:, :, :].rearrange("p k n -> p (k n)")[:, HALF:D]
            rcp = ept[:, 0:HALF]
            act_s = mix[:, 0, :].rearrange("p (b n) -> p b n", b=2)
            for i, (s, q) in enumerate(QUARTERS):
                b = buf[:, i % 2]
                dve.wait_ge(S("soft_ready"), i + 1)
                link(V.tensor_tensor(vv, b[:, 2, :], b[:, 3, :], ALU.mult))
                link(V.tensor_scalar(den, vv, oh[:, s, 2:3], par[:, 0, s:s + 1], ALU.mult, ALU.add))
                link(V.reciprocal(rcp, den))
                link(V.scalar_tensor_tensor(rcp, vv, par[:, 0, s:s + 1], rcp, ALU.subtract, ALU.mult))
                link(V.scalar_tensor_tensor(rcp, rcp, par[:, 1, s:s + 1], h3(B[i % 4]), ALU.mult, ALU.mult))
                if i >= 2:
                    dve.wait_ge(S("act_tr"), i - 1)
                V.scalar_tensor_tensor(act_s[:, i % 2, :], b[:, 1, :], par[:, 2, s:s + 1], rcp, ALU.mult,
                                       ALU.add).then_inc(S("act_ready"), 1)

            for h in range(2):
                dve.wait_ge(S("units_done"), R_L1 - 1 + h)
                n = halves(nodes)[h]
                link(V.tensor_tensor(n, h3(B[6 + h]), n, ALU.add))
                stats(h, n)
            spread_of(6)
            dve.wait_ge(S("xlb_ready"), 1)
            link(V.scalar_tensor_tensor(nodes[:, :], nodes[:, :], mv[:, 0:1], vec[:, V_LG, :], ALU.subtract, ALU.mult))
            for h in range(2):
                xh = halves(X)[h]
                link(V.scalar_tensor_tensor(xh, halves(nodes)[h], rstd[:, 0:1], xh, ALU.mult, ALU.add))
                stats(h, xh)
            spread_of(7)
            for h in range(2):
                norm(halves(nodes)[h], halves(X)[h]).then_inc(S("xn2_ready"), 1)
            dve.wait_ge(S("xn2_tr"), 2)
            V.tensor_copy(flat(nodT, 1), h3(B[5])).then_inc(S("xn2T_saved"), 1)

            def attend(g, hsb, bank, before=None):
                for i, v in enumerate((V_AS1 + 2 * g, V_AD1 + 2 * g)):
                    V.tensor_tensor_reduce(out=mvs, in0=hsb, in1=vec[:, v, :], scale=1.0, scalar=0.0,
                                           op0=ALU.mult, op1=ALU.add, accum_out=ab[:, i:i + 1]).then_inc(S("dve_chain"), 1)
                    chain[0] += 1
                    dve.wait_ge(S("dve_chain"), chain[0])
                V.tensor_scalar(blk[:, 0:P], ident, ab[:, 0:1], None, ALU.mult).then_inc(S("diag_ready"), 1)
                if before:
                    before()
                dve.wait_ge(S("spread_done"), g + 1)
                lo = blk[:, P:2 * P]
                sc = blk[:, 3 * P:4 * P]
                link(V.tensor_scalar(sc, bank[:, 0:P], ab[:, 1:2], None, ALU.add))
                link(V.scalar_tensor_tensor(sc, sc, 0.2, sc, ALU.mult, ALU.max))
                link(V.tensor_tensor(sc, sc, cneg[:, :], ALU.add))
                link(V.tensor_reduce(ab[:, 2:3], sc, AX, ALU.max))
                V.tensor_scalar(lo, sc, ab[:, 2:3], None, ALU.subtract).then_inc(S("gat_logit"), 1)
                dve.wait_ge(S("gat_exp"), g + 1)
                link(V.tensor_tensor(lo, lo, cnt[:, :], ALU.mult))
                link(V.tensor_reduce(ab[:, 3:4], lo, AX, ALU.add))
                link(V.reciprocal(ab[:, 4:5], ab[:, 3:4]))
                V.tensor_scalar(lo, lo, ab[:, 4:5], None, ALU.mult).then_inc(S("alpha_ready"), 1)
                dve.wait_ge(S("alpha_tr"), g + 1)
                V.tensor_copy(blk[:, 2 * P:3 * P], B[7 - 4 * g][:, 0:P]).then_inc(S("alphaT_saved"), 1)

            mvs = blk[:, 2048:2048 + D]
            dve.wait_ge(S("h1_saved"), 2)
            attend(0, agg[:, :, :].rearrange("p k n -> p (k n)"), B[6])
            for h in range(2):
                dve.wait_ge(S("units_done"), R_L1 + 3 + h)
                V.tensor_copy(mix[:, 1, h * HALF:(h + 1) * HALF], h3(B[4 + h])).then_inc(S("mk1_saved"), 1)
            for h in range(2):
                dve.wait_ge(S("units_done"), R_L1 + 7 + h)
                link(V.tensor_copy(ept[:, h * HALF:(h + 1) * HALF], h3(B[2 + h])))

            def between():
                dve.wait_ge(S("mq1_tr"), 2)
                V.tensor_copy(flat(xnT, 1), h3(B[7])).then_inc(S("mq1T_saved"), 1)

            attend(1, ept[:, 0:D], B[2], between)
            for h in range(2):
                dve.wait_ge(S("x3_done"), h + 1)
                xh = halves(X)[h]
                link(V.tensor_tensor(xh, h3(B[h]), xh, ALU.add))
                stats(h, xh)
            spread_of(8)
            for h in range(2):
                norm(halves(nodes)[h], halves(X)[h]).then_inc(S("xl3_ready"), 1)
            dve.wait_ge(S("xl3_tr"), 2)
            V.tensor_copy(flat(nodT, 1), h3(B[5])).then_inc(S("xl3T_saved"), 1)
            dve.wait_ge(S("route1_done"), 1)
            l8, w8, m8 = rt[:, 8:16], rt[:, 16:24], rt[:, 24:32]
            link(V.tensor_tensor(l8, B[6][:, 0:E_MOE], col[:, G_RB1:G_RB1 + E_MOE], ALU.add))
            link(V.tensor_reduce(rt[:, 50:51], l8, AX, ALU.max))
            V.tensor_scalar(rt[:, 32:40], l8, rt[:, 50:51], None, ALU.subtract).then_inc(S("moe_shift"), 1)
            link(V.scalar_tensor_tensor(w8, l8, rt[:, 50:51], con[:, K_W8:K_W8 + 8], ALU.is_equal, ALU.mult))
            link(V.tensor_reduce(rt[:, 51:52], w8, AX, ALU.max))
            link(V.tensor_scalar(m8, w8, rt[:, 51:52], None, ALU.is_equal))
            dve.wait_ge(S("moe_exp"), 1)
            link(V.reciprocal(rt[:, 52:53], rt[:, 48:49]))
            hm = agg[:, :, :].rearrange("p k n -> p (k n)")[:, 0:FH]
            dve.wait_ge(S("silu_ready"), 1)
            link(V.tensor_tensor(g3(z[:, 0:FH], HID), g3(z[:, 0:FH], HID), rep(m8, HID), ALU.mult))
            dve.wait_ge(S("moe_up_done"), 2)
            V.tensor_tensor(hm, B[3][:, :], z[:, 0:FH], ALU.mult).then_inc(S("moe_h_ready"), 1)
            o16 = blk[:, 0:HALF].bitcast(bf16)
            for h in range(2):
                dve.wait_ge(S("moe_done"), h + 1)
                link(V.tensor_copy(o16[:, h * HALF:(h + 1) * HALF], h3(B[h])))
                V.scalar_tensor_tensor(halves(nodes)[h], o16[:, h * HALF:(h + 1) * HALF], rt[:, 52:53],
                                       halves(X)[h], ALU.mult, ALU.add).then_inc(S("out_ready"), 1)

        @block.gpsimd
        def _(pool):
            pool.wait_ge(S("b4_free"), L_GNN + 1)
            pool.wait_ge(S("b5_free"), L_GNN + 1)
            va = ept[:, :].rearrange("p (g n) -> p g n", n=65)
            nc.gpsimd.memset(va[:, :, 64:65], 1.0)
            nc.gpsimd.tensor_copy(va[:, :, 0:64], mix[:, 2, :].rearrange("p (g n) -> p g n", n=64)).then_inc(S("vaug_ready"), 1)
            nc.gpsimd.memset(xnt[:, :], 0.0).then_inc(S("kv_clear"), 1)
            pool.wait_ge(S("xl_ready"), 2)
            pool.wait_ge(S("vec_loaded"), 16)
            nc.gpsimd.tensor_tensor(X[:, :], X[:, :], vec[:, V_LB, :], ALU.add).then_inc(S("xlb_ready"), 1)
            pool.wait_ge(S("xn2_ready"), 2)
            nc.gpsimd.memset(zh[:, 0, :], 0.0).then_inc(S("zh_clear"), 1)


def kernel(**inputs):
    import numpy as _np
    import concourse.bacc as _bacc
    from concourse import mybir as _mybir
    from concourse.bass_utils import run_bass_kernel_spmd as _run
    import ml_dtypes as _ml

    g = {k: _np.asarray(v) for k, v in inputs.items()}

    def chunk(w):
        k, n = w.shape
        return w.reshape(KT, P, n // HALF, HALF).transpose(2, 1, 0, 3).reshape(n // HALF, P, CH)

    def colk(v):
        return v.reshape(-1, KT, P).transpose(2, 0, 1).reshape(P, -1)

    parts = [chunk(g["L0_gnn_Wn"].T)]
    wm = g["L0_mix_w_qkv"].T
    for l in range(L_GNN):
        w1, w2 = g["L0_gnn_W1"][l].T, g["L0_gnn_W2"][l].T
        m = chunk(wm[:, l * D:(l + 1) * D])
        parts += [chunk(w1[:D]), chunk(w1[D:]), m[:1], chunk(w2), m[1:]]
    parts += [chunk(g["L0_gnn_Wqkv"].T), chunk(g["L0_mix_w_proj"].T), chunk(g["L0_gnn_Wo"].T)]
    for e in range(E_FFN):
        parts += [chunk(g["L0_ffn_w1"][e]), chunk(g["L0_ffn_w2"][e][:D]), chunk(g["L0_ffn_w2"][e][D:])]
    parts += [chunk(g["L1_gnn_W1"]), chunk(g["L1_mix_w_qkv"]), chunk(g["L1_gnn_W2"]), chunk(g["L1_mix_w_proj"])]
    chunks = _np.concatenate(parts)

    def rows(w):
        return w.reshape(-1, P, w.shape[1]).transpose(1, 0, 2).reshape(P, -1)

    up = [rows(g[n].transpose(1, 0, 2).reshape(D, FH)) for n in ("L1_ffn_w1", "L1_ffn_w2")]
    moe_w = _np.concatenate(up + [rows(g["L1_ffn_w3"].reshape(FH, D))], axis=1)

    table = _np.zeros((32, 3 * D), _np.float32)
    table[:N_BIAS, :D] = _np.concatenate([
        g["L0_gnn_bn"][None], g["L0_gnn_b1"], g["L0_gnn_b2"], g["L0_gnn_bqkv"].reshape(3, D), g["L0_gnn_bo"][None],
        g["L0_mix_b_proj"][None], g["L1_gnn_b2"][None], g["L1_mix_b_proj"][None]])
    table[:E_FFN, D:] = g["L0_ffn_b1"]
    bias_rows = _np.concatenate([table] * 3)

    cols = _np.concatenate([
        colk(g["L0_gnn_ln_g"]), colk(g["L0_gnn_ln_b"]), colk(g["L1_gnn_b1"]), rows(g["L0_ffn_router_w"].T),
        _np.broadcast_to(g["L0_ffn_router_b"], (P, E_FFN)), rows(g["L1_ffn_router_w"]),
        _np.broadcast_to(g["L1_ffn_router_b"], (P, E_MOE))], axis=1)
    vecs = _np.concatenate([g[n] for n in ("L1_gnn_att_src1", "L1_gnn_att_dst1", "L1_gnn_att_src2", "L1_gnn_att_dst2",
                                           "L0_ffn_ln_g", "L0_ffn_ln_b")])

    cst = _np.zeros((P, N_CST), _np.float32)
    cst[:, K_ID:K_ID + P] = _np.eye(P)
    cst[:, K_IOTA:K_IOTA + P] = _np.arange(P)
    cst[:, K_ONE:K_ONE + P] = 1
    cst[:, K_AVG:K_AVG + P] = 1 / P
    cst[:, K_EPS] = EPS
    cst[:, K_HALF] = 0.5
    cst[:, K_W4:K_W4 + 4] = E_FFN - _np.arange(E_FFN)
    cst[:, K_D4:K_D4 + 4] = _np.arange(P)[:, None] % 32 == _np.arange(E_FFN)
    cst[:, K_W8:K_W8 + 8] = E_MOE - _np.arange(E_MOE)
    sel = _np.zeros((96, N_BIAS, P), _ml.bfloat16)
    for b in range(N_BIAS):
        sel[b::32, b] = 1
    sel = sel.reshape(96, -1)

    f = [("x", g["x"]), ("src", g["src"]), ("dst", g["dst"]), ("edge", g["edge_attr_256"]),
         ("w_edge", rows(g["L0_gnn_We"].T)), ("be", g["L0_gnn_be"][None]), ("chunks", chunks), ("moe_w", moe_w),
         ("bias_rows", bias_rows), ("gate_b2", g["L0_ffn_b2"]), ("cols", cols), ("vecs", vecs), ("cst", cst),
         ("sel", sel)]
    nc = _bacc.Bacc("TRN2", target_bir_lowering=False, num_devices=1)
    arrays, args = {}, []
    for name, a in f:
        a = _np.ascontiguousarray(a)
        arrays[f"in_{name}"] = a
        args.append(nc.dram_tensor(f"in_{name}", a.shape, _mybir.dt.from_np(a.dtype), kind="ExternalInput").ap())
    args.append(nc.dram_tensor("out_x", (P, D), _mybir.dt.float32, kind="ExternalOutput").ap())
    gps_kernel(nc, *args)
    r = _run(nc, [arrays], core_ids=[0])
    return r.results[0]["out_x"]
```

```python
import numpy as np
import concourse.bass as bass
from concourse import mybir
from contextlib import ExitStack

P = 128
D = 768
HALF = D // 2
KT = D // P
E_EDGES = 2048
ET = E_EDGES // P
DE = 256
L_GNN = 3
CH = KT * HALF
SLOTS = 8
H0, DH0 = 8, D // 8
HM, DM = 12, D // 12
TOP_K = 2
E_FFN, E_MOE, HID = 4, 8, 64
FH = E_MOE * HID
EPS = 1e-5

C_WN = 0
C_LOOP = 2
C_QKV = C_LOOP + 8 * L_GNN
C_MIXP = C_QKV + 6
C_WO = C_MIXP + 2
C_FFN = C_WO + 2
C_GAT1 = C_FFN + 8 * E_FFN
C_L1 = C_GAT1 + 2
N_CHUNKS = C_L1 + 10
R_FFN = C_FFN
FFN_ORDER = [(0, 1), (0, 2), (0, 3), (1, 1), (1, 2), (0, 4), (0, 5), (1, 3), (0, 6), (0, 7), (1, 4), (1, 5),
             (1, 6), (1, 7)]
R_EXP = R_FFN + E_FFN
R_L1 = R_EXP + len(FFN_ORDER)
QUARTERS = [(0, 0), (1, 0), (0, 1), (0, 2), (0, 3), (1, 1), (1, 2), (1, 3)]
B_BN, B_B1, B_B2, B_QKV, B_BO, B_GAT2 = 0, 1, 4, 7, 10, 12
PAIRS = (B_BO, B_GAT2)
N_BIAS = 14
K_ID, K_IOTA, K_ONE, K_AVG, K_EPS, K_W4, K_D4, K_W8, K_HALF = 0, 128, 256, 384, 512, 513, 517, 521, 529
N_CST = 530
G_G, G_B, G_GB1, G_RW0, G_RB0, G_RW1, G_RB1 = 0, 18, 36, 42, 66, 70, 118
N_COLS = 126
V_AS1, V_AD1, V_AS2, V_AD2, V_LG, V_LB = range(6)


def gps_kernel(nc, x, src, dst, edge, w_edge, be_row, chunks, moe_w, bias_rows, gate_b2, cols, vecs,
               cst, sel, out):
    f32, bf16, i32 = mybir.dt.float32, mybir.dt.bfloat16, mybir.dt.int32
    ALU, ACT, AX = mybir.AluOpType, mybir.ActivationFunctionType, mybir.AxisListType.X
    ctx = ExitStack()
    with ctx:
        sems = {}

        def S(name):
            if name not in sems:
                sems[name] = ctx.enter_context(nc.semaphore(name))
            return sems[name]

        def sb(name, shape, dt=f32):
            return ctx.enter_context(nc.sbuf_tensor(name, shape, dt))

        ring = sb("ring", [P, SLOTS, CH])
        early = sb("early", [P, 2, CH])
        moe = sb("moe", [P, 4 * CH])
        vec = sb("vec", [P, 6, D])
        X = sb("X", [P, D])
        nodes = sb("nodes", [P, D])
        nodT = sb("nodT", [P, KT, P])
        agg = sb("agg", [P, KT, P])
        ept = sb("ept", [P, 780])
        xnt = sb("xnt", [P, 780])
        zh = sb("zh", [P, 2, D])
        mix = sb("mix", [P, 3, D])
        blk = sb("blk", [P, 3072])
        con = sb("con", [P, N_CST])
        col = sb("col", [P, N_COLS])
        selb = sb("selb", [96, N_BIAS * P], bf16)
        btab = sb("btab", [96, 3 * D], bf16)
        b2f = sb("b2f", [E_FFN, D])
        apT = sb("apT", [P, P])
        cnt = sb("cnt", [P, P])
        cneg = sb("cneg", [P, P])
        deg = sb("deg", [1, P])
        sd_i = sb("sd_i", [P, 2, ET], i32)
        sd_b = sb("sd_b", [P, 2, ET], bf16)
        iota_b = sb("iota_b", [P, P], bf16)
        st = sb("st", [P, 2, 6])
        mv = sb("mv", [P, 2])
        std = sb("std", [P, 1])
        rstd = sb("rstd", [P, 1])
        sm = sb("sm", [P, 3, 16])
        rt = sb("rt", [P, 96])
        oh = sb("oh", [P, TOP_K, E_FFN])
        gate = sb("gate", [P, TOP_K])
        par = sb("par", [P, 3, TOP_K])
        eidx = sb("eidx", [1, 8], mybir.dt.uint32)
        selx = sb("selx", [96, TOP_K * P], bf16)
        g4 = sb("g4", [E_FFN, P])
        ab = sb("ab", [P, 8])
        pooled, choice0 = rt[:, 80:86], rt[0:1, 56:60]
        lg8, top8 = rt[0:1, 8:16], rt[0:1, 16:24]
        eps = con[:, K_EPS:K_EPS + 1]

        ident = con[:, K_ID:K_ID + P]
        iota = con[:, K_IOTA:K_IOTA + P]
        xnT = xnt[:, 0:D].rearrange("p (k n) -> p k n", k=KT)
        eptT = ept[:, 0:D].rearrange("p (k n) -> p k n", k=KT)
        hT = zh[:, 1, :].rearrange("p (k n) -> p k n", k=KT)
        z = zh[:, 0, :]
        xn = mix[:, 0, :]
        edg = moe[:, 0:4096].rearrange("p (t k) -> p t k", t=ET)
        ohb = moe[:, 4096:7168].bitcast(bf16).rearrange("p (a t n) -> p a t n", a=3, t=ET)
        ohd32 = moe[:, 7168:9216].rearrange("p (t n) -> p t n", t=ET)
        we = zh[:, :, :]
        eat = agg[:, 0:2, :]
        be_s = blk[0:1, 0:D]
        bsrc = early[0:96, 0, :]

        B = [ctx.enter_context(nc.psum_tensor(f"B{i}", [P, 512], f32)) for i in range(8)]

        block = ctx.enter_context(nc.Block())

        @block.sync
        def _(sp):
            for h in range(2):
                cols_h = slice(h * HALF, (h + 1) * HALF)
                sp.dma_start(X[:, cols_h], x[:, cols_h]).then_inc(S(f"x{h}_loaded"), 16)
            sp.dma_start(con[:, :], cst).then_inc(S("con_loaded"), 16)

            def load(slot, index):
                sp.dma_start(ring[:, slot, :], chunks[index]).then_inc(S(f"slot{slot}"), 16)

            load(0, 0)
            sp.dma_start(sd_i[:, 0, :], src.rearrange("(p t) -> p t", t=ET)).then_inc(S("index_loaded"), 16)
            sp.dma_start(sd_i[:, 1, :], dst.rearrange("(p t) -> p t", t=ET)).then_inc(S("index_loaded"), 16)
            sp.dma_start(bsrc[:, 0:D], bias_rows[:, 0:D]).then_inc(S("bias_loaded"), 16)
            sp.dma_start(selb[:, 0:P], sel[:, 0:P]).then_inc(S("sel0_loaded"), 16)
            load(1, 1)
            sp.dma_start(edg, edge.rearrange("(p t) k -> p t k", t=ET)).then_inc(S("edge_loaded"), 16)
            sp.dma_start(we, w_edge.rearrange("p (k f) -> p k f", k=2)).then_inc(S("we_loaded"), 16)
            sp.dma_start(be_s, be_row).then_inc(S("we_loaded"), 16)
            load(2, 2)
            sp.dma_start(selb[:, P:N_BIAS * P], sel[:, P:N_BIAS * P]).then_inc(S("sel_loaded"), 16)
            load(3, 3)
            sp.dma_start(col[:, :], cols).then_inc(S("cols_loaded"), 16)
            load(4, 4)
            sp.dma_start(bsrc[:, D:3 * D], bias_rows[:, D:3 * D]).then_inc(S("bias2_loaded"), 16)
            for c in range(5, SLOTS):
                load(c, c)
            with sp.Fori(1, C_FFN // SLOTS) as r:
                for k in range(SLOTS):
                    sp.wait_ge(S("units_done"), (r - 1) * SLOTS + (k + 1))
                    load(k, r * SLOTS + k)
            for c in range(C_FFN // SLOTS * SLOTS, C_FFN):
                sp.wait_ge(S("units_done"), c - SLOTS + 1)
                load(c % SLOTS, c)
            for e in range(E_FFN):
                sp.wait_ge(S("units_done"), R_FFN + e - SLOTS + 1)
                load((R_FFN + e) % SLOTS, C_FFN + 8 * e)
            sp.wait_ge(S("elu_ready"), 1)
            sp.dma_start(vec[:, :, :], vecs.rearrange("(a v) -> a v", a=1).broadcast_to([P, 6 * D])
                         .rearrange("p (a v) -> p a v", a=6)).then_inc(S("vec_loaded"), 16)
            sp.dma_start(b2f[:, :], gate_b2).then_inc(S("b2_loaded"), 16)
            for h in range(2):
                sp.dma_start(early[:, h, :], chunks[C_GAT1 + h]).then_inc(S(f"early{h}_loaded"), 16)
            sp.dma_start(moe[:, :], moe_w).then_inc(S("moe_loaded"), 16)
            sp.wait_ge(S("routed"), 1)
            chosen = [sp.value_load(eidx[0:1, s:s + 1], min_val=0, max_val=E_FFN - 1) for s in range(TOP_K)]
            for i, (s, j) in enumerate(FFN_ORDER):
                sp.wait_ge(S("units_done"), R_EXP + i - SLOTS + 1)
                load((R_EXP + i) % SLOTS, chosen[s] * 8 + (C_FFN + j))
            for j in range(10):
                c = R_L1 + j
                sp.wait_ge(S("units_done"), c - SLOTS + 1)
                load(c % SLOTS, C_L1 + j)
            for h in range(2):
                sp.wait_ge(S("out_ready"), h + 1)
                sp.dma_start(out[:, h * HALF:(h + 1) * HALF],
                             nodes[:, h * HALF:(h + 1) * HALF]).then_inc(S("out_stored"), 16)
            sp.wait_ge(S("out_stored"), 32)

        @block.tensor
        def _(pe):
            mm = nc.tensor.matmul

            def transposes(src_tiles, bank, rows=P):
                for i, t in enumerate(src_tiles):
                    last = nc.tensor.transpose(bank[0:rows, i * P:(i + 1) * P], t, ident)
                return last

            def tiles(row, half, n=3, w=P):
                return [row[:, (half * n + i) * w:(half * n + i + 1) * w] for i in range(n)]

            def bias(bank, row, half, start=True, stop=False):
                return mm(bank[:, 0:HALF], selb[:, row * P:(row + 1) * P], btab[:, half * HALF:(half + 1) * HALF],
                          start=start, stop=stop)

            def keep_x(bank, rows, h):
                mm(bank[:, 0:HALF], ident, rows[:, h * HALF:(h + 1) * HALF], start=True, stop=False)

            FRONT, BACK, WHOLE = range(KT // 2), range(KT // 2, KT), range(KT)

            def unit(bank, lhsT, chunk, start=False, stop=True, ks=WHOLE):
                for k in ks:
                    last = mm(bank[:, 0:HALF], lhsT[:, k, :], chunk[:, k * HALF:(k + 1) * HALF],
                              start=start and k == 0, stop=stop and k == KT - 1)
                return last

            def ring_unit(c, turn, bank, lhsT, ks=WHOLE, **kw):
                if ks.start == 0:
                    pe.wait_ge(S(f"slot{c % SLOTS}"), 16 * (turn + 1))
                last = unit(bank, lhsT, ring[:, c % SLOTS, :], ks=ks, **kw)
                if ks.stop == KT:
                    last.then_inc(S("units_done"), 1)

            pe.wait_ge(S("con_loaded"), 16)
            for h in range(2):
                pe.wait_ge(S("xn_ready"), h + 1)
                transposes(tiles(xn, h), B[6 + h]).then_inc(S("xn_tr"), 1)
            pe.wait_ge(S("xnT0_saved"), 1)
            ring_unit(0, 0, B[2], xnT, start=True, stop=False, ks=FRONT)
            pe.wait_ge(S("xnT1_saved"), 1)
            ring_unit(0, 0, B[2], xnT, stop=False, ks=BACK)
            ring_unit(1, 0, B[3], xnT, start=True, stop=False)
            pe.wait_ge(S("onehot_ready"), 1)
            for o, a, b in ((0, 2, 1), (P, 1, 0)):
                for t in range(ET):
                    last = mm(B[5][:, o:o + P], ohb[:, a, t, :], ohb[:, b, t, :], start=t == 0, stop=t == ET - 1)
            last.then_inc(S("adj_done"), 1)
            pe.wait_ge(S("sel0_loaded"), 16)
            pe.wait_ge(S("btab_ready"), 2)
            for h in range(2):
                bias(B[2 + h], B_BN, h, start=False, stop=True).then_inc(S("wn_done"), 1)
            pe.wait_ge(S("edge_loaded"), 16)
            pe.wait_ge(S("onehot32_ready"), 1)
            for k in range(2):
                for t in range(ET):
                    last = mm(B[4][:, k * P:(k + 1) * P], edg[:, t, k * P:(k + 1) * P], ohd32[:, t, :],
                              start=t == 0, stop=t == ET - 1)
            last.then_inc(S("eat_done"), 1)
            pe.wait_ge(S("we_loaded"), 32)
            pe.wait_ge(S("b5_free"), 1)
            mm(B[5][0:1, 2 * P:3 * P], con[:, K_HALF:K_HALF + 1], apT[:, :], start=True, stop=True).then_inc(S("deg_done"), 1)
            pe.wait_ge(S("b4_free"), 1)
            for f in range(KT):
                o = B[f // 3][:, f % 3 * P:(f % 3 + 1) * P]
                for k in range(2):
                    mm(o, we[:, k, f * P:(f + 1) * P], eat[:, k, :], start=k == 0, stop=False)
                if f == 0:
                    pe.wait_ge(S("deg_saved"), 1)
                last = mm(o, be_s[:, f * P:(f + 1) * P], deg[:, :], start=False, stop=True)
                if f % 3 == 2:
                    last.then_inc(S("ept_done"), 1)
            pe.wait_ge(S("sel_loaded"), 16)
            with pe.Fori(0, L_GNN) as l:
                for h in range(2):
                    pe.wait_ge(S("nodes_ready"), 2 * l + (h + 1))
                    transposes(tiles(nodes, h), B[6 + h]).then_inc(S("nodes_tr"), 1)
                for h in range(2):
                    pe.wait_ge(S(f"b{4 + h}_free"), l + 1)
                    for i in range(3):
                        f = 3 * h + i
                        last = mm(B[4 + h][:, i * P:(i + 1) * P], nodes[:, f * P:(f + 1) * P], apT[:, :],
                                  start=True, stop=True)
                    last.then_inc(S("agg_done"), 1)
                pe.wait_ge(S("ept_saved"), 2)
                pe.wait_ge(S("nodT0_saved"), l + 1)
                pe.wait_ge(S("nodT1_saved"), l + 1)
                for h in range(2):
                    mm(B[h][:, 0:HALF], selb[:, bass.ds((l + B_B1) * P, P)], btab[:, h * HALF:(h + 1) * HALF],
                       start=True, stop=False)
                    ring_unit(C_LOOP + h, l + (C_LOOP + h) // SLOTS, B[h], nodT, stop=False)
                pe.wait_ge(S("agg_saved"), 2 * l + 2)
                for h in range(2):
                    c = C_LOOP + 2 + h
                    ring_unit(c, l + c // SLOTS, B[h], agg)
                def turn_z(h):
                    pe.wait_ge(S("z_ready"), 2 * l + (h + 1))
                    transposes(tiles(z, h), B[6 + h]).then_inc(S("z_tr"), 1)

                c = C_LOOP + 4
                ring_unit(c, l + c // SLOTS, B[4], xnT, start=True, ks=range(KT - 1))
                turn_z(0)
                ring_unit(c, l + c // SLOTS, B[4], xnT, ks=range(KT - 1, KT))
                turn_z(1)
                for h in range(2):
                    mm(B[2 + h][:, 0:HALF], selb[:, bass.ds((l + B_B2) * P, P)],
                       btab[:, h * HALF:(h + 1) * HALF], start=True, stop=False)
                c = C_LOOP + 5
                for k in FRONT:
                    pe.wait_ge(S("hT0_saved"), 3 * l + (k + 1))
                    ring_unit(c, l + c // SLOTS, B[2], hT, ks=range(k, k + 1))
                pe.wait_ge(S("hT1_saved"), l + 1)
                ring_unit(c, l + c // SLOTS, B[2], hT, ks=BACK)
                c = C_LOOP + 6
                ring_unit(c, l + c // SLOTS, B[3], hT)
                c = C_LOOP + 7
                ring_unit(c, l + c // SLOTS, B[5], xnT, start=True)

            for h in range(2):
                pe.wait_ge(S("nodes_ready"), 2 * L_GNN + h + 1)
                transposes(tiles(nodes, h), B[6 + h]).then_inc(S("nodes_tr"), 1)

            def qkv_unit(i, bank):
                bias(bank, B_QKV + i // 2, i % 2)
                ring_unit(C_QKV + i, (C_QKV + i) // SLOTS, bank, nodT)

            pe.wait_ge(S("nodT0_saved"), L_GNN + 1)
            bias(B[0], B_QKV, 0)
            ring_unit(C_QKV, C_QKV // SLOTS, B[0], nodT, ks=FRONT)
            pe.wait_ge(S("nodT1_saved"), L_GNN + 1)
            ring_unit(C_QKV, C_QKV // SLOTS, B[0], nodT, ks=BACK)
            for i in range(1, 4):
                qkv_unit(i, B[i])
            q0, k0 = zh[:, 0, :], zh[:, 1, :]
            for h in range(2):
                pe.wait_ge(S(f"qk{h}_saved"), 1)
                transposes(tiles(q0, h, 4, DH0), B[6 + h], DH0).then_inc(S("q_tr"), 1)
            pe.wait_ge(S("b4_free"), L_GNN + 1)
            qkv_unit(4, B[4])
            for h in range(2):
                pe.wait_ge(S(f"qk{h}_saved"), 2)
                transposes(tiles(k0, h, 4, DH0), B[h], DH0).then_inc(S("k_tr"), 1)
            pe.wait_ge(S("b5_free"), L_GNN + 1)
            qkv_unit(5, B[5])
            qT = blk[0:DH0, 0:1024]
            kT = blk[0:DH0, 1024:2048]
            for h in range(2):
                pe.wait_ge(S(f"q{h}T_saved"), 1)
                pe.wait_ge(S(f"k{h}T_saved"), 1)
                for i in range(4):
                    o = (4 * h + i) * P
                    last = mm(B[2 + h][:, i * P:(i + 1) * P], qT[:, o:o + P], kT[:, o:o + P], start=True, stop=True)
                last.then_inc(S("scores_done"), 1)
            pe.wait_ge(S("elu_ready"), 1)
            for h in range(2):
                transposes(tiles(mix[:, 0, :], h), B[6 + h]).then_inc(S("mq_tr"), 1)
            pe.wait_ge(S("vaug_ready"), 1)
            for h in range(2):
                for i in range(3):
                    g = 3 * h + i
                    last = mm(B[h][:, i * 130:(i + 1) * 130], mix[:, 1, g * P:(g + 1) * P],
                              ept[:, g * 130:(g + 1) * 130], start=True, stop=True)
                last.then_inc(S("kv_done"), 1)
            pe.wait_ge(S("mqT_saved"), 2)
            for h in range(2):
                pe.wait_ge(S("kv_saved"), h + 1)
                for i in range(3):
                    g = 3 * h + i
                    last = mm(B[6 + h][:, i * 130:(i + 1) * 130], nodT[:, g, :],
                              xnt[:, g * 130:(g + 1) * 130], start=True, stop=True)
                last.then_inc(S("lin_done"), 1)
            probs, probT = blk[:, 2048:3072], blk[:, 0:1024]
            for h in range(2):
                pe.wait_ge(S("probs_ready"), h + 1)
                transposes([probs[:, (4 * h + i) * P:(4 * h + i + 1) * P] for i in range(4)],
                           B[2 + h]).then_inc(S("probs_tr"), 1)
            pe.wait_ge(S("v0_saved"), 1)
            pe.wait_ge(S("v1_saved"), 1)
            for h in range(2):
                keep_x(B[4 + h], X, h)
                bias(B[4 + h], B_BO, h, start=False)
            for h in range(2):
                pe.wait_ge(S("lin_ready"), h + 1)
                transposes(tiles(zh[:, 0, :], h), B[h]).then_inc(S("lin_tr"), 1)
            v0 = agg[:, :, :].rearrange("p k n -> p (k n)")
            for h in range(2):
                pe.wait_ge(S("probT_saved"), h + 1)
                for i in range(4):
                    o = 4 * h + i
                    last = mm(B[6 + h][:, i * DH0:(i + 1) * DH0], probT[:, o * P:(o + 1) * P],
                              v0[:, o * DH0:(o + 1) * DH0], start=True, stop=True)
                last.then_inc(S("attn_done"), 1)
            def out_unit(c, h, lhsT, ks=WHOLE, stop=False):
                ring_unit(c + h, (c + h) // SLOTS, B[4 + h], lhsT, ks=ks, stop=stop)

            pe.wait_ge(S("linT0_saved"), 1)
            out_unit(C_MIXP, 0, hT, FRONT)
            pe.wait_ge(S("linT1_saved"), 1)
            out_unit(C_MIXP, 0, hT, BACK)
            out_unit(C_MIXP, 1, hT, FRONT)
            for h in range(2):
                pe.wait_ge(S("attn_ready"), h + 1)
                transposes(tiles(mix[:, 0, :], h), B[h]).then_inc(S("attn_tr"), 1)
            out_unit(C_MIXP, 1, hT, BACK)
            attnT = mix[:, 1, :].rearrange("p (k n) -> p k n", k=KT)
            pe.wait_ge(S("attnT0_saved"), 1)
            out_unit(C_WO, 0, attnT, FRONT)
            pe.wait_ge(S("attnT1_saved"), 1)
            out_unit(C_WO, 0, attnT, BACK, stop=True)
            out_unit(C_WO, 1, attnT, stop=True)

            for h in range(2):
                pe.wait_ge(S("xl_ready"), h + 1)
                transposes(tiles(nodes, h), B[6 + h]).then_inc(S("xl_tr"), 1)
            pe.wait_ge(S("cols_loaded"), 16)
            pe.wait_ge(S("pooled_ready"), 2)
            for k in range(KT):
                last = mm(B[0][0:1, 0:E_FFN], pooled[:, k:k + 1], col[:, G_RW0 + k * 4:G_RW0 + k * 4 + 4],
                          start=k == 0, stop=k == KT - 1)
            last.then_inc(S("logit_done"), 1)
            pe.wait_ge(S("xlT_saved"), 2)
            for h in range(2):
                keep_x(B[6 + h], nodes, h)
            act_s = mix[:, 0, :].rearrange("p (b n) -> p b n", b=2)
            heT = [zh[:, :, :].rearrange("p a (k n) -> p (a k) n", n=P),
                   mix[:, 1:3, :].rearrange("p a (k n) -> p (a k) n", n=P)]

            def up(i):
                s, q = QUARTERS[i]
                bank = B[i % 4]
                if i >= 4:
                    pe.wait_ge(S("act_ready"), i - 3)
                if q == 0:
                    for e in range(E_FFN if s == 0 else 0):
                        pe.wait_ge(S(f"slot{(R_FFN + e) % SLOTS}"), 16 * ((R_FFN + e) // SLOTS + 1))
                    for k in range(KT):
                        if i == 0 and k == 1:
                            pe.wait_ge(S("choice_ready"), 1)
                            mm(B[3][:, 0:4], con[0:1, K_ONE:K_ONE + P], choice0,
                               start=True, stop=True).then_inc(S("choice_done"), 1)
                        last = mm(
                           bank[:, 0:HALF], nodT[:, k, :],
                           ring[:, bass.ds(mine[s] + R_FFN % SLOTS, 1), k * HALF:(k + 1) * HALF]
                           .rearrange("p a n -> p (a n)"), start=k == 0, stop=False)
                    if s == 1:
                        last.then_inc(S("units_done"), E_FFN)
                else:
                    c = R_EXP + FFN_ORDER.index((s, q))
                    pe.wait_ge(S(f"slot{c % SLOTS}"), 16 * (c // SLOTS + 1))
                    unit(bank, nodT, ring[:, c % SLOTS, :], start=True, stop=False).then_inc(S("units_done"), 1)
                if i == 0:
                    pe.wait_ge(S("selx_ready"), 1)
                mm(bank[:, 0:HALF], selx[:, s * P:(s + 1) * P], btab[:, D + q * HALF:D + (q + 1) * HALF],
                   start=False, stop=True).then_inc(S("up_done"), 1)

            def turn(i):
                pe.wait_ge(S("act_ready"), i + 1)
                if i >= 2:
                    pe.wait_ge(S("heT_saved"), i - 1)
                transposes([act_s[:, i % 2, j * P:(j + 1) * P] for j in range(3)], B[4 + i % 2]).then_inc(S("act_tr"), 1)

            def down(s, g):
                for h in range(2):
                    c = R_EXP + FFN_ORDER.index((s, 4 + 2 * g + h))
                    pe.wait_ge(S("heT_saved"), QUARTERS.index((s, 2 * g + 1)) + 1)
                    ring_unit(c, c // SLOTS, B[6 + h], heT[s][:, 6 * g:6 * g + 6, :], stop=s == 1 and g == 1)

            pe.wait_ge(S("routed"), 1)
            mine = [pe.value_load(eidx[0:1, s:s + 1], min_val=0, max_val=E_FFN - 1) for s in range(TOP_K)]
            up(0)
            up(1)
            pe.wait_ge(S("b2_loaded"), 16)
            pe.wait_ge(S("gates_ready"), 1)
            for h in range(2):
                mm(B[6 + h][:, 0:HALF], g4[:, :], b2f[:, h * HALF:(h + 1) * HALF], start=False, stop=False)
            up(2)
            turn(0)
            up(3)
            turn(1)
            up(4)
            up(5)
            turn(2)
            up(6)
            turn(3)
            down(0, 0)
            turn(4)
            up(7)
            turn(5)
            down(0, 1)
            turn(6)
            turn(7)
            down(1, 0)
            down(1, 1)

            for h in range(2):
                pe.wait_ge(S("xn2_ready"), h + 1)
                transposes(tiles(nodes, h), B[4 + h]).then_inc(S("xn2_tr"), 1)

            def l1(j, bank, lhsT, **kw):
                c = R_L1 + j
                ring_unit(c, c // SLOTS, bank, lhsT, **kw)

            pe.wait_ge(S("xn2T0_saved"), 1)
            pe.wait_ge(S("early0_loaded"), 16)
            unit(B[0], nodT, early[:, 0, :], start=True, ks=FRONT)
            pe.wait_ge(S("xn2T1_saved"), 1)
            unit(B[0], nodT, early[:, 0, :], ks=BACK).then_inc(S("gat_h1_done"), 1)
            pe.wait_ge(S("early1_loaded"), 16)
            unit(B[1], nodT, early[:, 1, :], start=True).then_inc(S("gat_h1_done"), 1)
            l1(0, B[2], nodT, start=True)
            l1(1, B[3], nodT, start=True)

            def spread(g, bank):
                pe.wait_ge(S("diag_ready"), g + 1)
                mm(bank[:, 0:P], con[:, K_ONE:K_ONE + P], blk[:, 0:P], start=True, stop=True).then_inc(S("spread_done"), 1)

            def alpha_turn(g, bank):
                pe.wait_ge(S("alpha_ready"), g + 1)
                nc.tensor.transpose(bank[:, 0:P], blk[:, P:2 * P], ident).then_inc(S("alpha_tr"), 1)

            spread(0, B[6])
            l1(2, B[4], nodT, start=True)
            alpha_turn(0, B[7])
            l1(3, B[5], nodT, start=True)
            h1 = agg[:, :, :].rearrange("p k n -> p (k n)")
            h2 = ept[:, 0:D]
            alT = blk[:, 2 * P:3 * P]
            pe.wait_ge(S("alphaT_saved"), 1)
            for h in range(2):
                for i in range(3):
                    f = 3 * h + i
                    last = mm(B[6 + h][:, i * P:(i + 1) * P], h1[:, f * P:(f + 1) * P], alT, start=True, stop=True)
                last.then_inc(S("gat1_done"), 1)
            pe.wait_ge(S("h1_saved"), 2)
            l1(4, B[0], nodT, start=True)
            l1(5, B[1], nodT, start=True)
            g1T = blk[:, 1024:1024 + D].rearrange("p (k n) -> p k n", k=KT)
            pe.wait_ge(S("g1T_saved"), 2)
            pe.wait_ge(S("mq1_ready"), 2)
            l1(6, B[2], g1T, start=True)
            l1(7, B[3], g1T, start=True)
            for h in range(2):
                transposes(tiles(mix[:, 0, :], h), B[6 + h]).then_inc(S("mq1_tr"), 1)
            pe.wait_ge(S("mk1_saved"), 2)
            pe.wait_ge(S("mv1_saved"), 2)
            for h in range(2):
                for i in range(3):
                    g = 3 * h + i
                    last = mm(B[4 + h][:, i * P:(i + 1) * P], mix[:, 1, g * P:(g + 1) * P],
                              mix[:, 2, g * P:(g + 1) * P], start=True, stop=True)
                last.then_inc(S("kv1_done"), 1)
            for h in range(2):
                keep_x(B[h], X, h)
                bias(B[h], B_GAT2, h, start=False)
            spread(1, B[2])
            pe.wait_ge(S("mq1T0_saved"), 1)
            pe.wait_ge(S("mq1T1_saved"), 1)
            for h in range(2):
                pe.wait_ge(S("kv1_saved"), h + 1)
                for i in range(3):
                    g = 3 * h + i
                    last = mm(B[6 + h][:, i * P:(i + 1) * P], xnT[:, g, :], zh[:, 0, g * P:(g + 1) * P],
                              start=True, stop=True)
                last.then_inc(S("lin1_done"), 1)
            for h in range(2):
                pe.wait_ge(S("lin1_saved"), h + 1)
                transposes(tiles(zh[:, 1, :], h), B[4 + h]).then_inc(S("lin1_tr"), 1)
            l1T = blk[:, 2048:2048 + D].rearrange("p (k n) -> p k n", k=KT)
            pe.wait_ge(S("lin1T_saved"), 1)
            l1(8, B[0], l1T, stop=False, ks=FRONT)
            pe.wait_ge(S("lin1T_saved"), 2)
            l1(8, B[0], l1T, stop=False, ks=BACK)
            l1(9, B[1], l1T, stop=False, ks=FRONT)
            alpha_turn(1, B[3])
            l1(9, B[1], l1T, stop=False, ks=BACK)
            pe.wait_ge(S("alphaT_saved"), 2)
            for h in range(2):
                mm(B[h][:, 0:HALF], alT, h2[:, h * HALF:(h + 1) * HALF], start=False,
                   stop=True).then_inc(S("x3_done"), 1)

            for h in range(2):
                pe.wait_ge(S("xl3_ready"), h + 1)
                transposes(tiles(nodes, h), B[4 + h]).then_inc(S("xl3_tr"), 1)
            pe.wait_ge(S("moe_loaded"), 16)
            hm = agg[:, :, :].rearrange("p k n -> p (k n)")

            def moe_up(w, bank, cols, ks=WHOLE):
                for k in ks:
                    o = (w * KT + k) * FH
                    last = mm(bank[:, cols], nodT[:, k, :], moe[:, o + cols.start:o + cols.stop],
                              start=k == 0, stop=k == KT - 1)
                return last

            def moe_turn(p):
                pe.wait_ge(S("moe_h_ready"), p + 1)
                transposes([hm[:, i * P:(i + 1) * P] for i in (2 * p, 2 * p + 1)], B[6 + p]).then_inc(S("moe_h_tr"), 1)

            def moe_down(h, p):
                for k in (2 * p, 2 * p + 1):
                    o = 2 * KT * FH + k * D + h * HALF
                    last = mm(B[h][:, 0:HALF], ept[:, k * P:(k + 1) * P], moe[:, o:o + HALF],
                              start=k == 0, stop=k == 3)
                return last

            pe.wait_ge(S("xl3T0_saved"), 1)
            moe_up(0, B[2], slice(0, FH), FRONT)
            pe.wait_ge(S("xl3T1_saved"), 1)
            moe_up(0, B[2], slice(0, FH), BACK).then_inc(S("moe_up_done"), 1)
            for k in range(KT):
                last = mm(B[6][:, 0:E_MOE], nodT[:, k, :], col[:, G_RW1 + k * 8:G_RW1 + k * 8 + 8],
                          start=k == 0, stop=k == KT - 1)
            last.then_inc(S("route1_done"), 1)
            moe_up(1, B[3], slice(0, FH // 2)).then_inc(S("moe_up_done"), 1)
            moe_up(1, B[4], slice(FH // 2, FH), range(KT - 2))
            moe_turn(0)
            moe_up(1, B[4], slice(FH // 2, FH), range(KT - 2, KT)).then_inc(S("moe_up_done"), 1)
            pe.wait_ge(S("x_saved"), 4)
            pe.wait_ge(S("moe_hT_saved"), 1)
            moe_down(0, 0)
            moe_turn(1)
            moe_down(1, 0)
            pe.wait_ge(S("moe_hT_saved"), 2)
            for h in range(2):
                moe_down(h, 1).then_inc(S("moe_done"), 1)

        @block.scalar
        def _(act):
            A = nc.scalar.activation
            chain = [0]

            def link(ins):
                chain[0] += 1
                ins.then_inc(S("act_chain"), 1)
                act.wait_ge(S("act_chain"), chain[0])

            def root(k):
                act.wait_ge(S("var_ready"), k)
                A(std[:, :], mv[:, 1:2], ACT.Sqrt, bias=eps).then_inc(S("std_ready"), 1)

            def save(out_ap, in_ap, name):
                A(out_ap, in_ap, ACT.Copy).then_inc(S(name), 1)

            def h3(bank):
                return bank[:, 0:HALF]

            def flat(t, h):
                return t[:, 3 * h:3 * h + 3, :].rearrange("p k n -> p (k n)")

            act.wait_ge(S("first_set"), 1)
            A(std[:, :], mv[:, 1:2], ACT.Sqrt).then_inc(S("first_root"), 1)
            act.wait_ge(S("con_loaded"), 16)
            root(1)
            act.wait_ge(S("xn_tr"), 1)
            save(flat(xnT, 0), h3(B[6]), "xnT0_saved")
            act.wait_ge(S("onehot_dst_ready"), 1)
            save(ohd32, ohb[:, 1, :, :], "onehot32_ready")
            act.wait_ge(S("eat_done"), 1)
            save(eat.rearrange("p k n -> p (k n)"), B[4][:, 0:2 * P], "b4_free")
            act.wait_ge(S("ept_done"), 1)
            save(flat(eptT, 0), h3(B[0]), "ept_saved")
            act.wait_ge(S("cols_loaded"), 16)

            with act.Fori(0, L_GNN) as l:
                act.wait_ge(S("nodes_tr"), 2 * l + 1)
                save(flat(nodT, 0), h3(B[6]), "nodT0_saved")
                root(l + 2)
                act.wait_ge(S("z_tr"), 2 * l + 1)
                for f in range(3):
                    last = A(hT[:, f, :], B[6][:, f * P:(f + 1) * P], ACT.Relu,
                             scale=col[:, bass.ds(l * KT + (G_G + f), 1)],
                             bias=col[:, bass.ds(l * KT + (G_B + f), 1)])
                    last.then_inc(S("hT0_saved"), 1)
                act.wait_ge(S("units_done"), l * 8 + (C_LOOP + 5))
                A(mix[:, bass.ds(l, 1), 0:HALF].rearrange("p a n -> p (a n)"), h3(B[4]), ACT.Copy).then_inc(S("b4_free"), 1)
                act.wait_ge(S("units_done"), l * 8 + (C_LOOP + 8))
                A(mix[:, bass.ds(l, 1), HALF:D].rearrange("p a n -> p (a n)"), h3(B[5]), ACT.Copy).then_inc(S("b5_free"), 1)

            act.wait_ge(S("nodes_tr"), 2 * L_GNN + 1)
            save(flat(nodT, 0), h3(B[6]), "nodT0_saved")
            ex = early[:, 1, 0:2 * D]
            act.wait_ge(S("elu_min_ready"), 1)
            A(ex, ex, ACT.Exp).then_inc(S("elu_exp_ready"), 1)
            act.wait_ge(S("units_done"), C_QKV + 2)
            save(zh[:, 0, HALF:D], h3(B[1]), "qk1_saved")
            act.wait_ge(S("q_tr"), 1)
            save(blk[0:DH0, 0:512], B[6][0:DH0, :], "q0T_saved")
            act.wait_ge(S("units_done"), C_QKV + 4)
            save(zh[:, 1, HALF:D], h3(B[3]), "qk1_saved")
            act.wait_ge(S("k_tr"), 1)
            save(blk[0:DH0, 1024:1536], B[0][0:DH0, :], "k0T_saved")
            act.wait_ge(S("k_tr"), 2)
            save(blk[0:DH0, 1536:2048], B[1][0:DH0, :], "k1T_saved")
            act.wait_ge(S("units_done"), C_QKV + 6)
            save(agg[:, 3:6, :].rearrange("p k n -> p (k n)"), h3(B[5]), "v1_saved")
            for h in range(2):
                act.wait_ge(S("mq_tr"), h + 1)
                save(flat(nodT, h), h3(B[6 + h]), "mqT_saved")
            for h in range(2):
                act.wait_ge(S("shifted"), h + 1)
                pr = blk[:, 2048 + 512 * h:2560 + 512 * h]
                A(pr, pr, ACT.Exp, scale=DH0 ** -0.5).then_inc(S("probs_ready"), 1)
            act.wait_ge(S("probs_tr"), 1)
            save(blk[:, 0:512], B[2][:, :], "probT_saved")
            act.wait_ge(S("probs_tr"), 2)
            save(blk[:, 512:1024], B[3][:, :], "probT_saved")
            act.wait_ge(S("lin_tr"), 1)
            save(flat(hT, 0), h3(B[0]), "linT0_saved")
            act.wait_ge(S("attn_tr"), 1)
            save(mix[:, 1, 0:HALF], h3(B[0]), "attnT0_saved")

            root(5)
            for h in range(2):
                act.wait_ge(S("pooled_ready"), h + 1)
                save(flat(nodT, h), h3(B[6 + h]), "xlT_saved")
            for h in range(2):
                save(X[:, h * HALF:(h + 1) * HALF], h3(B[4 + h]), "x_saved")
            act.wait_ge(S("margin_ready"), 1)
            A(rt[0:1, 5:6], rt[0:1, 4:5], ACT.Tanh, scale=0.5).then_inc(S("margin_tanh"), 1)
            buf = blk[:, :].rearrange("p (b a n) -> p b a n", b=2, a=4)
            heT = [zh[:, :, :], mix[:, 1:3, :]]

            def quarter(i):
                s = QUARTERS[i][0]
                act.wait_ge(S("up_done"), i + 1)
                if i >= 2:
                    act.wait_ge(S("act_ready"), i - 1)
                b = buf[:, i % 2]
                A(b[:, 1, :], h3(B[i % 4]), ACT.Gelu)
                link(A(b[:, 0, :], h3(B[i % 4]), ACT.Tanh, scale=0.5))
                link(A(b[:, 2, :], b[:, 0, :], ACT.Copy, scale=-1.0, bias=1.0))
                A(b[:, 3, :], b[:, 2, :], ACT.Identity, scale=oh[:, s, 2:3], bias=oh[:, s, 1:2]).then_inc(S("soft_ready"), 1)

            def turned(i):
                s, q = QUARTERS[i]
                act.wait_ge(S("act_tr"), i + 1)
                A(heT[s][:, q // 2, q % 2 * HALF:(q % 2 + 1) * HALF], h3(B[4 + i % 2]), ACT.Copy).then_inc(S("heT_saved"), 1)

            quarter(0)
            quarter(1)
            for i in range(2, 8):
                quarter(i)
                turned(i - 2)
            turned(6)
            turned(7)

            root(6)
            root(7)
            act.wait_ge(S("xn2_tr"), 1)
            save(flat(nodT, 0), h3(B[4]), "xn2T0_saved")
            act.wait_ge(S("gat_h1_done"), 1)
            save(flat(agg, 0), h3(B[0]), "h1_saved")
            act.wait_ge(S("gat_h1_done"), 2)
            save(flat(agg, 1), h3(B[1]), "h1_saved")
            act.wait_ge(S("gat_logit"), 1)
            A(blk[:, P:2 * P], blk[:, P:2 * P], ACT.Exp).then_inc(S("gat_exp"), 1)
            for h in range(2):
                act.wait_ge(S("units_done"), R_L1 + 1 + h)
                A(mix[:, 0, h * HALF:(h + 1) * HALF], h3(B[2 + h]), ACT.Gelu).then_inc(S("mq1_ready"), 1)
            for h in range(2):
                act.wait_ge(S("gat1_done"), h + 1)
                for i in range(3):
                    f = 3 * h + i
                    last = A(blk[:, 1024 + f * P:1024 + (f + 1) * P], B[6 + h][:, i * P:(i + 1) * P], ACT.Relu,
                             bias=col[:, G_GB1 + f:G_GB1 + f + 1])
                last.then_inc(S("g1T_saved"), 1)
            for h in range(2):
                act.wait_ge(S("units_done"), R_L1 + 5 + h)
                save(mix[:, 2, h * HALF:(h + 1) * HALF], h3(B[h]), "mv1_saved")
            act.wait_ge(S("mq1_tr"), 1)
            save(flat(xnT, 0), h3(B[6]), "mq1T0_saved")
            act.wait_ge(S("zh_clear"), 1)
            for h in range(2):
                act.wait_ge(S("kv1_done"), h + 1)
                for o in range(2):
                    rows = slice(64 * o, 64 * o + 64)
                    dstk = zh[rows, 0, h * HALF:(h + 1) * HALF].rearrange("p (g c) -> p g c", g=3)[:, :, 64 * o:64 * o + 64]
                    srck = B[4 + h][rows, 0:HALF].rearrange("p (g c) -> p g c", g=3)[:, :, 64 * o:64 * o + 64]
                    last = A(dstk, srck, ACT.Gelu, scale=DM ** -0.5)
                last.then_inc(S("kv1_saved"), 1)
            act.wait_ge(S("lin1_done"), 1)
            save(zh[:, 1, 0:HALF], h3(B[6]), "lin1_saved")
            act.wait_ge(S("lin1_done"), 2)
            save(zh[:, 1, HALF:D], h3(B[7]), "lin1_saved")
            act.wait_ge(S("lin1_tr"), 1)
            save(blk[:, 2048:2048 + HALF], h3(B[4]), "lin1T_saved")
            act.wait_ge(S("lin1_tr"), 2)
            save(blk[:, 2048 + HALF:2048 + D], h3(B[5]), "lin1T_saved")
            act.wait_ge(S("gat_logit"), 2)
            A(blk[:, P:2 * P], blk[:, P:2 * P], ACT.Exp).then_inc(S("gat_exp"), 1)
            root(8)
            act.wait_ge(S("xl3_tr"), 1)
            save(flat(nodT, 0), h3(B[4]), "xl3T0_saved")
            for h in range(2):
                act.wait_ge(S("xl3_ready"), h + 1)
                save(X[:, h * HALF:(h + 1) * HALF], h3(B[h]), "x_saved")
            act.wait_ge(S("moe_up_done"), 1)
            A(z[:, 0:FH], B[2][:, :], ACT.Silu).then_inc(S("silu_ready"), 1)
            act.wait_ge(S("moe_h_tr"), 1)
            save(ept[:, 0:2 * P], B[6][:, 0:2 * P], "moe_hT_saved")
            act.wait_ge(S("moe_shift"), 1)
            A(rt[:, 40:48], rt[:, 32:40], ACT.Exp, accum_out=rt[:, 48:49]).then_inc(S("moe_exp"), 1)
            act.wait_ge(S("moe_h_tr"), 2)
            save(ept[:, 2 * P:4 * P], B[7][:, 0:2 * P], "moe_hT_saved")

        @block.vector
        def _(dve):
            V = nc.vector
            base, chain, in_loop, parts = [0], [0], [False], [0]

            def mark(ins):
                chain[0] += 1
                ins.then_inc(S("dve_chain"), 1)
                return base[0] + chain[0]

            def need(count):
                dve.wait_ge(S("dve_chain"), count)

            def link(ins):
                need(mark(ins))

            def h3(bank):
                return bank[:, 0:HALF]

            def halves(t):
                return t[:, 0:HALF], t[:, HALF:D]

            def flat(t, h):
                return t[:, 3 * h:3 * h + 3, :].rearrange("p k n -> p (k n)")

            def stats(h, ap):
                return mark(V.bn_stats(st[:, h, :], ap))

            def spread_of(k):
                need(base[0] + chain[0])
                if in_loop[0]:
                    V.tensor_copy(rt[:, 64:65], st[:, 0, 0:1])
                V.bn_aggr(mv[:, :], st[:, :, :].rearrange("p a b -> p (a b)")).then_inc(S("var_ready"), 1)
                dve.wait_ge(S("std_ready"), k)
                link(V.reciprocal(rstd[:, :], std[:, :]))

            def norm(o, i):
                return V.tensor_scalar(o, i, mv[:, 0:1], rstd[:, 0:1], ALU.subtract, ALU.mult)

            V.memset(mv[:, :], 1.0).then_inc(S("first_set"), 1)
            for h in range(2):
                dve.wait_ge(S(f"x{h}_loaded"), 16)
                stats(h, halves(X)[h])
            dve.wait_ge(S("first_root"), 1)
            spread_of(1)
            for h in range(2):
                norm(halves(xn)[h], halves(X)[h]).then_inc(S("xn_ready"), 1)
            dve.wait_ge(S("index_loaded"), 32)
            link(V.tensor_copy(sd_b[:, :, :], sd_i[:, :, :]))
            dve.wait_ge(S("xn_tr"), 2)
            V.tensor_copy(flat(xnT, 1), h3(B[7])).then_inc(S("xnT1_saved"), 1)
            dve.wait_ge(S("con_loaded"), 16)
            link(V.tensor_copy(iota_b[:, :], iota))
            for a in (1, 0):
                onehot = V.tensor_tensor(ohb[:, a, :, :],
                                         iota_b[:, :].rearrange("p (a n) -> p a n", a=1).broadcast_to([P, ET, P]),
                                         sd_b[:, a, :].rearrange("p (t a) -> p t a", a=1).broadcast_to([P, ET, P]),
                                         ALU.is_equal)
                if a == 1:
                    onehot.then_inc(S("onehot_dst_ready"), 1)
            link(onehot)
            dve.wait_ge(S("onehot_dst_ready"), 1)
            V.tensor_tensor(ohb[:, 2, :, :], ohb[:, 0, :, :], ohb[:, 1, :, :], ALU.add).then_inc(S("onehot_ready"), 1)

            def split_rows(c):
                link(V.tensor_copy(btab[:, c], bsrc[:, c]))
                for rows in (slice(0, 64), slice(0, 32)):
                    link(V.tensor_tensor(bsrc[rows, c], bsrc[rows, c], btab[rows, c], ALU.subtract))
                    V.tensor_copy(btab[rows, c], bsrc[rows, c]).then_inc(S("btab_ready"), 1)
                    parts[0] += 1
                    dve.wait_ge(S("btab_ready"), parts[0])

            dve.wait_ge(S("bias_loaded"), 16)
            split_rows(slice(0, D))
            for h in range(2):
                dve.wait_ge(S("wn_done"), h + 1)
                V.tensor_copy(halves(nodes)[h], h3(B[2 + h])).then_inc(S("nodes_ready"), 1)
            dve.wait_ge(S("adj_done"), 1)
            link(V.tensor_tensor(cnt[:, :], B[5][:, P:2 * P], ident, ALU.add))
            V.tensor_copy(apT[:, :], B[5][:, 0:P]).then_inc(S("b5_free"), 1)
            V.tensor_scalar(cneg[:, :], cnt[:, :], 0.0, -1e30, ALU.is_equal, ALU.mult)
            dve.wait_ge(S("deg_done"), 1)
            V.tensor_copy(deg[:, :], B[5][0:1, 2 * P:3 * P]).then_inc(S("deg_saved"), 1)
            dve.wait_ge(S("ept_done"), 2)
            V.tensor_copy(flat(eptT, 1), h3(B[1])).then_inc(S("ept_saved"), 1)
            dve.wait_ge(S("ept_saved"), 2)

            per_layer = 4
            c0 = chain[0]
            with dve.Fori(0, L_GNN) as l:
                chain[0] = c0
                base[0], in_loop[0] = l * per_layer, True
                dve.wait_ge(S("nodes_tr"), 2 * l + 2)
                V.tensor_copy(flat(nodT, 1), h3(B[7])).then_inc(S("nodT1_saved"), 1)
                for h in range(2):
                    dve.wait_ge(S("agg_done"), 2 * l + (h + 1))
                    V.tensor_tensor(flat(agg, h), h3(B[4 + h]), flat(eptT, h), ALU.add).then_inc(S("agg_saved"), 1)
                for h in range(2):
                    dve.wait_ge(S("units_done"), l * 8 + (C_LOOP + 3 + h))
                    stats(h, h3(B[h]))
                spread_of(l + 2)
                for h in range(2):
                    norm(halves(z)[h], h3(B[h])).then_inc(S("z_ready"), 1)
                dve.wait_ge(S("z_tr"), 2 * l + 2)
                for i in range(3):
                    last = V.tensor_scalar(hT[:, 3 + i, :], B[7][:, i * P:(i + 1) * P],
                                           col[:, bass.ds(l * KT + (G_G + 3 + i), 1)],
                                           col[:, bass.ds(l * KT + (G_B + 3 + i), 1)], ALU.mult, ALU.add)
                link(last)
                V.tensor_scalar(flat(hT, 1), flat(hT, 1), 0.0, None, ALU.max).then_inc(S("hT1_saved"), 1)
                for h in range(2):
                    dve.wait_ge(S("units_done"), l * 8 + (C_LOOP + 6 + h))
                    n = halves(nodes)[h]
                    V.tensor_tensor(n, h3(B[2 + h]), n, ALU.add).then_inc(S("nodes_ready"), 1)
            assert chain[0] == c0 + per_layer
            base[0], chain[0], in_loop[0] = 0, c0 + per_layer * L_GNN, False

            dve.wait_ge(S("nodes_tr"), 2 * L_GNN + 2)
            V.tensor_copy(flat(nodT, 1), h3(B[7])).then_inc(S("nodT1_saved"), 1)
            dve.wait_ge(S("bias2_loaded"), 16)
            split_rows(slice(D, 3 * D))
            dve.wait_ge(S("b4_free"), L_GNN + 1)
            dve.wait_ge(S("b5_free"), L_GNN + 1)
            ex = early[:, 1, 0:2 * D]
            mqk = mix[:, 0:2, :].rearrange("p a n -> p (a n)")
            V.tensor_scalar(ex, mqk, 0.0, None, ALU.min).then_inc(S("elu_min_ready"), 1)
            link(V.tensor_tensor(X[:, :], X[:, :], nodes[:, :], ALU.add))
            dve.wait_ge(S("elu_exp_ready"), 1)
            V.scalar_tensor_tensor(mqk, mqk, 0.0, ex, ALU.max, ALU.add).then_inc(S("elu_ready"), 1)
            dve.wait_ge(S("units_done"), C_QKV + 1)
            V.tensor_copy(zh[:, 0, 0:HALF], h3(B[0])).then_inc(S("qk0_saved"), 1)
            dve.wait_ge(S("units_done"), C_QKV + 3)
            V.tensor_copy(zh[:, 1, 0:HALF], h3(B[2])).then_inc(S("qk0_saved"), 1)
            dve.wait_ge(S("q_tr"), 2)
            V.tensor_copy(blk[0:DH0, 512:1024], B[7][0:DH0, :]).then_inc(S("q1T_saved"), 1)
            dve.wait_ge(S("units_done"), C_QKV + 5)
            V.tensor_copy(flat(agg, 0), h3(B[4])).then_inc(S("v0_saved"), 1)
            mxs, sums, rec = sm[:, 0, 0:H0], sm[:, 1, 0:H0], sm[:, 2, 0:H0]

            def g3(ap, n):
                return ap.rearrange("p (g n) -> p g n", n=n)

            def rep(ap, n):
                g = ap.shape[1]
                return ap.rearrange("p (g a) -> p g a", a=1).broadcast_to([P, g, n])

            for h in range(2):
                dve.wait_ge(S("scores_done"), h + 1)
                m4 = mxs[:, 4 * h:4 * h + 4]
                link(V.tensor_reduce(m4, g3(B[2 + h][:, :], P), AX, ALU.max))
                V.tensor_tensor(g3(blk[:, 2048 + 512 * h:2560 + 512 * h], P), g3(B[2 + h][:, :], P), rep(m4, P),
                                ALU.subtract).then_inc(S("shifted"), 1)
            dve.wait_ge(S("kv_clear"), 1)
            for h in range(2):
                dve.wait_ge(S("kv_done"), h + 1)
                for o in range(2):
                    rows = slice(64 * o, 64 * o + 64)
                    last = V.tensor_copy(g3(xnt[rows, h * 390:(h + 1) * 390], 130)[:, :, 65 * o:65 * o + 65],
                                         g3(B[h][rows, 0:390], 130)[:, :, 65 * o:65 * o + 65])
                last.then_inc(S("kv_saved"), 1)
            for h in range(2):
                dve.wait_ge(S("probs_ready"), h + 1)
                link(V.tensor_reduce(sums[:, 4 * h:4 * h + 4], g3(blk[:, 2048 + 512 * h:2560 + 512 * h], P), AX, ALU.add))
            link(V.reciprocal(rec, sums))
            for h in range(2):
                dve.wait_ge(S("lin_done"), h + 1)
                lin = g3(B[6 + h][:, 0:390], 65)
                zr = sm[:, h, 8:14]
                link(V.reciprocal(zr.rearrange("p (g a) -> p g a", a=1), lin[:, :, 64:65]))
                V.tensor_tensor(g3(zh[:, 0, h * HALF:(h + 1) * HALF], 64), lin[:, :, 0:64], rep(zr, 64),
                                ALU.mult).then_inc(S("lin_ready"), 1)
            dve.wait_ge(S("lin_tr"), 2)
            V.tensor_copy(flat(hT, 1), h3(B[1])).then_inc(S("linT1_saved"), 1)
            for h in range(2):
                dve.wait_ge(S("attn_done"), h + 1)
                V.tensor_tensor(g3(mix[:, 0, h * HALF:(h + 1) * HALF], DH0), g3(h3(B[6 + h]), DH0),
                                rep(rec[:, 4 * h:4 * h + 4], DH0), ALU.mult).then_inc(S("attn_ready"), 1)
            dve.wait_ge(S("attn_tr"), 2)
            V.tensor_copy(mix[:, 1, HALF:D], h3(B[1])).then_inc(S("attnT1_saved"), 1)
            for h in range(2):
                dve.wait_ge(S("units_done"), C_WO + 1 + h)
                stats(h, h3(B[4 + h]))
            spread_of(5)
            for h in range(2):
                norm(halves(nodes)[h], h3(B[4 + h])).then_inc(S("xl_ready"), 1)
            link(V.memset(lg8, -3e38))
            for h in range(2):
                dve.wait_ge(S("xl_tr"), h + 1)
                V.tensor_reduce(pooled[:, 3 * h:3 * h + 3], g3(h3(B[6 + h]), P), AX, ALU.add).then_inc(S("pooled_ready"), 1)

            d4 = con[:, K_D4:K_D4 + 4]
            dve.wait_ge(S("logit_done"), 1)
            link(V.scalar_tensor_tensor(lg8[:, 0:E_FFN], B[0][0:1, 0:E_FFN], 1.0 / P, col[0:1, G_RB0:G_RB0 + E_FFN],
                                        ALU.mult, ALU.add))
            link(V.max(top8, lg8))
            V.max_index(eidx[:, :], top8, lg8).then_inc(S("routed"), 1)
            V.tensor_tensor(rt[0:1, 4:5], top8[:, 0:1], top8[:, 1:2], ALU.subtract).then_inc(S("margin_ready"), 1)
            dve.wait_ge(S("routed"), 1)
            V.tensor_copy(choice0[:, 0:2], eidx[:, 0:2])
            dve.wait_ge(S("margin_tanh"), 1)
            V.tensor_scalar(choice0[:, 2:3], rt[0:1, 5:6], 0.5, 0.5, ALU.mult, ALU.add)
            V.tensor_scalar(choice0[:, 3:4], rt[0:1, 5:6], -0.5, 0.5, ALU.mult, ALU.add).then_inc(S("choice_ready"), 1)
            dve.wait_ge(S("choice_done"), 1)
            V.tensor_copy(gate[:, :], B[3][:, 2:4])
            link(V.tensor_copy(rt[:, 0:2], B[3][:, 0:2]))
            link(V.tensor_tensor(oh[:, :, :], iota[:, 0:E_FFN].rearrange("p (a e) -> p a e", a=1)
                                 .broadcast_to([P, TOP_K, E_FFN]), rep(rt[:, 0:2], E_FFN), ALU.is_equal))
            own = rt[:, 66:68]
            tmp = rt[:, 68:76].rearrange("p (s e) -> p s e", s=2)
            link(V.tensor_tensor(tmp, oh[:, :, :], d4.rearrange("p (a e) -> p a e", a=1).broadcast_to([P, 2, 4]), ALU.mult))
            link(V.tensor_reduce(own, tmp, AX, ALU.add))
            V.tensor_copy(selx[:, :].rearrange("p (s n) -> p s n", s=2),
                          own[0:96, :].rearrange("p (s a) -> p s a", a=1).broadcast_to([96, 2, P])).then_inc(S("selx_ready"), 1)
            link(V.tensor_tensor(rt[:, 76:78], own, gate[:, :], ALU.mult))
            link(V.tensor_reduce(rt[:, 78:79], rt[:, 76:78], AX, ALU.add))
            V.tensor_copy(g4[:, :], rt[0:E_FFN, 78:79].broadcast_to([E_FFN, P])).then_inc(S("gates_ready"), 1)
            silu, mish = oh[:, :, 1], oh[:, :, 2]
            link(V.tensor_tensor(rt[:, 86:88], silu, mish, ALU.add))
            link(V.tensor_scalar(par[:, 0, :], mish, 2.0, 1.0, ALU.mult, ALU.add))
            link(V.tensor_tensor(par[:, 0, :], par[:, 0, :], rt[:, 86:88], ALU.add))
            link(V.scalar_tensor_tensor(par[:, 1, :], rt[:, 86:88], -1.0, gate[:, :], ALU.mult, ALU.mult))
            V.tensor_tensor(par[:, 2, :], par[:, 1, :], gate[:, :], ALU.add).then_inc(S("params_ready"), 1)
            dve.wait_ge(S("params_ready"), 1)

            buf = blk[:, :].rearrange("p (b a n) -> p b a n", b=2, a=4)
            vv = agg[:, :, :].rearrange("p k n -> p (k n)")[:, 0:HALF]
            den = agg[:, :, :].rearrange("p k n -> p (k n)")[:, HALF:D]
            rcp = ept[:, 0:HALF]
            act_s = mix[:, 0, :].rearrange("p (b n) -> p b n", b=2)
            for i, (s, q) in enumerate(QUARTERS):
                b = buf[:, i % 2]
                dve.wait_ge(S("soft_ready"), i + 1)
                link(V.tensor_tensor(vv, b[:, 2, :], b[:, 3, :], ALU.mult))
                link(V.tensor_scalar(den, vv, oh[:, s, 2:3], par[:, 0, s:s + 1], ALU.mult, ALU.add))
                link(V.reciprocal(rcp, den))
                link(V.scalar_tensor_tensor(rcp, vv, par[:, 0, s:s + 1], rcp, ALU.subtract, ALU.mult))
                link(V.scalar_tensor_tensor(rcp, rcp, par[:, 1, s:s + 1], h3(B[i % 4]), ALU.mult, ALU.mult))
                if i >= 2:
                    dve.wait_ge(S("act_tr"), i - 1)
                V.scalar_tensor_tensor(act_s[:, i % 2, :], b[:, 1, :], par[:, 2, s:s + 1], rcp, ALU.mult,
                                       ALU.add).then_inc(S("act_ready"), 1)

            for h in range(2):
                dve.wait_ge(S("units_done"), R_L1 - 1 + h)
                stats(h, h3(B[6 + h]))
            need(base[0] + chain[0])
            V.bn_aggr(mv[:, :], st[:, :, :].rearrange("p a b -> p (a b)")).then_inc(S("var_ready"), 1)
            dve.wait_ge(S("var_ready"), 6)
            scaled = []
            for h in range(2):
                scaled.append(mark(V.scalar_tensor_tensor(halves(nodes)[h], h3(B[6 + h]), mv[:, 0:1], halves(vec[:, V_LG, :])[h],
                                                          ALU.subtract, ALU.mult)))
            dve.wait_ge(S("std_ready"), 6)
            link(V.reciprocal(rstd[:, :], std[:, :]))
            dve.wait_ge(S("xlb_ready"), 1)
            x2 = []
            for h in range(2):
                xh = halves(X)[h]
                need(scaled[h])
                x2.append(mark(V.scalar_tensor_tensor(xh, halves(nodes)[h], rstd[:, 0:1], xh, ALU.mult, ALU.add)))
            for h in range(2):
                need(x2[h])
                stats(h, halves(X)[h])
            spread_of(7)
            for h in range(2):
                norm(halves(nodes)[h], halves(X)[h]).then_inc(S("xn2_ready"), 1)
            dve.wait_ge(S("xn2_tr"), 2)
            V.tensor_copy(flat(nodT, 1), h3(B[5])).then_inc(S("xn2T1_saved"), 1)

            def attention_dots(g, hsb):
                for i, v in enumerate((V_AS1 + 2 * g, V_AD1 + 2 * g)):
                    V.tensor_tensor_reduce(out=mvs, in0=hsb, in1=vec[:, v, :], scale=1.0, scalar=0.0,
                                           op0=ALU.mult, op1=ALU.add, accum_out=ab[:, i:i + 1]).then_inc(S("dve_chain"), 1)
                    chain[0] += 1
                    dve.wait_ge(S("dve_chain"), chain[0])
                V.tensor_scalar(blk[:, 0:P], ident, ab[:, 0:1], None, ALU.mult).then_inc(S("diag_ready"), 1)

            def attention_weights(g, bank):
                dve.wait_ge(S("spread_done"), g + 1)
                lo = blk[:, P:2 * P]
                sc = blk[:, 3 * P:4 * P]
                link(V.tensor_scalar(sc, bank[:, 0:P], ab[:, 1:2], None, ALU.add))
                link(V.scalar_tensor_tensor(sc, sc, 0.2, sc, ALU.mult, ALU.max))
                link(V.tensor_tensor(sc, sc, cneg[:, :], ALU.add))
                link(V.tensor_reduce(ab[:, 2:3], sc, AX, ALU.max))
                V.tensor_scalar(lo, sc, ab[:, 2:3], None, ALU.subtract).then_inc(S("gat_logit"), 1)
                dve.wait_ge(S("gat_exp"), g + 1)
                link(V.tensor_tensor(lo, lo, cnt[:, :], ALU.mult))
                link(V.tensor_reduce(ab[:, 3:4], lo, AX, ALU.add))
                link(V.reciprocal(ab[:, 4:5], ab[:, 3:4]))
                V.tensor_scalar(lo, lo, ab[:, 4:5], None, ALU.mult).then_inc(S("alpha_ready"), 1)
                dve.wait_ge(S("alpha_tr"), g + 1)
                V.tensor_copy(blk[:, 2 * P:3 * P], B[7 - 4 * g][:, 0:P]).then_inc(S("alphaT_saved"), 1)

            mvs = blk[:, 2048:2048 + D]
            dve.wait_ge(S("h1_saved"), 2)
            attention_dots(0, agg[:, :, :].rearrange("p k n -> p (k n)"))
            attention_weights(0, B[6])
            for h in range(2):
                dve.wait_ge(S("units_done"), R_L1 + 3 + h)
                V.tensor_copy(mix[:, 1, h * HALF:(h + 1) * HALF], h3(B[4 + h])).then_inc(S("mk1_saved"), 1)
            for h in range(2):
                dve.wait_ge(S("units_done"), R_L1 + 7 + h)
                link(V.tensor_copy(ept[:, h * HALF:(h + 1) * HALF], h3(B[2 + h])))

            attention_dots(1, ept[:, 0:D])
            dve.wait_ge(S("mq1_tr"), 2)
            V.tensor_copy(flat(xnT, 1), h3(B[7])).then_inc(S("mq1T1_saved"), 1)
            attention_weights(1, B[2])
            for h in range(2):
                dve.wait_ge(S("x3_done"), h + 1)
                stats(h, h3(B[h]))
            spread_of(8)
            for h in range(2):
                norm(halves(nodes)[h], h3(B[h])).then_inc(S("xl3_ready"), 1)
            dve.wait_ge(S("xl3_tr"), 2)
            V.tensor_copy(flat(nodT, 1), h3(B[5])).then_inc(S("xl3T1_saved"), 1)
            dve.wait_ge(S("route1_done"), 1)
            l8, w8, m8 = rt[:, 8:16], rt[:, 16:24], rt[:, 24:32]
            link(V.tensor_tensor(l8, B[6][:, 0:E_MOE], col[:, G_RB1:G_RB1 + E_MOE], ALU.add))
            link(V.tensor_reduce(rt[:, 50:51], l8, AX, ALU.max))
            V.tensor_scalar(rt[:, 32:40], l8, rt[:, 50:51], None, ALU.subtract).then_inc(S("moe_shift"), 1)
            link(V.scalar_tensor_tensor(w8, l8, rt[:, 50:51], con[:, K_W8:K_W8 + 8], ALU.is_equal, ALU.mult))
            link(V.tensor_reduce(rt[:, 51:52], w8, AX, ALU.max))
            link(V.tensor_scalar(m8, w8, rt[:, 51:52], None, ALU.is_equal))
            hm = agg[:, :, :].rearrange("p k n -> p (k n)")[:, 0:FH]
            dve.wait_ge(S("silu_ready"), 1)
            link(V.tensor_tensor(g3(z[:, 0:FH], HID), g3(z[:, 0:FH], HID), rep(m8, HID), ALU.mult))
            for p in range(2):
                dve.wait_ge(S("moe_up_done"), 2 + p)
                part = slice(p * FH // 2, (p + 1) * FH // 2)
                V.tensor_tensor(hm[:, part], B[3 + p][:, part], z[:, part], ALU.mult).then_inc(S("moe_h_ready"), 1)
            dve.wait_ge(S("moe_exp"), 1)
            link(V.reciprocal(rt[:, 52:53], rt[:, 48:49]))
            o16 = blk[:, 0:HALF].bitcast(bf16)
            for h in range(2):
                dve.wait_ge(S("moe_done"), h + 1)
                link(V.tensor_copy(o16[:, h * HALF:(h + 1) * HALF], h3(B[h])))
                V.scalar_tensor_tensor(halves(nodes)[h], o16[:, h * HALF:(h + 1) * HALF], rt[:, 52:53],
                                       halves(X)[h], ALU.mult, ALU.add).then_inc(S("out_ready"), 1)

        @block.gpsimd
        def _(pool):
            pool.wait_ge(S("b4_free"), L_GNN + 1)
            pool.wait_ge(S("b5_free"), L_GNN + 1)
            va = ept[:, :].rearrange("p (g n) -> p g n", n=65)
            nc.gpsimd.memset(va[:, :, 64:65], 1.0)
            nc.gpsimd.tensor_copy(va[:, :, 0:64], mix[:, 2, :].rearrange("p (g n) -> p g n", n=64)).then_inc(S("vaug_ready"), 1)
            nc.gpsimd.memset(xnt[:, :], 0.0).then_inc(S("kv_clear"), 1)
            pool.wait_ge(S("x_saved"), 2)
            pool.wait_ge(S("vec_loaded"), 16)
            nc.gpsimd.tensor_tensor(X[:, :], X[:, :], vec[:, V_LB, :], ALU.add).then_inc(S("xlb_ready"), 1)
            pool.wait_ge(S("xn2_ready"), 2)
            nc.gpsimd.memset(zh[:, 0, :], 0.0).then_inc(S("zh_clear"), 1)


def kernel(**inputs):
    import numpy as _np
    import concourse.bacc as _bacc
    from concourse import mybir as _mybir
    from concourse.bass_utils import run_bass_kernel_spmd as _run
    import ml_dtypes as _ml

    g = {k: _np.asarray(v) for k, v in inputs.items()}

    def chunk(w):
        k, n = w.shape
        return w.reshape(KT, P, n // HALF, HALF).transpose(2, 1, 0, 3).reshape(n // HALF, P, CH)

    def colk(v):
        return v.reshape(-1, KT, P).transpose(2, 0, 1).reshape(P, -1)

    parts = [chunk(g["L0_gnn_Wn"].T)]
    wm = g["L0_mix_w_qkv"].T
    for l in range(L_GNN):
        w1, w2 = g["L0_gnn_W1"][l].T, g["L0_gnn_W2"][l].T
        m = chunk(wm[:, l * D:(l + 1) * D])
        parts += [chunk(w1[:D]), chunk(w1[D:]), m[:1], chunk(w2), m[1:]]
    parts += [chunk(g["L0_gnn_Wqkv"].T), chunk(g["L0_mix_w_proj"].T), chunk(g["L0_gnn_Wo"].T)]
    for e in range(E_FFN):
        parts += [chunk(g["L0_ffn_w1"][e]), chunk(g["L0_ffn_w2"][e][:D]), chunk(g["L0_ffn_w2"][e][D:])]
    parts += [chunk(g["L1_gnn_W1"]), chunk(g["L1_mix_w_qkv"]), chunk(g["L1_gnn_W2"]), chunk(g["L1_mix_w_proj"])]
    chunks = _np.concatenate(parts)

    def rows(w):
        return w.reshape(-1, P, w.shape[1]).transpose(1, 0, 2).reshape(P, -1)

    up = [rows(g[n].transpose(1, 0, 2).reshape(D, FH)) for n in ("L1_ffn_w1", "L1_ffn_w2")]
    moe_w = _np.concatenate(up + [rows(g["L1_ffn_w3"].reshape(FH, D))], axis=1)

    table = _np.zeros((32, 3 * D), _np.float32)
    table[:N_BIAS, :D] = _np.concatenate([
        g["L0_gnn_bn"][None], g["L0_gnn_b1"], g["L0_gnn_b2"], g["L0_gnn_bqkv"].reshape(3, D), g["L0_gnn_bo"][None],
        g["L0_mix_b_proj"][None], g["L1_gnn_b2"][None], g["L1_mix_b_proj"][None]])
    table[:E_FFN, D:] = g["L0_ffn_b1"]
    bias_rows = _np.concatenate([table] * 3)

    cols = _np.concatenate([
        colk(g["L0_gnn_ln_g"]), colk(g["L0_gnn_ln_b"]), colk(g["L1_gnn_b1"]), rows(g["L0_ffn_router_w"].T),
        _np.broadcast_to(g["L0_ffn_router_b"], (P, E_FFN)), rows(g["L1_ffn_router_w"]),
        _np.broadcast_to(g["L1_ffn_router_b"], (P, E_MOE))], axis=1)
    vecs = _np.concatenate([g[n] for n in ("L1_gnn_att_src1", "L1_gnn_att_dst1", "L1_gnn_att_src2", "L1_gnn_att_dst2",
                                           "L0_ffn_ln_g", "L0_ffn_ln_b")])

    cst = _np.zeros((P, N_CST), _np.float32)
    cst[:, K_ID:K_ID + P] = _np.eye(P)
    cst[:, K_IOTA:K_IOTA + P] = _np.arange(P)
    cst[:, K_ONE:K_ONE + P] = 1
    cst[:, K_AVG:K_AVG + P] = 1 / P
    cst[:, K_EPS] = EPS
    cst[:, K_HALF] = 0.5
    cst[:, K_W4:K_W4 + 4] = E_FFN - _np.arange(E_FFN)
    cst[:, K_D4:K_D4 + 4] = _np.arange(P)[:, None] % 32 == _np.arange(E_FFN)
    cst[:, K_W8:K_W8 + 8] = E_MOE - _np.arange(E_MOE)
    sel = _np.zeros((96, N_BIAS, P), _ml.bfloat16)
    for b in range(N_BIAS):
        sel[b::32, b] = 1
        if b in PAIRS:
            sel[b + 1::32, b] = 1
    sel = sel.reshape(96, -1)

    f = [("x", g["x"]), ("src", g["src"]), ("dst", g["dst"]), ("edge", g["edge_attr_256"]),
         ("w_edge", rows(g["L0_gnn_We"].T)), ("be", g["L0_gnn_be"][None]), ("chunks", chunks), ("moe_w", moe_w),
         ("bias_rows", bias_rows), ("gate_b2", g["L0_ffn_b2"]), ("cols", cols), ("vecs", vecs), ("cst", cst),
         ("sel", sel)]
    nc = _bacc.Bacc("TRN2", target_bir_lowering=False, num_devices=1)
    arrays, args = {}, []
    for name, a in f:
        a = _np.ascontiguousarray(a)
        arrays[f"in_{name}"] = a
        args.append(nc.dram_tensor(f"in_{name}", a.shape, _mybir.dt.from_np(a.dtype), kind="ExternalInput").ap())
    args.append(nc.dram_tensor("out_x", (P, D), _mybir.dt.float32, kind="ExternalOutput").ap())
    gps_kernel(nc, *args)
    r = _run(nc, [arrays], core_ids=[0])
    return r.results[0]["out_x"]
```
